# Optimizing a Trainium2 kernel written in Bass

```python
import numpy as np
import jax
import jax.numpy as jnp

def _softmax(x, axis=-1):
    return jax.nn.softmax(x, axis=axis)

def _gelu(x):
    return jax.nn.gelu(x, approximate=True)

def _silu(x):
    return jax.nn.silu(x)

def _sigmoid(x):
    return jax.nn.sigmoid(x)

def _layernorm(x, axis=-1, eps=1e-05):
    m = jnp.mean(x, axis=axis, keepdims=True)
    v = jnp.var(x, axis=axis, keepdims=True)
    return (x - m) / jnp.sqrt(v + eps)

def _scatter_add(tgt, idx, src, axis=0):
    return tgt.at[idx].add(src)

def _segment_sum(src, seg, n):
    return jax.ops.segment_sum(src, seg, n)
kernel_name = 'mk_recurrent_d1_jaxref_r8_d6016f'

def setup_inputs(seed: int=0):
    np.random.seed(seed)
    _w = jnp.asarray

    def _L0_attn_setup():
        import jax, jax.numpy as jnp
        import numpy as np
        H_HEADS = 16
        SEG = 32
        EPS = 1e-06
        key = jax.random.key(seed)
        ks = jax.random.split(key, 6)
        B, T, D = (2, 512, 128)
        sc = 1.0 / np.sqrt(D)
        return {'x': jax.random.normal(ks[0], (B, T, D), jnp.float32), 'norm_w': jnp.ones((D,), jnp.float32), 'Wq': jax.random.normal(ks[1], (D, D), jnp.float32) * sc, 'Wk': jax.random.normal(ks[2], (D, D), jnp.float32) * sc, 'Wv': jax.random.normal(ks[3], (D, D), jnp.float32) * sc, 'Wo': jax.random.normal(ks[4], (D, D), jnp.float32) * sc, 'Wu': jax.random.normal(ks[5], (D, D), jnp.float32) * sc}
    _L0_attn_in = _L0_attn_setup()

    def _L0_ffn_setup():
        import jax, jax.numpy as jnp
        import numpy as np
        D = 128
        H = 16
        DK = D // H
        E = 8
        DFF = 4 * D
        TOPK = 2
        EPS = 1e-05

        def _layernorm(x, g, b):
            m = jnp.mean(x, axis=-1, keepdims=True)
            v = jnp.mean(jnp.square(x - m), axis=-1, keepdims=True)
            return (x - m) * jax.lax.rsqrt(v + EPS) * g + b
        key = jax.random.key(seed)
        ks = jax.random.split(key, 16)
        s_in = 1.0 / np.sqrt(D)
        s_ff = 1.0 / np.sqrt(DFF)
        return {'x': jax.random.normal(ks[0], (2, 256, D), dtype=jnp.float32), 'ln1_g': jnp.ones((D,), jnp.float32), 'ln1_b': jnp.zeros((D,), jnp.float32), 'w_qkv': jax.random.normal(ks[1], (D, 3 * D), jnp.float32) * s_in, 'b_qkv': jnp.zeros((3 * D,), jnp.float32), 'w_o': jax.random.normal(ks[2], (D, D), jnp.float32) * s_in, 'b_o': jnp.zeros((D,), jnp.float32), 'ln2_g': jnp.ones((D,), jnp.float32), 'ln2_b': jnp.zeros((D,), jnp.float32), 'gate_w': jax.random.normal(ks[3], (D, E), jnp.float32) * s_in, 'gate_b': jnp.zeros((E,), jnp.float32), 'W1': jax.random.normal(ks[4], (E, D, DFF), jnp.float32) * s_in, 'b1': jnp.zeros((E, DFF), jnp.float32), 'W2': jax.random.normal(ks[5], (E, DFF, D), jnp.float32) * s_ff, 'b2': jnp.zeros((E, D), jnp.float32)}
    _L0_ffn_in = _L0_ffn_setup()
    _d = {'L0_attn_x': _L0_attn_in['x'], 'L0_attn_norm_w': _L0_attn_in['norm_w'], 'L0_attn_Wq': _L0_attn_in['Wq'], 'L0_attn_Wk': _L0_attn_in['Wk'], 'L0_attn_Wv': _L0_attn_in['Wv'], 'L0_attn_Wo': _L0_attn_in['Wo'], 'L0_attn_Wu': _L0_attn_in['Wu'], 'L0_ffn_ln1_g': _L0_ffn_in['ln1_g'], 'L0_ffn_ln1_b': _L0_ffn_in['ln1_b'], 'L0_ffn_w_qkv': _L0_ffn_in['w_qkv'], 'L0_ffn_b_qkv': _L0_ffn_in['b_qkv'], 'L0_ffn_w_o': _L0_ffn_in['w_o'], 'L0_ffn_b_o': _L0_ffn_in['b_o'], 'L0_ffn_ln2_g': _L0_ffn_in['ln2_g'], 'L0_ffn_ln2_b': _L0_ffn_in['ln2_b'], 'L0_ffn_gate_w': _L0_ffn_in['gate_w'], 'L0_ffn_gate_b': _L0_ffn_in['gate_b'], 'L0_ffn_W1': _L0_ffn_in['W1'], 'L0_ffn_b1': _L0_ffn_in['b1'], 'L0_ffn_W2': _L0_ffn_in['W2'], 'L0_ffn_b2': _L0_ffn_in['b2']}
    _x0 = _d['L0_attn_x']
    _d['L0_attn_x'] = jax.random.normal(jax.random.fold_in(jax.random.key(seed), 1), (4, 1024, 128), dtype=_x0.dtype)
    del _x0
    return _d

def reference(L0_attn_x, L0_attn_norm_w, L0_attn_Wq, L0_attn_Wk, L0_attn_Wv, L0_attn_Wo, L0_attn_Wu, L0_ffn_ln1_g, L0_ffn_ln1_b, L0_ffn_w_qkv, L0_ffn_b_qkv, L0_ffn_w_o, L0_ffn_b_o, L0_ffn_ln2_g, L0_ffn_ln2_b, L0_ffn_gate_w, L0_ffn_gate_b, L0_ffn_W1, L0_ffn_b1, L0_ffn_W2, L0_ffn_b2):

    def _L0_attn_ref(x, norm_w, Wq, Wk, Wv, Wo, Wu):
        import jax, jax.numpy as jnp
        import numpy as np
        H_HEADS = 16
        SEG = 32
        EPS = 1e-06
        B, T, D = x.shape
        H = H_HEADS
        dk = D // H
        N = T // SEG
        xn = x * jax.lax.rsqrt(jnp.mean(x * x, axis=-1, keepdims=True) + EPS) * norm_w

        def proj(W):
            return (xn @ W.T).reshape(B, T, H, dk)
        q, k, v = (proj(Wq), proj(Wk), proj(Wv))
        pq = jax.nn.elu(q) + 1.0
        pk = jax.nn.elu(k) + 1.0
        pqc = pq.reshape(B, N, SEG, H, dk)
        pkc = pk.reshape(B, N, SEG, H, dk)
        vc = v.reshape(B, N, SEG, H, dk)
        S_chunk = jnp.einsum('bnchk,bnchv->bnhkv', pkc, vc)
        S_cum = jnp.cumsum(S_chunk, axis=1)
        S_excl = S_cum - S_chunk
        boundary_states = S_cum
        inter = jnp.einsum('bnchk,bnhkv->bnchv', pqc, S_excl)
        tri = jnp.tril(jnp.ones((SEG, SEG), x.dtype))
        A = jnp.einsum('bnchk,bndhk->bnhcd', pqc, pkc) * tri
        intra = jnp.einsum('bnhcd,bndhv->bnchv', A, vc)
        zk = pkc.sum(axis=2)
        z_excl = jnp.cumsum(zk, axis=1) - zk
        z = z_excl[:, :, None] + jnp.cumsum(pkc, axis=2)
        denom = jnp.einsum('bnchk,bnchk->bnch', pqc, z) + EPS
        attn_out = ((inter + intra) / denom[..., None]).reshape(B, T, D) @ Wo.T
        x_out = x + attn_out
        xc = x.reshape(B, N, SEG, D)
        m_stack = xc.mean(axis=2)
        counts = jnp.arange(1, SEG + 1, dtype=x.dtype)[None, None, :, None]
        m_current = (jnp.cumsum(xc, axis=2) / counts).reshape(B, T, D)
        causal_mask = (jnp.arange(T) // SEG)[:, None] > jnp.arange(N)[None, :]
        u = x @ Wu.T
        scale = 1.0 / jnp.sqrt(jnp.asarray(D, x.dtype))
        sc_cached = jnp.einsum('btd,bnd->btn', u, m_stack) * scale
        sc_cached = jnp.where(causal_mask[None], sc_cached, -jnp.inf)
        sc_cur = jnp.sum(u * m_current, axis=-1, keepdims=True) * scale
        attn_w = jax.nn.softmax(jnp.concatenate([sc_cached, sc_cur], axis=-1), axis=-1)
        gates_cached = attn_w[..., :N]
        gate_current = attn_w[..., N:]
        h_retrieved = jnp.einsum('btn,bthk,bnhkv->bthv', gates_cached, pq, boundary_states).reshape(B, T, D)
        retrieval_scale = 1.0
        return gate_current * x_out + retrieval_scale * h_retrieved

    def _L0_ffn_ref(x, ln1_g, ln1_b, w_qkv, b_qkv, w_o, b_o, ln2_g, ln2_b, gate_w, gate_b, W1, b1, W2, b2):
        import jax, jax.numpy as jnp
        import numpy as np
        D = 128
        H = 16
        DK = D // H
        E = 8
        DFF = 4 * D
        TOPK = 2
        EPS = 1e-05

        def _layernorm(x, g, b):
            m = jnp.mean(x, axis=-1, keepdims=True)
            v = jnp.mean(jnp.square(x - m), axis=-1, keepdims=True)
            return (x - m) * jax.lax.rsqrt(v + EPS) * g + b
        B, S, _ = x.shape
        h = _layernorm(x, ln1_g, ln1_b)
        qkv = h @ w_qkv + b_qkv
        q, k, v = jnp.split(qkv, 3, axis=-1)
        q = q.reshape(B, S, H, DK)
        k = k.reshape(B, S, H, DK)
        v = v.reshape(B, S, H, DK)
        scores = jnp.einsum('bqhd,bkhd->bhqk', q, k) / np.sqrt(DK)
        attn = jax.nn.softmax(scores, axis=-1)
        o = jnp.einsum('bhqk,bkhd->bqhd', attn, v).reshape(B, S, D)
        x = x + o @ w_o + b_o
        h = _layernorm(x, ln2_g, ln2_b).reshape(B * S, D)
        logits = h @ gate_w + gate_b
        topv, topi = jax.lax.top_k(logits, TOPK)
        gw = jax.nn.softmax(topv, axis=-1)
        ew = jnp.sum(jax.nn.one_hot(topi, E, dtype=h.dtype) * gw[..., None], axis=1)
        hid = jax.nn.relu(jnp.einsum('td,edf->etf', h, W1) + b1[:, None, :])
        out_e = jnp.einsum('etf,efd->etd', hid, W2) + b2[:, None, :]
        moe = jnp.einsum('etd,te->td', out_e, ew)
        return x + moe.reshape(B, S, D)
    x = L0_attn_x
    xn = _layernorm(x, axis=-1)
    s = _L0_attn_ref(xn, L0_attn_norm_w, L0_attn_Wq, L0_attn_Wk, L0_attn_Wv, L0_attn_Wo, L0_attn_Wu)
    g = _silu(_L0_ffn_ref(xn, L0_ffn_ln1_g, L0_ffn_ln1_b, L0_ffn_w_qkv, L0_ffn_b_qkv, L0_ffn_w_o, L0_ffn_b_o, L0_ffn_ln2_g, L0_ffn_ln2_b, L0_ffn_gate_w, L0_ffn_gate_b, L0_ffn_W1, L0_ffn_b1, L0_ffn_W2, L0_ffn_b2))
    x = x + s * g
    return x

_drawn_inputs = setup_inputs


def setup_inputs(seed=0):
    import zlib

    import numpy as np

    out = dict(_drawn_inputs(seed))
    spreads = {'L0_attn_norm_w': (1.0, 0.2),
     'L0_ffn_ln1_g': (1.0, 0.2),
     'L0_ffn_ln1_b': (0.0, 0.1),
     'L0_ffn_b_qkv': (0.0, 0.1),
     'L0_ffn_b_o': (0.0, 0.1),
     'L0_ffn_ln2_g': (1.0, 0.2),
     'L0_ffn_ln2_b': (0.0, 0.1),
     'L0_ffn_gate_b': (0.0, 0.1),
     'L0_ffn_b1': (0.0, 0.1),
     'L0_ffn_b2': (0.0, 0.1)}
    factors = {'L0_attn_Wo': 64.0}
    for name, (base, spread) in spreads.items():
        noise = np.random.default_rng([zlib.crc32(name.encode()), seed]).standard_normal(out[name].shape)
        drawn = base * np.exp(spread * noise) if base else spread * noise
        out[name] = jnp.asarray(drawn.astype(out[name].dtype))
    for name, factor in factors.items():
        out[name] = (out[name] * factor).astype(out[name].dtype)
    return out
```

```python
import concourse.bass as bass
from concourse import mybir
from contextlib import ExitStack

FP32 = mybir.dt.float32
BF16 = mybir.dt.bfloat16
I32 = mybir.dt.int32
U32 = mybir.dt.uint32
ALU = mybir.AluOpType
ACT = mybir.ActivationFunctionType
X_AXIS = mybir.AxisListType.X

B, T, D = 4, 1024, 128
P = 128
TILES = T // P
H, DK = 16, 8
SEG = 32
NSEG = T // SEG
TSEG = P // SEG
EXPERTS, DFF = 8, 512
FC = DFF // P
HG = 4
G = H // HG
HALF = T // 2
HT = TILES // 2
PVW = H * DK * DK
ZW = H * DK
STW = PVW + ZW
STC = STW // 3
EPS_LN, EPS_RMS = 1e-5, 1e-6
ATT_SCALE = float(DK) ** -0.5
GATE_SCALE = float(D) ** -0.5
MASKED = -1e30
RING = 3
RSQRT_MAGIC = 0x5F3759DF

JOBS_SETUP = 3
JOBS_TILE = 15
JOBS_GROUP = 12
JOBS_ROUTE = 12
JOBS_EXPERT = 12
JOBS_BATCH = TILES * JOBS_TILE + G * JOBS_GROUP + JOBS_ROUTE + EXPERTS * JOBS_EXPERT
MAXES = 4 * TILES
STEPS = 2 * TILES


def program(nc, x, norm_w, Wq, Wk, Wv, Wo, Wu, ln1_g, ln1_b, w_qkv, b_qkv, w_o, b_o,
            ln2_g, ln2_b, gate_w, gate_b, W1, b1, W2, b2, out):
    with ExitStack() as ctx:
        def sb(name, shape, dt=FP32):
            return ctx.enter_context(nc.sbuf_tensor(name, shape, dt))

        def sem(name):
            return ctx.enter_context(nc.semaphore(name))

        ident = sb("ident", [P, P])
        tri = sb("tri", [P, P])
        seg_mean = sb("seg_mean", [P, TSEG, SEG])
        seg_ends = sb("seg_ends", [P, TILES, NSEG])
        seg_mask = sb("seg_mask", [P, TILES, NSEG])
        last_seg = sb("last_seg", [NSEG, P])
        ones_row = sb("ones_row", [1, P])
        iota8 = sb("iota8", [P, EXPERTS])
        wnat = sb("wnat", [P, 5, P])
        wT = sb("wT", [P, 5, P])
        b1_rows = sb("b1_rows", [EXPERTS * FC, P])
        vec_rows = sb("vec_rows", [5, P])
        bq_rows = sb("bq_rows", [G, HG, 32])
        bk_rows = sb("bk_rows", [G, HG, 32])
        cols = sb("cols", [P, 48])
        b1_cols = cols[:, 0:32]
        nw_col, g1_col, c1_col, g2_col, c2_col = (cols[:, 32 + i:33 + i] for i in range(5))
        bqk_cols = cols[:, 37:45]
        wqkv_nat = sb("wqkv_nat", [P, 3 * D])
        wqk_pad = sb("wqk_pad", [P, 2, G, P])
        wv_pad = sb("wv_pad", [P, G, P])
        bv_pad = sb("bv_pad", [1, G, HG, 32])
        wo_f = sb("wo_f", [P, D])
        bo_row = sb("bo_row", [1, D])
        gate_sb = sb("gate_sb", [P, EXPERTS])
        gateb_row = sb("gateb_row", [1, EXPERTS])
        b2_sb = sb("b2_sb", [EXPERTS, D])
        w1_buf = [sb(f"w1_buf{i}", [P, DFF]) for i in range(2)]
        w2_buf = [sb(f"w2_buf{i}", [P, FC, D]) for i in range(2)]
        xin = sb("xin", [P, TILES, D])
        xs_all = sb("xs_all", [P, TILES, D])
        hT = sb("hT", [P, T])
        s_all = sb("s_all", [P, TILES, D])
        bn6 = sb("bn6", [P, TILES, 6])
        mv = sb("mv", [P, TILES, 2])
        var3 = sb("var3", [P, 3, TILES])
        rs3 = sb("rs3", [P, 3, TILES])
        rtmp = sb("rtmp", [P, 3 * TILES])
        rtmp2 = sb("rtmp2", [P, 3 * TILES])
        xs = sb("xs", [P, 3, D])
        xT = sb("xT", [P, P])
        xnT = sb("xnT", [P, P])
        qk_min = sb("qk_min", [P, 2 * D])
        qk_pos = sb("qk_pos", [P, 2 * D])
        qk_exp = sb("qk_exp", [P, 2 * D])
        pqk = sb("pqk", [P, 2 * D])
        v_t = sb("v_t", [P, D])
        pv = sb("pv", [P, STW])
        u_both = sb("u_both", [P, 2, D])
        um = sb("um", [P, D])
        mT = sb("mT", [P, NSEG])
        msum = sb("msum", [P, TSEG])
        sc = sb("sc", [P, NSEG + 1])
        mx1 = sb("mx1", [P, 1])
        nb1 = sb("nb1", [P, 1])
        eg = sb("eg", [P, NSEG + 1])
        egsum = sb("egsum", [P, 1])
        egr = sb("egr", [P, 1])
        gates = sb("gates", [P, NSEG + 1])
        gT = sb("gT", [NSEG, P])
        ends_t = sb("ends_t", [P, NSEG])
        state = sb("state", [NSEG, STW])
        prod = sb("prod", [P, STW])
        num = sb("num", [P, ZW])
        den = sb("den", [P, H])
        rden = sb("rden", [P, H])
        lin = sb("lin", [P, D])
        linT = sb("linT", [P, P])
        hret = sb("hret", [P, D])
        xout = sb("xout", [P, D])
        w_grp = sb("w_grp", [P, 2, P])
        b_grp = sb("b_grp", [P, 2])
        kf = sb("kf", [P, T])
        kb = sb("kb", [P, T], BF16)
        qf = sb("qf", [P, T])
        qb = sb("qb", [P, T], BF16)
        vf = sb("vf", [P, TILES, P])
        mx = sb("mx", [P, TILES, HG, 2])
        mneg = sb("mneg", [P, TILES, P])
        ebuf = sb("ebuf", [P, 2, HG, HALF])
        ot = sb("ot", [P, T])
        osum = sb("osum", [P, 2, HG])
        on = sb("on", [P, TILES, D])
        onT = sb("onT", [P, HALF])
        x2 = sb("x2", [P, HT, D])
        z2 = sb("z2", [P, HT, D])
        h2T = sb("h2T", [P, T])
        logit = sb("logit", [P, HT, EXPERTS])
        top8 = sb("top8", [P, HT, 8])
        idx8 = sb("idx8", [P, HT, 8], U32)
        idxf = sb("idxf", [P, HT, 8])
        tdiff = sb("tdiff", [P, HT])
        texp = sb("texp", [P, HT])
        tone = sb("tone", [P, HT])
        w_top = sb("w_top", [P, 2, HT])
        pick = sb("pick", [P, 2, HT, EXPERTS])
        ew = sb("ew", [P, TILES, EXPERTS])
        ewT = sb("ewT", [EXPERTS, HALF])
        acc = sb("acc", [P, TILES, D])
        hid = sb("hid", [P, 2, FC, HALF])
        sg_e = sb("sg_e", [P, TILES * D])
        sg_d = sb("sg_d", [P, TILES * D])
        sg_r = sb("sg_r", [P, TILES * D])
        fin = sb("fin", [P, TILES * D])

        psum = ctx.enter_context(nc.psum_tensor("psum", [P, 8, HALF], FP32))
        score = psum[:, 0:4, :]
        o_ps = psum[:, 4, :]
        ring = [psum[:, 5 + i, :] for i in range(RING)]

        ld_w = sem("ld_w")
        pool_const = sem("pool_const")
        pool_step = sem("pool_step")
        dve_step = sem("dve_step")
        act_step = sem("act_step")
        setup_done = sem("setup_done")
        job_full = sem("job_full")
        job_free = sem("job_free")
        x_loaded = sem("x_loaded")
        xs_ready = sem("xs_ready")
        xT_ready = sem("xT_ready")
        qkmin_ready = sem("qkmin_ready")
        qkexp_ready = sem("qkexp_ready")
        pq_ready = sem("pq_ready")
        pv_ready = sem("pv_ready")
        uT_ready = sem("uT_ready")
        nb_ready = sem("nb_ready")
        eg_ready = sem("eg_ready")
        gates_ready = sem("gates_ready")
        gT_ready = sem("gT_ready")
        state_zero = sem("state_zero")
        state_ready = sem("state_ready")
        lin_ready = sem("lin_ready")
        linT_ready = sem("linT_ready")
        tile_done = sem("tile_done")
        wgrp_ready = sem("wgrp_ready")
        kqv_ready = sem("kqv_ready")
        max_full = sem("max_full")
        max_free = sem("max_free")
        mneg_ready = sem("mneg_ready")
        qf_ready = sem("qf_ready")
        score_full = sem("score_full")
        exp_done = sem("exp_done")
        e_used = sem("e_used")
        o_out = sem("o_out")
        group_done = sem("group_done")
        onT_ready = sem("onT_ready")
        z2_ready = sem("z2_ready")
        h2T_ready = sem("h2T_ready")
        tdiff_ready = sem("tdiff_ready")
        texp_ready = sem("texp_ready")
        ew_ready = sem("ew_ready")
        ewT_ready = sem("ewT_ready")
        w_loaded = [sem(f"w_loaded{i}") for i in range(2)]
        hid_ready = sem("hid_ready")
        acc_ready = sem("acc_ready")
        sg_ready = sem("sg_ready")
        fin_ready = sem("fin_ready")
        stored = sem("stored")

        x_dram = x.rearrange("b (t p) d -> b p t d", p=P)
        out_dram = out.rearrange("b (t p) d -> b p t d", p=P)
        w1_dram = W1.rearrange("e d f -> (e d) f")
        w2_dram = W2.rearrange("e (c p) d -> e p c d", p=P)

        def row(v):
            return v.rearrange("(a n) -> a n", a=1)

        block = ctx.enter_context(nc.Block())

        def ring_base(b):
            return JOBS_SETUP + b * JOBS_BATCH

        GROUP_AT = TILES * JOBS_TILE
        ROUTE_AT = GROUP_AT + G * JOBS_GROUP
        EXPERT_AT = ROUTE_AT + JOBS_ROUTE

        @block.sync
        def _(sp):
            for i, w in enumerate((Wq, Wk, Wv, Wo, Wu)):
                sp.dma_start(wnat[:, i, :], w).then_inc(ld_w, 16)
            sp.dma_start(b1_rows[:, :], b1.rearrange("e (c p) -> (e c) p", p=P)).then_inc(ld_w, 16)
            for i, v in enumerate((norm_w, ln1_g, ln1_b, ln2_g, ln2_b)):
                sp.dma_start(vec_rows[i:i + 1, :], row(v)).then_inc(ld_w, 16)
            sp.dma_start(wqkv_nat[:, :], w_qkv).then_inc(ld_w, 16)
            sp.dma_start(wo_f[:, :], w_o).then_inc(ld_w, 16)
            sp.dma_start(bo_row[:, :], row(b_o)).then_inc(ld_w, 16)
            sp.dma_start(gate_sb[:, :], gate_w).then_inc(ld_w, 16)
            sp.dma_start(gateb_row[:, :], row(gate_b)).then_inc(ld_w, 16)
            sp.dma_start(b2_sb[:, :], b2).then_inc(ld_w, 16)
            sp.wait_ge(pool_const, 1)
            head_rows = b_qkv.rearrange("(a g j d) -> a g j d", a=3, g=G, j=HG)
            sp.dma_start(bq_rows[:, :, 0:DK], head_rows[0]).then_inc(ld_w, 16)
            sp.dma_start(bk_rows[:, :, 0:DK], head_rows[1]).then_inc(ld_w, 16)
            sp.dma_start(bv_pad[:, :, :, 0:DK].rearrange("a g j d -> a (g j) d"),
                         b_qkv[2 * D:3 * D].rearrange("(a h d) -> a h d", a=1, d=DK)).then_inc(ld_w, 16)
            with sp.Fori(0, B) as b:
                sp.wait_ge(fin_ready, b + 1)
                sp.dma_start(xin[:, :, :], x_dram[bass.ds(b, 1)].rearrange("a p t d -> p (a t) d")).then_inc(x_loaded, 16)
                with sp.Fori(0, EXPERTS // 2) as e2:
                    for i in range(2):
                        sp.wait_ge(acc_ready, (b * (EXPERTS // 2) + e2) * 2 + i + 1)
                        e = e2 * 2 + i
                        sp.dma_start(w1_buf[i][:, :], w1_dram[bass.ds(e * D, D), :]).then_inc(w_loaded[i], 16)
                        sp.dma_start(w2_buf[i][:, :, :],
                                     w2_dram[bass.ds(e, 1)].rearrange("a p c d -> p (a c) d")).then_inc(w_loaded[i], 16)
                sp.wait_ge(fin_ready, b + 2)
                sp.dma_start(out_dram[bass.ds(b, 1)].rearrange("a p t d -> p (a t) d"),
                             fin[:, :].rearrange("p (t d) -> p t d", d=D)).then_inc(stored, 16)
            sp.wait_ge(stored, 16 * (B + 1))

        @block.gpsimd
        def _(pool):
            step = 0

            def link(ins):
                nonlocal step
                step += 1
                ins.then_inc(pool_step, 1)
                pool.wait_ge(pool_step, step)

            pool.memset(bq_rows[:, :, :], 0.0)
            pool.memset(bv_pad[:, :, :, :], 0.0)
            link(pool.memset(bk_rows[:, :, :], 0.0))
            link(pool.memset(bk_rows[:, :, DK:DK + 1], 1.0))
            pool.memset(bv_pad[:, :, :, DK:DK + 1], 1.0).then_inc(pool_const, 1)
            pool.memset(ones_row[:, :], 1.0)
            pool.memset(ident[:, :], 0.0)
            pool.memset(tri[:, :], 1.0)
            pool.memset(seg_ends[:, :, :], 1.0)
            pool.memset(seg_mask[:, :, :], 0.0)
            pool.memset(last_seg[:, :], 1.0)
            pool.memset(mneg[:, :, :], 0.0)
            pool.memset(mT[:, :], 0.0)
            for c in range(SEG):
                pool.memset(seg_mean[:, :, c:c + 1], 1.0 / (c + 1))
            pool.iota(iota8[:, :], [[1, EXPERTS]], base=0, channel_multiplier=0,
                      allow_small_or_imprecise_dtypes=True)
            pool.memset(wqk_pad[:, :, :, :], 0.0)
            link(pool.memset(wv_pad[:, :, :], 0.0))
            pool.affine_select(out=ident[:, :], in_=ident[:, :], compare_op=ALU.not_equal, fill=1.0, base=0,
                               pattern=[[-1, P]], channel_multiplier=1)
            pool.affine_select(out=tri[:, :], in_=tri[:, :], compare_op=ALU.is_ge, fill=0.0, base=0,
                               pattern=[[1, P]], channel_multiplier=-1)
            link(pool.affine_select(out=seg_mean[:, :, :], in_=seg_mean[:, :, :], compare_op=ALU.is_ge, fill=0.0,
                                    base=0, pattern=[[SEG, TSEG], [1, SEG]], channel_multiplier=-1))
            pool.affine_select(out=seg_mean[:, :, :], in_=seg_mean[:, :, :], compare_op=ALU.is_ge, fill=0.0,
                               base=0, pattern=[[-SEG, TSEG], [0, SEG]], channel_multiplier=1)
            pool.affine_select(out=seg_ends[:, :, :], in_=seg_ends[:, :, :], compare_op=ALU.is_ge, fill=0.0,
                               base=SEG - 1, pattern=[[-P, TILES], [SEG, NSEG]], channel_multiplier=-1)
            pool.affine_select(out=seg_mask[:, :, :], in_=seg_mask[:, :, :], compare_op=ALU.is_ge, fill=MASKED,
                               base=-SEG, pattern=[[P, TILES], [-SEG, NSEG]], channel_multiplier=1)
            pool.affine_select(out=last_seg[:, :], in_=last_seg[:, :], compare_op=ALU.is_ge, fill=0.0,
                               base=1 - NSEG, pattern=[[0, P]], channel_multiplier=1).then_inc(pool_const, 1)

            with pool.Fori(0, B) as b:
                with pool.Fori(0, TILES) as t:
                    i = b * TILES + t
                    pool.wait_ge(qkexp_ready, i + 1)
                    pool.tensor_tensor(pqk[:, :], qk_exp[:, :], qk_pos[:, :], ALU.add).then_inc(pq_ready, 1)
                    pool.wait_ge(pq_ready, i + 1)
                    keys = pqk[:, D:2 * D].rearrange("p (h k) -> p h k", k=DK)
                    vals = v_t[:, :].rearrange("p (h v) -> p h v", v=DK)
                    pool.tensor_tensor(pv[:, 0:PVW].rearrange("p (h k v) -> p h k v", k=DK, v=DK),
                                       keys.unsqueeze(3).broadcast_to([P, H, DK, DK]),
                                       vals.unsqueeze(2).broadcast_to([P, H, DK, DK]), ALU.mult)
                    pool.tensor_copy(pv[:, PVW:STW], pqk[:, D:2 * D]).then_inc(pv_ready, 1)
                with pool.Fori(0, G) as g:
                    pool.wait_ge(setup_done, 1)
                    pool.wait_ge(group_done, b * G + g + 1)
                    pool.tensor_copy(w_grp[:, :, :], wqk_pad[:, :, bass.ds(g, 1), :].rearrange("p a g n -> p a (g n)"))
                    pool.tensor_copy(b_grp[:, 0:1], bqk_cols[:, bass.ds(g, 1)])
                    pool.tensor_copy(b_grp[:, 1:2], bqk_cols[:, bass.ds(g + G, 1)]).then_inc(wgrp_ready, 1)

        @block.scalar
        def _(act):
            with act.Fori(0, B) as b:
                with act.Fori(0, TILES) as t:
                    i = b * TILES + t
                    act.wait_ge(qkmin_ready, i + 1)
                    act.activation(qk_exp[:, :], qk_min[:, :], ACT.Exp).then_inc(qkexp_ready, 1)
                    act.wait_ge(nb_ready, i + 1)
                    act.activation(eg[:, :], sc[:, :], ACT.Exp, bias=nb1[:, 0:1], scale=GATE_SCALE,
                                   accum_out=egsum[:, 0:1]).then_inc(eg_ready, 1)
                with act.Fori(0, G) as g:
                    for s in range(STEPS):
                        for half in range(2):
                            n = 2 * s + half
                            act.wait_ge(score_full, (b * G + g) * 2 * STEPS + n + 1)
                            act.wait_ge(e_used, (b * G + g) * STEPS + s + 1)
                            act.activation(ebuf[:, s % 2, 2 * half:2 * half + 2, :], score[:, 2 * half:2 * half + 2, :],
                                           ACT.Exp, scale=ATT_SCALE).then_inc(exp_done, 1)
                for hb in range(2):
                    act.wait_ge(tdiff_ready, b * 2 + hb + 1)
                    act.activation(texp[:, :], tdiff[:, :], ACT.Exp).then_inc(texp_ready, 1)
                act.wait_ge(acc_ready, (b + 1) * EXPERTS + 2)
                act.activation(sg_e[:, :], acc[:, :, :].rearrange("p t d -> p (t d)"), ACT.Exp,
                               scale=-1.0).then_inc(sg_ready, 1)

        @block.vector
        def _(dve):
            chain = [0]

            def link(ins):
                chain[0] += 1
                ins.then_inc(dve_step, 1)
                dve.wait_ge(dve_step, chain[0])

            def end_chain():
                link(nc.vector.memset(rtmp2[:, 0:1], 0.0))
                dve.sem_clear(dve_step)
                chain[0] = 0

            def rsqrt(dst, src, w):
                a, c = rtmp[:, 0:w], rtmp2[:, 0:w]
                link(nc.vector.tensor_scalar(a.bitcast(I32), src.bitcast(I32), 1, None, ALU.arith_shift_right))
                link(nc.vector.tensor_scalar(dst.bitcast(I32), a.bitcast(I32), -1, RSQRT_MAGIC, ALU.mult, ALU.add))
                for _ in range(4):
                    link(nc.vector.tensor_tensor(c, dst, dst, ALU.mult))
                    link(nc.vector.tensor_tensor(c, c, src, ALU.mult))
                    link(nc.vector.tensor_scalar(c, c, -0.5, 1.5, ALU.mult, ALU.add))
                    link(nc.vector.tensor_tensor(dst, dst, c, ALU.mult))

            def job(n):
                dve.wait_ge(job_full, n + 1)

            def freed(ins):
                ins.then_inc(job_free, 1)

            nc.vector.memset(state[:, :], 0.0).then_inc(job_free, RING)
            dve.wait_ge(ld_w, 16 * 20)
            dve.wait_ge(pool_const, 2)
            job(0)
            freed(nc.vector.tensor_copy(wT[:, 0:3, :].rearrange("p a n -> p (a n)"), ring[0][:, 0:3 * P]))
            job(1)
            freed(nc.vector.tensor_copy(wT[:, 3:5, :].rearrange("p a n -> p (a n)"), ring[1][:, 0:2 * P]))
            job(2)
            freed(nc.vector.tensor_copy(cols[:, 0:45], ring[2][:, 0:45]))
            for a in range(2):
                nc.vector.tensor_copy(wqk_pad[:, a].rearrange("p g (j r) -> p (g j) r", r=32)[:, :, 0:DK],
                                      wqkv_nat[:, a * D:(a + 1) * D].rearrange("p (h d) -> p h d", d=DK))
            nc.vector.tensor_copy(wv_pad[:, :, :].rearrange("p g (j r) -> p (g j) r", r=32)[:, :, 0:DK],
                                  wqkv_nat[:, 2 * D:3 * D].rearrange("p (h d) -> p h d", d=DK)).then_inc(setup_done, 1)
            dve.sem_inc(fin_ready, 1)
            dve.sem_inc(acc_ready, 2)
            dve.sem_inc(group_done, 1)
            dve.sem_inc(max_free, 2)
            dve.sem_inc(e_used, 2)
            dve.sem_inc(stored, 16)
            link(nc.vector.memset(rtmp[:, 0:1], 0.0))
            end_chain()

            with dve.Fori(0, B) as b:
                dve.wait_ge(x_loaded, b * 16 + 16)
                for t in range(TILES):
                    nc.vector.bn_stats(bn6[:, t, :], xin[:, t, :])
                link(nc.vector.memset(state[:, :], 0.0))
                for t in range(TILES - 1):
                    nc.vector.bn_aggr(mv[:, t, :], bn6[:, t, :])
                link(nc.vector.bn_aggr(mv[:, TILES - 1, :], bn6[:, TILES - 1, :]))
                link(nc.vector.tensor_scalar(var3[:, 0, :], mv[:, :, 1], EPS_LN, None, ALU.add))
                rsqrt(rs3[:, 0, :], var3[:, 0, :], TILES)
                link(nc.vector.tensor_tensor(var3[:, 0, :], mv[:, :, 1], rs3[:, 0, :], ALU.mult))
                link(nc.vector.tensor_tensor(var3[:, 0, :], var3[:, 0, :], rs3[:, 0, :], ALU.mult))
                nc.vector.tensor_scalar(var3[:, 1, :], var3[:, 0, :], EPS_RMS, None, ALU.add)
                link(nc.vector.tensor_scalar(var3[:, 2, :], var3[:, 0, :], EPS_LN, None, ALU.add))
                rsqrt(rs3[:, 1:3, :].rearrange("p a t -> p (a t)"), var3[:, 1:3, :].rearrange("p a t -> p (a t)"),
                      2 * TILES)
                end_chain()

                with dve.Fori(0, TILES) as t:
                    i = b * TILES + t
                    r0 = ring_base(b) + t * JOBS_TILE
                    one = bass.ds(t, 1)
                    link(nc.vector.tensor_scalar(xs[:, 0, :], xin[:, one, :].rearrange("p a d -> p (a d)"),
                                                 mv[:, one, 0], rs3[:, 0, one], ALU.subtract, ALU.mult))
                    nc.vector.tensor_scalar(xs[:, 1, :], xs[:, 0, :], rs3[:, 1, one], None, ALU.mult)
                    nc.vector.tensor_copy(ends_t[:, :], seg_ends[:, one, :].rearrange("p a n -> p (a n)"))
                    nc.vector.tensor_scalar(xs[:, 2, :], xs[:, 0, :], rs3[:, 2, one], None, ALU.mult)\
                        .then_inc(xs_ready, 1)
                    nc.vector.tensor_copy(xs_all[:, one, :].rearrange("p a d -> p (a d)"), xs[:, 0, :])
                    job(r0 + 0)
                    link(nc.vector.tensor_copy(xT[:, :], ring[0][:, 0:P]))
                    nc.vector.tensor_scalar(hT[:, bass.ds(t * P, P)], ring[0][:, 2 * P:3 * P], g1_col, c1_col,
                                            ALU.mult, ALU.add)
                    nc.vector.tensor_reduce(msum[:, :], xT[:, :].rearrange("p (n c) -> p n c", c=SEG), X_AXIS, ALU.add)
                    link(nc.vector.tensor_scalar(xnT[:, :], ring[0][:, P:2 * P], nw_col, None, ALU.mult))
                    link(nc.vector.tensor_scalar(mT[:, bass.ds(t * TSEG, TSEG)], msum[:, :], 1.0 / SEG, None, ALU.mult))
                    dve.sem_inc(xT_ready, 1)
                    dve.sem_inc(job_free, 1)
                    job(r0 + 1)
                    nc.vector.tensor_scalar(qk_min[:, :], ring[1][:, 0:2 * D], 0.0, None, ALU.min)
                    nc.vector.tensor_scalar(qk_pos[:, :], ring[1][:, 0:2 * D], 0.0, None, ALU.max)
                    link(nc.vector.tensor_copy(v_t[:, :], ring[1][:, 2 * D:3 * D]))
                    dve.sem_inc(qkmin_ready, 1)
                    dve.sem_inc(job_free, 1)
                    job(r0 + 2)
                    link(nc.vector.tensor_copy(u_both[:, :, :].rearrange("p a n -> p (a n)"), ring[2][:, 0:2 * D]))
                    dve.sem_inc(uT_ready, 1)
                    link(nc.vector.tensor_tensor(um[:, :], ring[2][:, 2 * D:3 * D], u_both[:, 1, :], ALU.mult))
                    freed(nc.vector.tensor_reduce(sc[:, NSEG:NSEG + 1], um[:, :], X_AXIS, ALU.add))
                    job(r0 + 3)
                    link(nc.vector.tensor_tensor(sc[:, 0:NSEG], ring[0][:, 0:NSEG],
                                                 seg_mask[:, one, :].rearrange("p a n -> p (a n)"), ALU.add))
                    link(nc.vector.tensor_reduce(mx1[:, :], sc[:, :], X_AXIS, ALU.max))
                    dve.sem_inc(job_free, 1)
                    nc.vector.tensor_scalar(nb1[:, :], mx1[:, :], -GATE_SCALE, None, ALU.mult).then_inc(nb_ready, 1)
                    dve.wait_ge(eg_ready, i + 1)
                    link(nc.vector.reciprocal(egr[:, :], egsum[:, :]))
                    link(nc.vector.tensor_scalar(gates[:, :], eg[:, :], egr[:, 0:1], None, ALU.mult))
                    dve.sem_inc(gates_ready, 1)
                    job(r0 + 4)
                    link(nc.vector.tensor_copy(gT[:, :], ring[1][0:NSEG, 0:P]))
                    dve.sem_inc(gT_ready, 1)
                    dve.sem_inc(job_free, 1)
                    dve.wait_ge(pq_ready, i + 1)

                    def times_queries(bank, heads, h0, at):
                        return nc.vector.tensor_tensor(
                            prod[:, at:at + heads * 64].rearrange("p (h k v) -> p h k v", k=DK, v=DK),
                            bank[:, 0:heads * 64].rearrange("p (h k v) -> p h k v", k=DK, v=DK),
                            pqk[:, h0 * DK:(h0 + heads) * DK].rearrange("p (h k) -> p h k", k=DK)
                            .unsqueeze(3).broadcast_to([P, heads, DK, DK]), ALU.mult)

                    def sum_keys(dst):
                        return nc.vector.tensor_reduce(dst[:, :].rearrange("p (h v) -> p h v", v=DK),
                                                       prod[:, 0:PVW].rearrange("p (h k v) -> p h v k", k=DK, v=DK),
                                                       X_AXIS, ALU.add)

                    job(r0 + 5)
                    freed(times_queries(ring[2], 6, 0, 0))
                    job(r0 + 6)
                    freed(times_queries(ring[0], 6, 6, 384))
                    job(r0 + 7)
                    link(times_queries(ring[1], 4, 12, 768))
                    link(nc.vector.tensor_tensor(prod[:, PVW:STW], ring[1][:, 256:384], pqk[:, 0:D], ALU.mult))
                    dve.sem_inc(job_free, 1)
                    sum_keys(num)
                    link(nc.vector.tensor_reduce(den[:, :], prod[:, PVW:STW].rearrange("p (h k) -> p h k", k=DK),
                                                 X_AXIS, ALU.add))
                    link(nc.vector.tensor_scalar(den[:, :], den[:, :], EPS_RMS, None, ALU.add))
                    link(nc.vector.reciprocal(rden[:, :], den[:, :]))
                    nc.vector.tensor_tensor(lin[:, :].rearrange("p (h v) -> p h v", v=DK),
                                            num[:, :].rearrange("p (h v) -> p h v", v=DK),
                                            rden[:, :].unsqueeze(2).broadcast_to([P, H, DK]), ALU.mult)\
                        .then_inc(lin_ready, 1)
                    for j in range(3):
                        job(r0 + 8 + j)
                        at = state[:, j * STC:(j + 1) * STC]
                        freed(nc.vector.tensor_tensor(at, ring[(8 + j) % RING][0:NSEG, 0:STC], at, ALU.add))
                    link(nc.vector.memset(rtmp[:, 0:1], 0.0))
                    dve.sem_inc(state_ready, 1)
                    job(r0 + 11)
                    freed(times_queries(ring[2], 8, 0, 0))
                    job(r0 + 12)
                    link(times_queries(ring[0], 8, 8, 512))
                    freed(sum_keys(hret))
                    job(r0 + 13)
                    link(nc.vector.tensor_copy(linT[:, :], ring[1][:, 0:P]))
                    dve.sem_inc(linT_ready, 1)
                    dve.sem_inc(job_free, 1)
                    job(r0 + 14)
                    link(nc.vector.tensor_tensor(xout[:, :], ring[2][:, 0:D], xs[:, 0, :], ALU.add))
                    freed(nc.vector.scalar_tensor_tensor(s_all[:, one, :].rearrange("p a d -> p (a d)"), xout[:, :],
                                                         gates[:, NSEG:NSEG + 1], hret[:, :], ALU.mult, ALU.add))
                    end_chain()

                with dve.Fori(0, G) as g:
                    gi = b * G + g
                    r0 = ring_base(b) + GROUP_AT + g * JOBS_GROUP
                    dve.wait_ge(wgrp_ready, gi + 1)
                    for n in range(2):
                        job(r0 + n)
                        blk = slice(n * HALF, (n + 1) * HALF)
                        link(nc.vector.tensor_scalar(kf[:, blk], ring[n][:, :], b_grp[:, 1:2], None, ALU.add))
                        freed(nc.vector.tensor_copy(kb[:, blk], kf[:, blk]))
                    for n in range(2):
                        job(r0 + 2 + n)
                        freed(nc.vector.tensor_scalar(qb[:, n * HALF:(n + 1) * HALF], ring[(2 + n) % RING][:, :],
                                                      b_grp[:, 0:1], None, ALU.add))
                    for n in range(2):
                        job(r0 + 4 + n)
                        freed(nc.vector.tensor_copy(vf[:, n * HT:(n + 1) * HT, :].rearrange("p t n -> p (t n)"),
                                                    ring[(4 + n) % RING][:, :]))
                    link(nc.vector.memset(rtmp[:, 0:1], 0.0))
                    dve.sem_inc(kqv_ready, 1)
                    for m in range(MAXES):
                        qt, kk, hh = m // 4, (m // 2) % 2, m % 2
                        dve.wait_ge(max_full, gi * MAXES + m + 1)
                        nc.vector.tensor_reduce(mx[:, qt, 2 * hh:2 * hh + 2, kk], score[:, 2 * hh:2 * hh + 2, :],
                                                X_AXIS, ALU.max).then_inc(max_free, 1)
                    link(nc.vector.memset(rtmp[:, 0:1], 0.0))
                    link(nc.vector.tensor_tensor(mx[:, :, :, 0], mx[:, :, :, 0], mx[:, :, :, 1], ALU.max))
                    nc.vector.tensor_scalar(
                        mneg[:, :, :].rearrange("p t (j r) -> p t j r", r=32)[:, :, :, DK],
                        mx[:, :, :, 0], -1.0, None, ALU.mult).then_inc(mneg_ready, 1)
                    for n in range(2):
                        job(r0 + 6 + n)
                        freed(nc.vector.tensor_scalar(qf[:, n * HALF:(n + 1) * HALF], ring[n][:, :],
                                                      b_grp[:, 0:1], None, ALU.add))
                    link(nc.vector.memset(rtmp[:, 0:1], 0.0))
                    dve.sem_inc(qf_ready, 1)
                    for n in range(2):
                        dve.wait_ge(e_used, gi * STEPS + (n + 1) * TILES + 2)
                        nc.vector.tensor_copy(ot[:, n * HALF:(n + 1) * HALF], o_ps[:, :]).then_inc(o_out, 1)
                    for n in range(4):
                        job(r0 + 8 + n)
                        o4 = ring[(8 + n) % RING][:, 0:2 * P].rearrange("p (t j r) -> p t j r", t=2, r=32)
                        link(nc.vector.reciprocal(osum[:, :, :], o4[:, :, :, DK]))
                        for t in range(2):
                            ins = nc.vector.tensor_tensor(
                                on[:, 2 * n + t, bass.ds(g * HG * DK, HG * DK)].rearrange("p (j d) -> p j d", d=DK),
                                o4[:, t, :, 0:DK], osum[:, t, :].unsqueeze(2).broadcast_to([P, HG, DK]), ALU.mult)
                        link(ins)
                        dve.sem_inc(job_free, 1)
                    dve.sem_inc(group_done, 1)
                    end_chain()

                for hb in range(2):
                    r0 = ring_base(b) + ROUTE_AT + hb * 6
                    hi = b * 2 + hb
                    tl = slice(hb * HT, (hb + 1) * HT)
                    job(r0)
                    link(nc.vector.tensor_copy(onT[:, :], ring[0][:, :]))
                    dve.sem_inc(onT_ready, 1)
                    dve.sem_inc(job_free, 1)
                    job(r0 + 1)
                    link(nc.vector.tensor_tensor(x2[:, :, :].rearrange("p t d -> p (t d)"), ring[1][:, :],
                                                 xs_all[:, tl, :].rearrange("p t d -> p (t d)"), ALU.add))
                    for t in range(HT):
                        ins = nc.vector.bn_stats(bn6[:, t, :], x2[:, t, :])
                    link(ins)
                    dve.sem_inc(job_free, 1)
                    for t in range(HT):
                        ins = nc.vector.bn_aggr(mv[:, t, :], bn6[:, t, :])
                    link(ins)
                    link(nc.vector.tensor_scalar(var3[:, 0, 0:HT], mv[:, 0:HT, 1], EPS_LN, None, ALU.add))
                    rsqrt(rs3[:, 0, 0:HT], var3[:, 0, 0:HT], HT)
                    for t in range(HT):
                        ins = nc.vector.tensor_scalar(z2[:, t, :], x2[:, t, :], mv[:, t, 0:1], rs3[:, 0, t:t + 1],
                                                      ALU.subtract, ALU.mult)
                    link(ins)
                    dve.sem_inc(z2_ready, 1)
                    job(r0 + 2)
                    link(nc.vector.tensor_scalar(h2T[:, hb * HALF:(hb + 1) * HALF], ring[2][:, :], g2_col, c2_col,
                                                 ALU.mult, ALU.add))
                    dve.sem_inc(h2T_ready, 1)
                    dve.sem_inc(job_free, 1)
                    job(r0 + 3)
                    link(nc.vector.tensor_copy(logit[:, :, :].rearrange("p t e -> p (t e)"),
                                               ring[0][:, 0:HT * EXPERTS]))
                    for t in range(HT):
                        ins = nc.vector.max(top8[:, t, :], logit[:, t, :])
                    link(ins)
                    freed(nc.vector.tensor_tensor(tdiff[:, :], top8[:, :, 1], top8[:, :, 0], ALU.subtract))
                    for t in range(HT):
                        ins = nc.vector.max_index(idx8[:, t, :], top8[:, t, :], logit[:, t, :])
                    link(ins)
                    dve.sem_inc(tdiff_ready, 1)
                    link(nc.vector.tensor_copy(idxf[:, :, :], idx8[:, :, :]))
                    for k in range(2):
                        ins = nc.vector.tensor_tensor(pick[:, k, :, :],
                                                      iota8[:, :].unsqueeze(1).broadcast_to([P, HT, EXPERTS]),
                                                      idxf[:, :, k].unsqueeze(2).broadcast_to([P, HT, EXPERTS]),
                                                      ALU.is_equal)
                    link(ins)
                    dve.wait_ge(texp_ready, hi + 1)
                    link(nc.vector.tensor_scalar(tone[:, :], texp[:, :], 1.0, None, ALU.add))
                    link(nc.vector.reciprocal(w_top[:, 0, :], tone[:, :]))
                    link(nc.vector.tensor_tensor(w_top[:, 1, :], w_top[:, 0, :], texp[:, :], ALU.mult))
                    for k in range(2):
                        ins = nc.vector.tensor_tensor(pick[:, k, :, :], pick[:, k, :, :],
                                                      w_top[:, k, :].unsqueeze(2).broadcast_to([P, HT, EXPERTS]),
                                                      ALU.mult)
                    link(ins)
                    link(nc.vector.tensor_tensor(ew[:, tl, :], pick[:, 0, :, :], pick[:, 1, :, :], ALU.add))
                    dve.sem_inc(ew_ready, 1)
                    job(r0 + 4)
                    link(nc.vector.tensor_copy(ewT[:, :], ring[1][0:EXPERTS, :]))
                    dve.sem_inc(ewT_ready, 1)
                    dve.sem_inc(job_free, 1)
                    job(r0 + 5)
                    freed(nc.vector.tensor_tensor(acc[:, tl, :].rearrange("p t d -> p (t d)"), ring[2][:, :],
                                                  x2[:, :, :].rearrange("p t d -> p (t d)"), ALU.add))
                    link(nc.vector.memset(rtmp[:, 0:1], 0.0))
                end_chain()

                with dve.Fori(0, EXPERTS) as e:
                    r0 = ring_base(b) + EXPERT_AT + e * JOBS_EXPERT
                    for tb in range(2):
                        for c in range(FC):
                            job(r0 + tb * 6 + c)
                            nc.vector.tensor_scalar(hid[:, tb, c, :], ring[c % RING][:, :],
                                                    b1_cols[:, bass.ds(e * FC + c, 1)], 0.0,
                                                    ALU.add, ALU.max).then_inc(job_free, 1)
                        link(nc.vector.memset(rtmp[:, 0:1], 0.0))
                        dve.sem_inc(hid_ready, 1)
                        for q in range(2):
                            job(r0 + tb * 6 + 4 + q)
                            for t in range(2):
                                tile = tb * HT + 2 * q + t
                                at = acc[:, tile, :]
                                ins = nc.vector.scalar_tensor_tensor(at, ring[(4 + q) % RING][:, t * D:(t + 1) * D],
                                                                     ew[:, tile, bass.ds(e, 1)], at, ALU.mult, ALU.add)
                            freed(ins)
                    link(nc.vector.memset(rtmp[:, 0:1], 0.0))
                    dve.sem_inc(acc_ready, 1)
                    end_chain()

                dve.wait_ge(sg_ready, b + 1)
                dve.wait_ge(stored, b * 16 + 16)
                link(nc.vector.tensor_scalar(sg_d[:, :], sg_e[:, :], 1.0, None, ALU.add))
                link(nc.vector.reciprocal(sg_r[:, :], sg_d[:, :]))
                link(nc.vector.tensor_tensor(sg_d[:, :], sg_r[:, :], acc[:, :, :].rearrange("p t d -> p (t d)"), ALU.mult))
                link(nc.vector.tensor_tensor(sg_r[:, :], sg_d[:, :], s_all[:, :, :].rearrange("p t d -> p (t d)"), ALU.mult))
                link(nc.vector.tensor_tensor(fin[:, :], sg_r[:, :], xin[:, :, :].rearrange("p t d -> p (t d)"), ALU.add))
                dve.sem_inc(fin_ready, 1)
                end_chain()

        @block.tensor
        def _(pe):
            def start(n):
                pe.wait_ge(job_free, n + 1)

            def mm(dst, lhsT, rhs, first=True, last=True, **kw):
                return pe.matmul(dst, lhsT, rhs, start=first, stop=last, **kw)

            pe.wait_ge(ld_w, 16 * 20)
            pe.wait_ge(pool_const, 2)
            start(0)
            for i in range(3):
                ins = pe.transpose(ring[0][:, i * P:(i + 1) * P], wnat[:, i, :], ident[:, :])
            ins.then_inc(job_full, 1)
            start(1)
            for i in range(2):
                ins = pe.transpose(ring[1][:, i * P:(i + 1) * P], wnat[:, 3 + i, :], ident[:, :])
            ins.then_inc(job_full, 1)
            start(2)
            pe.transpose(ring[2][:, 0:32], b1_rows[:, :], ident[0:32, 0:32])
            pe.transpose(ring[2][:, 32:37], vec_rows[:, :], ident[0:5, 0:5])
            pe.transpose(ring[2][:, 37:41], bq_rows[:, :, :].rearrange("g j r -> g (j r)"), ident[0:G, 0:G])
            pe.transpose(ring[2][:, 41:45], bk_rows[:, :, :].rearrange("g j r -> g (j r)"), ident[0:G, 0:G])\
                .then_inc(job_full, 1)
            pe.wait_ge(setup_done, 1)

            with pe.Fori(0, B) as b:
                with pe.Fori(0, TILES) as t:
                    i = b * TILES + t
                    r0 = ring_base(b) + t * JOBS_TILE
                    start(r0)
                    pe.wait_ge(xs_ready, i + 1)
                    for k in range(3):
                        ins = pe.transpose(ring[0][:, k * P:(k + 1) * P], xs[:, k, :], ident[:, :])
                    ins.then_inc(job_full, 1)
                    start(r0 + 1)
                    pe.wait_ge(xT_ready, i + 1)
                    mm(ring[1][:, 0:3 * D], xnT[:, :], wT[:, 0:3, :].rearrange("p a n -> p (a n)")).then_inc(job_full, 1)
                    start(r0 + 2)
                    mm(ring[2][:, 0:D], wT[:, 4, :], xT[:, :])
                    mm(ring[2][:, D:2 * D], xT[:, :], wT[:, 4, :])
                    mm(ring[2][:, 2 * D:3 * D], seg_mean[:, :, :].rearrange("p a n -> p (a n)"), xs[:, 0, :])\
                        .then_inc(job_full, 1)
                    start(r0 + 3)
                    pe.wait_ge(uT_ready, i + 1)
                    mm(ring[0][:, 0:NSEG], u_both[:, 0, :], mT[:, :]).then_inc(job_full, 1)
                    start(r0 + 4)
                    pe.wait_ge(gates_ready, i + 1)
                    pe.transpose(ring[1][0:NSEG, 0:P], gates[:, 0:NSEG], ident[:, :]).then_inc(job_full, 1)
                    pe.wait_ge(pv_ready, i + 1)
                    for j in range(3):
                        start(r0 + 5 + j)
                        bank = ring[(5 + j) % RING][:, 0:STC]
                        mm(bank, tri[:, :], pv[:, j * STC:(j + 1) * STC], True, False)
                        mm(bank, last_seg[:, :], state[:, j * STC:(j + 1) * STC], False, True).then_inc(job_full, 1)
                    for j in range(3):
                        start(r0 + 8 + j)
                        mm(ring[(8 + j) % RING][0:NSEG, 0:STC], ends_t[:, :], pv[:, j * STC:(j + 1) * STC])\
                            .then_inc(job_full, 1)
                    pe.wait_ge(gT_ready, i + 1)
                    pe.wait_ge(state_ready, i + 1)
                    for j in range(2):
                        start(r0 + 11 + j)
                        mm(ring[(11 + j) % RING][:, :], gT[:, :], state[:, j * HALF:(j + 1) * HALF]).then_inc(job_full, 1)
                    start(r0 + 13)
                    pe.wait_ge(lin_ready, i + 1)
                    pe.transpose(ring[1][:, 0:P], lin[:, :], ident[:, :]).then_inc(job_full, 1)
                    start(r0 + 14)
                    pe.wait_ge(linT_ready, i + 1)
                    mm(ring[2][:, 0:D], linT[:, :], wT[:, 3, :]).then_inc(job_full, 1)

                with pe.Fori(0, G) as g:
                    gi = b * G + g
                    r0 = ring_base(b) + GROUP_AT + g * JOBS_GROUP
                    pe.wait_ge(wgrp_ready, gi + 1)
                    for n in range(4):
                        start(r0 + n)
                        mm(ring[n % RING][:, :], w_grp[:, 1 - n // 2, :], hT[:, (n % 2) * HALF:(n % 2 + 1) * HALF])\
                            .then_inc(job_full, 1)
                    for n in range(2):
                        start(r0 + 4 + n)
                        for t in range(HT):
                            at = ring[(4 + n) % RING][:, t * P:(t + 1) * P]
                            tile = n * HT + t
                            mm(at, hT[:, tile * P:(tile + 1) * P], wv_pad[:, bass.ds(g, 1), :].rearrange("p a n -> p (a n)"),
                               True, False)
                            ins = mm(at, ones_row[:, :], bv_pad[:, bass.ds(g, 1), :, :].rearrange("p a j r -> p (a j r)"),
                                     False, True)
                        ins.then_inc(job_full, 1)
                    pe.wait_ge(kqv_ready, gi + 1)
                    for m in range(MAXES):
                        qt, kk, hh = m // 4, (m // 2) % 2, m % 2
                        pe.wait_ge(max_free, gi * MAXES + m + 1)
                        for j in (2 * hh, 2 * hh + 1):
                            ins = mm(score[:, j, :], qb[32 * j:32 * j + DK, qt * P:(qt + 1) * P],
                                     kb[32 * j:32 * j + DK, kk * HALF:(kk + 1) * HALF])
                        ins.then_inc(max_full, 1)
                    pe.wait_ge(mneg_ready, gi + 1)
                    for n in range(2):
                        start(r0 + 6 + n)
                        mm(ring[n][:, :], w_grp[:, 0, :], hT[:, n * HALF:(n + 1) * HALF], True, False, skip_group_check=True)
                        for t in range(HT):
                            ins = mm(ring[n][:, t * P:(t + 1) * P], mneg[:, n * HT + t, :], ident[:, :], False,
                                     t == HT - 1, skip_group_check=True)
                        ins.then_inc(job_full, 1)
                    pe.wait_ge(qf_ready, gi + 1)
                    pe.wait_ge(max_free, (gi + 1) * MAXES + 2)

                    def scores(s):
                        qh, kt = s // TILES, s % TILES
                        for half in range(2):
                            if s >= 1:
                                pe.wait_ge(exp_done, gi * 2 * STEPS + 2 * (s - 1) + half + 1)
                            for j in (2 * half, 2 * half + 1):
                                ins = mm(score[:, j, :], kf[32 * j:32 * j + DK + 1, kt * P:(kt + 1) * P],
                                         qf[32 * j:32 * j + DK + 1, qh * HALF:(qh + 1) * HALF])
                            ins.then_inc(score_full, 1)

                    def weigh(s):
                        qh, kt = s // TILES, s % TILES
                        pe.wait_ge(exp_done, gi * 2 * STEPS + 2 * s + 2)
                        if s == TILES:
                            pe.wait_ge(o_out, gi * 2 + 1)
                        for j in range(HG):
                            ins = mm(o_ps[32 * j:32 * j + 32, :], vf[:, kt, 32 * j:32 * j + 32], ebuf[:, s % 2, j, :],
                                     kt == 0, kt == TILES - 1)
                        ins.then_inc(e_used, 1)

                    scores(0)
                    for s in range(STEPS):
                        if s + 1 < STEPS:
                            scores(s + 1)
                        weigh(s)
                    for n in range(4):
                        if n % 2 == 0:
                            pe.wait_ge(o_out, gi * 2 + n // 2 + 1)
                        start(r0 + 8 + n)
                        for t in range(2):
                            tile = 2 * n + t
                            ins = pe.transpose(ring[(8 + n) % RING][:, t * P:(t + 1) * P],
                                               ot[:, tile * P:(tile + 1) * P], ident[:, :])
                        ins.then_inc(job_full, 1)

                pe.wait_ge(group_done, (b + 1) * G + 1)
                for hb in range(2):
                    hi = b * 2 + hb
                    r0 = ring_base(b) + ROUTE_AT + hb * 6
                    start(r0)
                    for t in range(HT):
                        ins = pe.transpose(ring[0][:, t * P:(t + 1) * P], on[:, hb * HT + t, :], ident[:, :])
                    ins.then_inc(job_full, 1)
                    start(r0 + 1)
                    pe.wait_ge(onT_ready, hi + 1)
                    for t in range(HT):
                        mm(ring[1][:, t * P:(t + 1) * P], onT[:, t * P:(t + 1) * P], wo_f[:, :], True, False)
                        ins = mm(ring[1][:, t * P:(t + 1) * P], ones_row[:, :], bo_row[:, :], False, True)
                    ins.then_inc(job_full, 1)
                    start(r0 + 2)
                    pe.wait_ge(z2_ready, hi + 1)
                    for t in range(HT):
                        ins = pe.transpose(ring[2][:, t * P:(t + 1) * P], z2[:, t, :], ident[:, :])
                    ins.then_inc(job_full, 1)
                    start(r0 + 3)
                    pe.wait_ge(h2T_ready, hi + 1)
                    for t in range(HT):
                        at = ring[0][:, t * EXPERTS:(t + 1) * EXPERTS]
                        tile = hb * HT + t
                        mm(at, h2T[:, tile * P:(tile + 1) * P], gate_sb[:, :], True, False)
                        ins = mm(at, ones_row[:, :], gateb_row[:, :], False, True)
                    ins.then_inc(job_full, 1)
                    start(r0 + 4)
                    pe.wait_ge(ew_ready, hi + 1)
                    for t in range(HT):
                        ins = pe.transpose(ring[1][0:EXPERTS, t * P:(t + 1) * P], ew[:, hb * HT + t, :], ident[:, :])
                    ins.then_inc(job_full, 1)
                    start(r0 + 5)
                    pe.wait_ge(ewT_ready, hi + 1)
                    for t in range(HT):
                        ins = mm(ring[2][:, t * P:(t + 1) * P], ewT[:, t * P:(t + 1) * P], b2_sb[:, :])
                    ins.then_inc(job_full, 1)

                with pe.Fori(0, EXPERTS // 2) as e2:
                    for k in range(2):
                        ei = (b * (EXPERTS // 2) + e2) * 2 + k
                        r0 = ring_base(b) + EXPERT_AT + (e2 * 2 + k) * JOBS_EXPERT
                        pe.wait_ge(w_loaded[k], (b * (EXPERTS // 2) + e2 + 1) * 32)
                        for tb in range(2):
                            for c in range(FC):
                                start(r0 + tb * 6 + c)
                                mm(ring[c % RING][:, :], w1_buf[k][:, c * P:(c + 1) * P],
                                   h2T[:, tb * HALF:(tb + 1) * HALF]).then_inc(job_full, 1)
                            pe.wait_ge(hid_ready, ei * 2 + tb + 1)
                            for q in range(2):
                                start(r0 + tb * 6 + 4 + q)
                                for t in range(2):
                                    for c in range(FC):
                                        ins = mm(ring[(4 + q) % RING][:, t * D:(t + 1) * D],
                                                 hid[:, tb, c, (2 * q + t) * P:(2 * q + t + 1) * P],
                                                 w2_buf[k][:, c, :], c == 0, c == FC - 1)
                                ins.then_inc(job_full, 1)


_INS = ['L0_attn_x', 'L0_attn_norm_w', 'L0_attn_Wq', 'L0_attn_Wk', 'L0_attn_Wv', 'L0_attn_Wo', 'L0_attn_Wu',
        'L0_ffn_ln1_g', 'L0_ffn_ln1_b', 'L0_ffn_w_qkv', 'L0_ffn_b_qkv', 'L0_ffn_w_o', 'L0_ffn_b_o',
        'L0_ffn_ln2_g', 'L0_ffn_ln2_b', 'L0_ffn_gate_w', 'L0_ffn_gate_b', 'L0_ffn_W1', 'L0_ffn_b1',
        'L0_ffn_W2', 'L0_ffn_b2']
_OUTS = [((B, T, D), 'float32')]


def kernel(**inputs):
    import numpy as _np
    import concourse.bacc as _bacc
    from concourse import mybir as _mybir
    from concourse.bass_utils import run_bass_kernel_spmd as _run

    nc = _bacc.Bacc("TRN2", target_bir_lowering=False, num_devices=1)
    arrays, args = {}, []
    for name in _INS:
        a = _np.ascontiguousarray(inputs[name])
        arrays[f"in_{name}_dram"] = a
        args.append(nc.dram_tensor(f"in_{name}_dram", a.shape, _mybir.dt.from_np(a.dtype), kind="ExternalInput").ap())
    for i, (shape, dtype) in enumerate(_OUTS):
        dt = _mybir.dt.from_np(_np.dtype(dtype))
        args.append(nc.dram_tensor(f"out_{i}_dram", shape, dt, kind="ExternalOutput").ap())
    program(nc, *args)
    r = _run(nc, [arrays], core_ids=[0])
    return r.results[0]["out_0_dram"]
```

```python
import concourse.bass as bass
from concourse import mybir
from contextlib import ExitStack

FP32 = mybir.dt.float32
BF16 = mybir.dt.bfloat16
I32 = mybir.dt.int32
U32 = mybir.dt.uint32
ALU = mybir.AluOpType
ACT = mybir.ActivationFunctionType
X_AXIS = mybir.AxisListType.X

B, T, D = 4, 1024, 128
P = 128
TILES = T // P
H, DK = 16, 8
SEG = 32
NSEG = T // SEG
TSEG = P // SEG
EXPERTS, DFF = 8, 512
FC = DFF // P
HG = 4
G = H // HG
HALF = T // 2
HT = TILES // 2
PVW = H * DK * DK
ZW = H * DK
EPS_LN, EPS_RMS = 1e-5, 1e-6
ATT_SCALE = float(DK) ** -0.5
GATE_SCALE = float(D) ** -0.5
MASKED = -1e30
RING = 3
RSQRT_MAGIC = 0x5F3759DF


Q_PARTS = (0, 0, 0, 1, 1, 2)
K_PARTS = (0, 1, 2, 0, 1, 0)
QK_ROWS = DK * len(Q_PARTS)
SC_ROWS = QK_ROWS + 3
PAIRS = H // 2
BUFS = 4
HW = DK * DK + DK
STC = H * HW // 4

SETUP_JOBS = 3
PRE_JOBS = 9
MAX_JOBS = 33
ROUTE_JOBS = 12
UNIT_JOBS = 51
EXPERT_D, EXPERT_A = 4, 8
LOOP_JOBS = ROUTE_JOBS + PRE_JOBS + PAIRS * (UNIT_JOBS + EXPERT_D)
FIRST_AT = SETUP_JOBS + PRE_JOBS + MAX_JOBS + PRE_JOBS
LOOP_AT = FIRST_AT + PAIRS * UNIT_JOBS
TAIL_AT = LOOP_AT + (B - 1) * LOOP_JOBS


MAX_STEPS = [((6 * s, 6 * s + 3), (6 * s + 3, 6 * s + 6)) for s in range(5)] + [((30, 32), (32, 32))] \
    + [((32, 32), (32, 32))] * 2
RELU_AT = (6, 15, 25, 34)


class Ring:

    def __init__(self, banks, free_d, free_a, at_d, at_a):
        self.banks, self.free, self.at = banks, (free_d, free_a), (at_d, at_a)
        self.n, self.made, self.users = 0, [0, 0], [(0, i - RING) for i in range(RING)]

    def start(self, pe, who=0):
        bank = self.n % RING
        user, index = self.users[bank]
        pe.wait_ge(self.free[user], self.at[user] + index + 1 + (RING, 1)[user])
        self.users[bank] = (who, self.made[who])
        self.made[who] += 1
        self.n += 1
        return self.banks[bank]


class Taker:

    def __init__(self, banks, full, at):
        self.banks, self.full, self.at, self.n, self.k = banks, full, at, 0, 0

    def skip(self, jobs=1):
        self.n += jobs

    def take(self, engine):
        engine.wait_ge(self.full, self.at + self.k + 1)
        self.k += 1
        self.n += 1
        return self.banks[(self.n - 1) % RING]


def program(nc, x, norm_w, Wq, Wk, Wv, Wo, Wu, ln1_g, ln1_b, w_qkv, b_qkv, w_o, b_o,
            ln2_g, ln2_b, gate_w, gate_b, W1, b1, W2, b2, out):
    with ExitStack() as ctx:
        def sb(name, shape, dt=FP32):
            return ctx.enter_context(nc.sbuf_tensor(name, shape, dt))

        def sem(name):
            return ctx.enter_context(nc.semaphore(name))

        ident = sb("ident", [P, P])
        tri = sb("tri", [P, P])
        seg_mean = sb("seg_mean", [P, TSEG, SEG])
        seg_ends = sb("seg_ends", [P, TILES, NSEG])
        seg_mask = sb("seg_mask", [P, TILES, NSEG])
        last_seg = sb("last_seg", [P, P])
        ones_row = sb("ones_row", [1, P])
        iota8 = sb("iota8", [P, EXPERTS])
        wnat = sb("wnat", [P, 5, P])
        wT = sb("wT", [P, 5, P])
        b1_rows = sb("b1_rows", [EXPERTS * FC, P])
        vec_rows = sb("vec_rows", [7, P])
        cols = sb("cols", [P, 39])
        b1_cols = cols[:, 0:32]
        nw_col, g1_col, c1_col, g2_col, c2_col, bq_col, bk_col = (cols[:, 32 + i:33 + i] for i in range(7))
        wqkv = sb("wqkv", [P, 3 * D])
        bv_row = sb("bv_row", [1, D])
        bv_all = sb("bv_all", [P, D])
        wo_f = sb("wo_f", [P, D])
        bo_row = sb("bo_row", [1, D])
        gate_sb = sb("gate_sb", [P, EXPERTS])
        gateb_row = sb("gateb_row", [1, EXPERTS])
        b2_sb = sb("b2_sb", [EXPERTS, D])
        w1_buf = [sb(f"w1_buf{i}", [P, DFF]) for i in range(2)]
        w2_buf = [sb(f"w2_buf{i}", [P, FC, D]) for i in range(2)]
        xin = sb("xin", [P, TILES, D])
        bn6 = sb("bn6", [P, TILES, 6])
        mv = sb("mv", [P, TILES, 2])
        var3 = sb("var3", [P, 3, TILES])
        rs3 = sb("rs3", [P, 3, TILES])
        r13 = sb("r13", [P, TILES])
        rtmp = sb("rtmp", [P, 3 * TILES])
        rtmp2 = sb("rtmp2", [P, 3 * TILES])
        xh = sb("xh", [P, TILES, D])
        hT = sb("hT", [P, T])
        q_f = sb("q_f", [P, HALF])
        q_r = sb("q_r", [P, HALF])
        parts = sb("parts", [P, 2, 3, T], BF16)
        xs_all = sb("xs_all", [P, 2 * TILES, D])
        rms_all = sb("rms_all", [P, (B + 1) * TILES])
        v_all = sb("v_all", [P, 2 * PAIRS, TILES, 2 * DK])
        s_all = sb("s_all", [P, 2 * TILES, D])
        acc = sb("acc", [P, 2 * TILES, D])
        xs = sb("xs", [P, 2, D])
        xT = sb("xT", [P, P])
        xnT = sb("xnT", [P, P])
        qk_min = sb("qk_min", [P, 2 * D])
        qk_pos = sb("qk_pos", [P, 2 * D])
        qk_exp = sb("qk_exp", [P, 2 * D])
        pqk = sb("pqk", [P, 2 * D])
        v_t = sb("v_t", [P, D])
        pv = sb("pv", [P, H, HW])
        u_both = sb("u_both", [P, 2, D])
        um = sb("um", [P, D])
        mT = sb("mT", [P, NSEG])
        msum = sb("msum", [P, TSEG])
        sc = sb("sc", [P, NSEG + 1])
        mx1 = sb("mx1", [P, 1])
        nb1 = sb("nb1", [P, 1])
        eg = sb("eg", [P, NSEG + 1])
        egsum = sb("egsum", [P, 1])
        egr = sb("egr", [P, 1])
        gates = sb("gates", [P, 4, NSEG])
        gate_cur = sb("gate_cur", [P, 1])
        gT = sb("gT", [P, P])
        ends_t = sb("ends_t", [P, NSEG])
        state = sb("state", [P, 4, HW])
        prod = sb("prod", [P, PVW])
        prodz = sb("prodz", [P, ZW])
        prodr = sb("prodr", [P, PVW])
        num = sb("num", [P, ZW])
        den = sb("den", [P, H])
        rden = sb("rden", [P, H])
        lin = sb("lin", [P, D])
        linT = sb("linT", [P, P])
        hret = sb("hret", [P, D])
        xout = sb("xout", [P, D])
        qs = [sb(f"qs{i}", [P, T], BF16) for i in range(BUFS)]
        ks = [sb(f"ks{i}", [P, T], BF16) for i in range(BUFS)]
        vbuf = [sb(f"vbuf{i}", [P, TILES, 2, 32]) for i in range(2)]
        mx = sb("mx", [P, 2, 2, TILES])
        mneg = sb("mneg", [P, 2, TILES])
        mres = sb("mres", [P, 2, TILES])
        mparts = sb("mparts", [P, P])
        mrow16 = sb("mrow16", [P, 2, 3, TILES], BF16)
        mrows = sb("mrows", [2 * 3 * TILES, P], BF16)
        ebuf = sb("ebuf", [P, 2, 4, HALF])
        ot = sb("ot", [P, HALF])
        osum = sb("osum", [P, 2, 2, 4])
        on = sb("on", [P, TILES, D])
        onT = sb("onT", [P, HALF])
        x2 = sb("x2", [P, HT, D])
        z2 = sb("z2", [P, HT, D])
        h2T = sb("h2T", [P, T])
        logit = sb("logit", [P, HT, EXPERTS])
        top8 = sb("top8", [P, HT, 8])
        idx8 = sb("idx8", [P, HT, 8], U32)
        idxf = sb("idxf", [P, HT, 8])
        tdiff = sb("tdiff", [P, HT])
        texp = sb("texp", [P, HT])
        tone = sb("tone", [P, HT])
        w_top = sb("w_top", [P, 2, HT])
        pick = sb("pick", [P, 2, HT, EXPERTS])
        ew = sb("ew", [P, TILES, EXPERTS])
        ewT = sb("ewT", [EXPERTS, HALF])
        b1_t = sb("b1_t", [P, FC])
        hid = sb("hid", [P, 2, FC, HALF])
        sg_e = sb("sg_e", [P, TILES, D])
        fin = sb("fin", [P, TILES, D])

        psum = ctx.enter_context(nc.psum_tensor("psum", [P, 8, HALF], FP32))
        score = psum[:, 0:4, :]
        o_ps = psum[:, 4, :]
        ring = [psum[:, 5 + i, :] for i in range(RING)]

        scratch = nc.dram_tensor("qk_parts", (2, (B + 1) * H, QK_ROWS, T), BF16, kind="Internal").ap()

        ld_w = sem("ld_w")
        pool_const = sem("pool_const")
        pool_step = sem("pool_step")
        dve_step = sem("dve_step")
        setup_done = sem("setup_done")
        full_d = sem("full_d")
        free_d = sem("free_d")
        full_a = sem("full_a")
        free_a = sem("free_a")
        x_loaded = sem("x_loaded")
        x_used = sem("x_used")
        hT_ready = sem("hT_ready")
        xh_ready = sem("xh_ready")
        parts_ready = sem("parts_ready")
        parts_out = sem("parts_out")
        v_ready = sem("v_ready")
        pair_loaded = [sem(f"pair_loaded{i}") for i in range(BUFS)]
        vbuf_ready = sem("vbuf_ready")
        mparts_ready = sem("mparts_ready")
        mrows_ready = sem("mrows_ready")
        mrows_loaded = sem("mrows_loaded")
        score_full = sem("score_full")
        exp_done = sem("exp_done")
        e_used = sem("e_used")
        o_out = sem("o_out")
        unit_done = sem("unit_done")
        xs_ready = sem("xs_ready")
        xT_ready = sem("xT_ready")
        qkmin_ready = sem("qkmin_ready")
        qkexp_ready = sem("qkexp_ready")
        pq_ready = sem("pq_ready")
        pv_ready = sem("pv_ready")
        uT_ready = sem("uT_ready")
        nb_ready = sem("nb_ready")
        eg_ready = sem("eg_ready")
        gates_ready = sem("gates_ready")
        gT_ready = sem("gT_ready")
        state_ready = sem("state_ready")
        lin_ready = sem("lin_ready")
        linT_ready = sem("linT_ready")
        on_ready = sem("on_ready")
        onT_ready = sem("onT_ready")
        z2_ready = sem("z2_ready")
        h2T_ready = sem("h2T_ready")
        tdiff_ready = sem("tdiff_ready")
        texp_ready = sem("texp_ready")
        ew_ready = sem("ew_ready")
        ewT_ready = sem("ewT_ready")
        w_loaded = [sem(f"w_loaded{i}") for i in range(2)]
        acc_ready = sem("acc_ready")
        b1_ready = sem("b1_ready")
        sg_exp = sem("sg_exp")
        sg_ready = sem("sg_ready")
        fin_step = sem("fin_step")
        fin_loaded = sem("fin_loaded")
        fin_done = sem("fin_done")
        stored = sem("stored")

        x_dram = x.rearrange("b (t p) d -> b p t d", p=P)
        out_dram = out.rearrange("b (t p) d -> b p t d", p=P)
        w1_dram = W1.rearrange("e d f -> (e d) f")
        w2_dram = W2.rearrange("e (c p) d -> e p c d", p=P)
        N_LOADS = 20

        def row(v):
            return v.rearrange("(a n) -> a n", a=1)

        def base_d(b):
            return LOOP_AT + (b - 1) * LOOP_JOBS

        def settled(eng):
            eng.wait_ge(pool_const, 2)

        block = ctx.enter_context(nc.Block())

        @block.sync
        def _(sp):
            def load_x(src, count):
                sp.wait_ge(x_used, count + 1)
                sp.dma_start(xin[:, :, :], src).then_inc(x_loaded, 16)

            def write_parts(pb):
                sp.wait_ge(parts_ready, pb + 1)
                for w, which in enumerate((Q_PARTS, K_PARTS)):
                    for slot, part in enumerate(which):
                        sp.dma_start(scratch[w, bass.ds(pb * H, H), slot * DK:(slot + 1) * DK, :],
                                     parts[:, w, part, :]).then_inc(parts_out, 16)

            def load_pair(pi, r):
                for w, buf in enumerate((qs[r], ks[r])):
                    for hd in range(2):
                        sp.dma_start(buf[64 * hd:64 * hd + QK_ROWS, :],
                                     scratch[w, bass.ds(pi * 2 + hd, 1)].rearrange("a r n -> (a r) n"))\
                            .then_inc(pair_loaded[r], 16)

            def load_maxima(pi, r):
                sp.wait_ge(mrows_ready, pi + 1)
                for hd in range(2):
                    sp.dma_start(qs[r][64 * hd + QK_ROWS:64 * hd + SC_ROWS, :],
                                 mrows[3 * TILES * hd:3 * TILES * (hd + 1), :]).then_inc(mrows_loaded, 16)

            def load_expert(ei, e, r):
                sp.wait_ge(acc_ready, ei + 1)
                sp.dma_start(w1_buf[r][:, :], w1_dram[bass.ds(e * D, D), :]).then_inc(w_loaded[r], 16)
                sp.dma_start(w2_buf[r][:, :, :], w2_dram[bass.ds(e, 1)].rearrange("a p c d -> p (a c) d"))\
                    .then_inc(w_loaded[r], 16)

            def load_final(b):
                sp.wait_ge(stored, b * 16 + 16)
                sp.dma_start(fin[:, :, :], x_dram[bass.ds(b, 1)].rearrange("a p t d -> p (a t) d"))\
                    .then_inc(fin_loaded, 16)

            def store(b):
                sp.wait_ge(fin_done, b + 3)
                sp.dma_start(out_dram[bass.ds(b, 1)].rearrange("a p t d -> p (a t) d"), fin[:, :, :])\
                    .then_inc(stored, 16)

            sp.dma_start(xin[:, :, :], x_dram[0]).then_inc(x_loaded, 16)
            for i, w in enumerate((Wq, Wk, Wv, Wo, Wu)):
                sp.dma_start(wnat[:, i, :], w).then_inc(ld_w, 16)
            sp.dma_start(b1_rows[:, :], b1.rearrange("e (c p) -> (e c) p", p=P)).then_inc(ld_w, 16)
            for i, v in enumerate((norm_w, ln1_g, ln1_b, ln2_g, ln2_b, b_qkv[0:D], b_qkv[D:2 * D])):
                sp.dma_start(vec_rows[i:i + 1, :], row(v)).then_inc(ld_w, 16)
            sp.dma_start(wqkv[:, :], w_qkv).then_inc(ld_w, 16)
            sp.dma_start(bv_row[:, :], row(b_qkv[2 * D:3 * D])).then_inc(ld_w, 16)
            sp.dma_start(wo_f[:, :], w_o).then_inc(ld_w, 16)
            sp.dma_start(bo_row[:, :], row(b_o)).then_inc(ld_w, 16)
            sp.dma_start(gate_sb[:, :], gate_w).then_inc(ld_w, 16)
            sp.dma_start(gateb_row[:, :], row(gate_b)).then_inc(ld_w, 16)
            sp.dma_start(b2_sb[:, :], b2).then_inc(ld_w, 16)
            write_parts(0)
            load_x(x_dram[1], 1)
            sp.wait_ge(pool_const, 2)
            sp.wait_ge(parts_out, 12 * 16 + 16)
            load_pair(0, 0)
            load_pair(1, 1)
            load_maxima(0, 0)
            write_parts(1)
            load_x(x_dram[2], 2)

            def unit(ui, r, batches, ei=None, e=None):
                if ei is not None:
                    load_expert(ei, e, r % 2)
                sp.wait_ge(parts_out, batches * 12 * 16 + 16)
                sp.wait_ge(unit_done, ui + 1)
                load_pair(ui + 2, (r + 2) % BUFS)
                load_maxima(ui + 1, (r + 1) % BUFS)

            with sp.Fori(0, PAIRS // BUFS) as it:
                for r in range(BUFS):
                    unit(it * BUFS + r, r, 2)
            with sp.Fori(1, B) as b:
                write_parts(b + 1)
                load_x(x_dram[B - 1], b + 2)
                with sp.Fori(0, PAIRS // BUFS) as it:
                    for r in range(BUFS):
                        u = it * BUFS + r
                        unit(b * PAIRS + u, r, b + 2, (b - 1) * EXPERTS + u, u)
                load_final(b - 1)
                store(b - 1)
            with sp.Fori(0, EXPERTS // 2) as e2:
                for r in range(2):
                    load_expert((B - 1) * EXPERTS + e2 * 2 + r, e2 * 2 + r, r)
            load_final(B - 1)
            store(B - 1)
            sp.wait_ge(stored, 16 * (B + 1))
            sp.wait_ge(mrows_loaded, 32 * (B * PAIRS + 1))
            sp.wait_ge(x_loaded, 16 * (B + 2))
            for r in range(BUFS):
                sp.wait_ge(pair_loaded[r], 64 * (B * PAIRS // BUFS + (1 if r < 2 else 0)))

        @block.gpsimd
        def _(pool):
            step = 0

            def link(ins):
                nonlocal step
                step += 1
                ins.then_inc(pool_step, 1)
                pool.wait_ge(pool_step, step)

            pool.memset(ones_row[:, :], 1.0)
            pool.memset(ident[:, :], 0.0)
            pool.memset(tri[:, :], 1.0)
            pool.memset(seg_ends[:, :, :], 1.0)
            pool.memset(seg_mask[:, :, :], 0.0)
            pool.memset(last_seg[:, :], 0.0)
            pool.memset(mT[:, :], 0.0)
            pool.memset(mparts[:, :], 0.0)
            for i in range(2):
                link(pool.memset(vbuf[i][:, :, :, :], 0.0))
            for i in range(BUFS):
                link(pool.memset(ks[i][32:64, :], 1.0))
                link(pool.memset(ks[i][96:128, :], 1.0))
            for c in range(SEG):
                pool.memset(seg_mean[:, :, c:c + 1], 1.0 / (c + 1))
            link(pool.iota(iota8[:, :], [[1, EXPERTS]], base=0, channel_multiplier=0,
                           allow_small_or_imprecise_dtypes=True))
            for i in range(2):
                pool.memset(vbuf[i][:, :, :, DK:DK + 1], 1.0)
            pool.affine_select(out=ident[:, :], in_=ident[:, :], compare_op=ALU.not_equal, fill=1.0, base=0,
                               pattern=[[-1, P]], channel_multiplier=1)
            pool.affine_select(out=tri[:, :], in_=tri[:, :], compare_op=ALU.is_ge, fill=0.0, base=0,
                               pattern=[[1, P]], channel_multiplier=-1)
            link(pool.affine_select(out=seg_mean[:, :, :], in_=seg_mean[:, :, :], compare_op=ALU.is_ge, fill=0.0,
                                    base=0, pattern=[[SEG, TSEG], [1, SEG]], channel_multiplier=-1))
            pool.affine_select(out=seg_mean[:, :, :], in_=seg_mean[:, :, :], compare_op=ALU.is_ge, fill=0.0,
                               base=0, pattern=[[-SEG, TSEG], [0, SEG]], channel_multiplier=1)
            pool.affine_select(out=seg_ends[:, :, :], in_=seg_ends[:, :, :], compare_op=ALU.is_ge, fill=0.0,
                               base=SEG - 1, pattern=[[-P, TILES], [SEG, NSEG]], channel_multiplier=-1)
            for j in range(4):
                link(pool.affine_select(out=last_seg[:, :], in_=last_seg[:, :], compare_op=ALU.not_equal, fill=1.0,
                                        base=-(NSEG * j + NSEG - 1), pattern=[[0, P]], channel_multiplier=1))
            pool.affine_select(out=seg_mask[:, :, :], in_=seg_mask[:, :, :], compare_op=ALU.is_ge, fill=MASKED,
                               base=-SEG, pattern=[[P, TILES], [-SEG, NSEG]], channel_multiplier=1)\
                .then_inc(pool_const, 2)

            def values(pi, r):
                pool.tensor_copy(vbuf[r % 2][:, :, :, 0:DK],
                                 v_all[:, bass.ds(pi & (2 * PAIRS - 1), 1), :, :].rearrange("p a t (h d) -> p (a t) h d", d=DK))\
                    .then_inc(vbuf_ready, 1)

            def unit(ui, r, batches):
                pool.wait_ge(v_ready, batches)
                pool.wait_ge(unit_done, ui + 2)
                values(ui + 1, r + 1)
                pool.wait_ge(qkexp_ready, ui + 1)
                pool.tensor_tensor(pqk[:, :], qk_exp[:, :], qk_pos[:, :], ALU.add).then_inc(pq_ready, 1)
                pool.wait_ge(pq_ready, ui + 1)
                keys = pqk[:, D:2 * D].rearrange("p (h k) -> p h k", k=DK)
                vals = v_t[:, :].rearrange("p (h v) -> p h v", v=DK)
                pool.tensor_tensor(pv[:, :, 0:DK * DK].rearrange("p h (k v) -> p h k v", k=DK),
                                   keys.unsqueeze(3).broadcast_to([P, H, DK, DK]),
                                   vals.unsqueeze(2).broadcast_to([P, H, DK, DK]), ALU.mult)
                pool.tensor_copy(pv[:, :, DK * DK:HW], keys).then_inc(pv_ready, 1)

            def final(b):
                tl = bass.ds((b & 1) * TILES, TILES)
                pool.wait_ge(sg_ready, b + 1)
                pool.tensor_tensor(sg_e[:, :, :], acc[:, tl, :], sg_e[:, :, :], ALU.mult).then_inc(fin_step, 1)
                pool.wait_ge(fin_step, b * 2 + 1)
                pool.tensor_tensor(sg_e[:, :, :], sg_e[:, :, :], s_all[:, tl, :], ALU.mult).then_inc(fin_step, 1)
                pool.wait_ge(fin_step, b * 2 + 2)
                pool.wait_ge(fin_loaded, b * 16 + 16)
                pool.tensor_tensor(fin[:, :, :], fin[:, :, :], sg_e[:, :, :], ALU.add).then_inc(fin_done, 1)

            pool.wait_ge(v_ready, 1)
            values(0, 0)
            with pool.Fori(0, PAIRS // BUFS) as it:
                for r in range(BUFS):
                    unit(it * BUFS + r, r, 2)
            with pool.Fori(1, B) as b:
                with pool.Fori(0, PAIRS // BUFS) as it:
                    for r in range(BUFS):
                        unit(b * PAIRS + it * BUFS + r, r, b + 2)
                final(b - 1)
            final(B - 1)

        @block.scalar
        def _(act):
            def exps(ui, s):
                for half in range(2):
                    act.wait_ge(score_full, ui * 2 * TILES + 2 * s + half + 1)
                    act.wait_ge(e_used, ui * TILES + s + 1)
                    act.activation(ebuf[:, s % 2, 2 * half:2 * half + 2, :], score[:, 2 * half:2 * half + 2, :],
                                   ACT.Exp, scale=ATT_SCALE).then_inc(exp_done, 1)

            def bias(ei, e):
                act.wait_ge(free_a, ei * EXPERT_A + 1)
                act.activation(b1_t[:, :], b1_cols[:, bass.ds(e * FC, FC)], ACT.Copy).then_inc(b1_ready, 1)
                act.wait_ge(b1_ready, ei + 1)

            def hidden(job, c):
                for tb in range(2):
                    bank = job.take(act)
                    act.activation(hid[:, tb, c, :], bank[:, :], ACT.Relu, bias=b1_t[:, c:c + 1])\
                        .then_inc(free_a, 1)

            def unit(ui, job=None, ei=None, e=None):
                exps(ui, 0)
                if job is not None:
                    bias(ei, e)
                for s in range(TILES):
                    if s + 1 < TILES:
                        exps(ui, s + 1)
                    if job is not None and s < FC:
                        job.n = RELU_AT[s]
                        hidden(job, s)
                    if s == 1:
                        act.wait_ge(qkmin_ready, ui + 1)
                        act.activation(qk_exp[:, :], qk_min[:, :], ACT.Exp).then_inc(qkexp_ready, 1)
                    if s == 2:
                        act.wait_ge(nb_ready, ui + 1)
                        act.activation(eg[:, :], sc[:, :], ACT.Exp, bias=nb1[:, 0:1], scale=GATE_SCALE,
                                       accum_out=egsum[:, 0:1]).then_inc(eg_ready, 1)

            def route(b):
                for hb in range(2):
                    act.wait_ge(tdiff_ready, b * 2 + hb + 1)
                    act.activation(texp[:, :], tdiff[:, :], ACT.Exp).then_inc(texp_ready, 1)

            def silu(b):
                act.wait_ge(acc_ready, (b + 1) * EXPERTS + 2)
                act.wait_ge(fin_done, b + 2)
                settled(act)
                act.activation(sg_e[:, :, :], acc[:, bass.ds((b & 1) * TILES, TILES), :], ACT.Exp, scale=-1.0)\
                    .then_inc(sg_exp, 1)

            with act.Fori(0, PAIRS // BUFS) as it:
                for r in range(BUFS):
                    unit(it * BUFS + r)
            with act.Fori(1, B) as b:
                route(b - 1)
                with act.Fori(0, PAIRS // BUFS) as it:
                    for r in range(BUFS):
                        u = it * BUFS + r
                        ei = (b - 1) * EXPERTS + u
                        unit(b * PAIRS + u, Taker(ring, full_a, ei * EXPERT_A), ei, u)
                silu(b - 1)
            route(B - 1)
            with act.Fori(0, EXPERTS) as e:
                bias((B - 1) * EXPERTS + e, e)
                job = Taker(ring, full_a, ((B - 1) * EXPERTS + e) * EXPERT_A)
                for c in range(FC):
                    hidden(job, c)
            silu(B - 1)

        @block.vector
        def _(dve):
            chain = [0]

            def link(ins):
                chain[0] += 1
                ins.then_inc(dve_step, 1)
                dve.wait_ge(dve_step, chain[0])

            def done():
                link(nc.vector.memset(rtmp2[:, 0:1], 0.0))

            def end_chain():
                done()
                dve.sem_clear(dve_step)
                chain[0] = 0

            def rsqrt(dst, src, w):
                a, c = rtmp[:, 0:w], rtmp2[:, 0:w]
                link(nc.vector.tensor_scalar(a.bitcast(I32), src.bitcast(I32), 1, None, ALU.arith_shift_right))
                link(nc.vector.tensor_scalar(dst.bitcast(I32), a.bitcast(I32), -1, RSQRT_MAGIC, ALU.mult, ALU.add))
                for _ in range(4):
                    link(nc.vector.tensor_tensor(c, dst, dst, ALU.mult))
                    link(nc.vector.tensor_tensor(c, c, src, ALU.mult))
                    link(nc.vector.tensor_scalar(c, c, -0.5, 1.5, ALU.mult, ALU.add))
                    link(nc.vector.tensor_tensor(dst, dst, c, ALU.mult))

            def freed(ins):
                ins.then_inc(free_d, 1)

            def pre(pb, at):
                job = Taker(ring, full_d, at)
                dve.wait_ge(x_loaded, pb * 16 + 16)
                for t in range(TILES):
                    ins = nc.vector.bn_stats(bn6[:, t, :], xin[:, t, :])
                link(ins)
                for t in range(TILES):
                    ins = nc.vector.bn_aggr(mv[:, t, :], bn6[:, t, :])
                link(ins)
                link(nc.vector.tensor_scalar(var3[:, 0, :], mv[:, :, 1], EPS_LN, None, ALU.add))
                rsqrt(rs3[:, 0, :], var3[:, 0, :], TILES)
                link(nc.vector.tensor_tensor(var3[:, 0, :], mv[:, :, 1], rs3[:, 0, :], ALU.mult))
                link(nc.vector.tensor_tensor(var3[:, 0, :], var3[:, 0, :], rs3[:, 0, :], ALU.mult))
                nc.vector.tensor_scalar(var3[:, 1, :], var3[:, 0, :], EPS_RMS, None, ALU.add)
                link(nc.vector.tensor_scalar(var3[:, 2, :], var3[:, 0, :], EPS_LN, None, ALU.add))
                rsqrt(rs3[:, 1:3, :].rearrange("p a t -> p (a t)"), var3[:, 1:3, :].rearrange("p a t -> p (a t)"),
                      2 * TILES)
                nc.vector.tensor_copy(rms_all[:, bass.ds(pb * TILES, TILES)], rs3[:, 1, :])
                link(nc.vector.tensor_tensor(r13[:, :], rs3[:, 0, :], rs3[:, 2, :], ALU.mult))
                for t in range(TILES):
                    ins = nc.vector.tensor_scalar(xh[:, t, :], xin[:, t, :], mv[:, t, 0:1], r13[:, t:t + 1],
                                                  ALU.subtract, ALU.mult)
                link(ins)
                dve.sem_inc(xh_ready, 1)
                for t in range(TILES):
                    ins = nc.vector.tensor_scalar(
                        xs_all[:, bass.ds((pb & 1) * TILES + t, 1), :].rearrange("p a d -> p (a d)"),
                        xin[:, t, :], mv[:, t, 0:1], rs3[:, 0, t:t + 1], ALU.subtract, ALU.mult)
                link(ins)
                dve.sem_inc(x_used, 1)
                for t0, tiles in ((0, 4), (4, 2), (6, 2)):
                    bank = job.take(dve)
                    freed(nc.vector.tensor_scalar(hT[:, t0 * P:(t0 + tiles) * P], bank[:, 0:tiles * P], g1_col, c1_col,
                                                  ALU.mult, ALU.add))
                done()
                dve.sem_inc(hT_ready, 1)
                dve.wait_ge(parts_out, pb * 12 * 16 + 16)
                for w, bias in enumerate((bq_col, bk_col)):
                    for n in range(2):
                        blk = slice(n * HALF, (n + 1) * HALF)
                        bank = job.take(dve)
                        freed(nc.vector.tensor_scalar(q_f[:, :], bank[:, :], bias, None, ALU.add))
                        done()
                        link(nc.vector.tensor_copy(parts[:, w, 0, blk], q_f[:, :]))
                        link(nc.vector.tensor_tensor(q_r[:, :], q_f[:, :], parts[:, w, 0, blk], ALU.subtract))
                        link(nc.vector.tensor_copy(parts[:, w, 1, blk], q_r[:, :]))
                        link(nc.vector.tensor_tensor(parts[:, w, 2, blk], q_r[:, :], parts[:, w, 1, blk], ALU.subtract))
                dve.sem_inc(parts_ready, 1)
                for n in range(2):
                    bank = job.take(dve)
                    for t in range(HT):
                        ins = nc.vector.tensor_tensor(
                            v_all[:, bass.ds((pb & 1) * PAIRS, PAIRS), n * HT + t, :],
                            bank[:, t * P:(t + 1) * P].rearrange("p (a c) -> p a c", c=2 * DK),
                            bv_all[:, :].rearrange("p (a c) -> p a c", c=2 * DK), ALU.add)
                    freed(ins)
                done()
                dve.sem_inc(v_ready, 1)

            def maxima(job, m0, m1):
                for m in range(m0, m1):
                    t, kk, hd = m // 4, (m // 2) % 2, m % 2
                    bank = job.take(dve)
                    freed(nc.vector.tensor_reduce(mx[:, kk, hd, t:t + 1], bank[:, :], X_AXIS, ALU.max))

            def split_maxima():
                done()
                link(nc.vector.tensor_tensor(mneg[:, :, :], mx[:, 0], mx[:, 1], ALU.max))
                link(nc.vector.tensor_scalar(mneg[:, :, :], mneg[:, :, :], -1.0, None, ALU.mult))
                link(nc.vector.tensor_copy(mrow16[:, :, 0, :], mneg[:, :, :]))
                link(nc.vector.tensor_tensor(mres[:, :, :], mneg[:, :, :], mrow16[:, :, 0, :], ALU.subtract))
                link(nc.vector.tensor_copy(mrow16[:, :, 1, :], mres[:, :, :]))
                link(nc.vector.tensor_tensor(mrow16[:, :, 2, :], mres[:, :, :], mrow16[:, :, 1, :], ALU.subtract))
                link(nc.vector.tensor_copy(mparts[:, 0:2 * 3 * TILES], mrow16[:, :, :, :].rearrange("p h s t -> p (h s t)")))
                dve.sem_inc(mparts_ready, 1)

            def take_maxima(job, pi):
                bank = job.take(dve)
                if pi is not None:
                    dve.wait_ge(mrows_loaded, 32 * pi)
                link(nc.vector.tensor_copy(mrows[:, :], bank[0:2 * 3 * TILES, 0:P]))
                dve.sem_inc(free_d, 1)
                dve.sem_inc(mrows_ready, 1)

            def unit(ui, u, job, acc_at=None):
                expert = acc_at is not None
                nc.vector.tensor_copy(xs[:, 0, :], xs_all[:, bass.ds(ui & (2 * TILES - 1), 1), :].rearrange("p a d -> p (a d)"))
                nc.vector.tensor_copy(ends_t[:, :], seg_ends[:, bass.ds(u, 1), :].rearrange("p a n -> p (a n)"))
                link(nc.vector.tensor_scalar(xs[:, 1, :], xs_all[:, bass.ds(ui & (2 * TILES - 1), 1), :].rearrange("p a d -> p (a d)"),
                                             rms_all[:, bass.ds(ui, 1)], None, ALU.mult))
                dve.sem_inc(xs_ready, 1)

                def times_queries(dst, bank, width, j):
                    return nc.vector.tensor_tensor(
                        dst[:, j * 256:(j + 1) * 256].rearrange("p (h k v) -> p h k v", k=DK, v=DK),
                        bank[:, 0:4 * width].rearrange("p (h x) -> p h x", x=width)[:, :, 0:DK * DK]
                        .rearrange("p h (k v) -> p h k v", k=DK),
                        pqk[:, j * 32:(j + 1) * 32].rearrange("p (h k) -> p h k", k=DK)
                        .unsqueeze(3).broadcast_to([P, 4, DK, DK]), ALU.mult)

                def sum_keys(dst, src):
                    return nc.vector.tensor_reduce(dst[:, :].rearrange("p (h v) -> p h v", v=DK),
                                                   src[:, :].rearrange("p (h k v) -> p h v k", k=DK, v=DK),
                                                   X_AXIS, ALU.add)

                def prefix(j):
                    bank = job.take(dve)
                    times_queries(prod, bank, HW, j)
                    freed(nc.vector.tensor_tensor(
                        prodz[:, j * 32:(j + 1) * 32].rearrange("p (h k) -> p h k", k=DK),
                        bank[:, 0:STC].rearrange("p (h x) -> p h x", x=HW)[:, :, DK * DK:HW],
                        pqk[:, j * 32:(j + 1) * 32].rearrange("p (h k) -> p h k", k=DK), ALU.mult))

                for s in range(TILES):
                    if s == 3:
                        dve.wait_ge(eg_ready, ui + 1)
                        link(nc.vector.reciprocal(egr[:, :], egsum[:, :]))
                        nc.vector.tensor_scalar(gates[:, :, :], eg[:, 0:NSEG].unsqueeze(1).broadcast_to([P, 4, NSEG]),
                                                egr[:, 0:1], None, ALU.mult)
                        link(nc.vector.tensor_scalar(gate_cur[:, :], eg[:, NSEG:NSEG + 1], egr[:, 0:1], None, ALU.mult))
                        dve.sem_inc(gates_ready, 1)
                    maxima(job, *MAX_STEPS[s][0])
                    if s == 6:
                        take_maxima(job, ui + 1)
                    maxima(job, *MAX_STEPS[s][1])
                    if s == 5:
                        split_maxima()
                    if s == TILES - 1:
                        dve.wait_ge(e_used, (ui + 1) * TILES + 2)
                        link(nc.vector.tensor_copy(ot[:, :], o_ps[:, :]))
                        dve.sem_inc(o_out, 1)
                        dve.sem_inc(unit_done, 1)
                    if expert:
                        if s < FC:
                            job.skip(2)
                        else:
                            bank = job.take(dve)
                            for t in range(2):
                                tile = 2 * (s - FC) + t
                                at = acc[:, bass.ds(acc_at + tile, 1), :].rearrange("p a d -> p (a d)")
                                ins = nc.vector.scalar_tensor_tensor(at, bank[:, t * D:(t + 1) * D],
                                                                     ew[:, tile, bass.ds(u, 1)], at, ALU.mult, ALU.add)
                            freed(ins)
                    if s == 0:
                        bank = job.take(dve)
                        link(nc.vector.tensor_copy(xT[:, :], bank[:, 0:P]))
                        nc.vector.tensor_reduce(msum[:, :], xT[:, :].rearrange("p (n c) -> p n c", c=SEG), X_AXIS, ALU.add)
                        link(nc.vector.tensor_scalar(xnT[:, :], bank[:, P:2 * P], nw_col, None, ALU.mult))
                        dve.sem_inc(free_d, 1)
                        link(nc.vector.tensor_scalar(mT[:, bass.ds(u * TSEG, TSEG)], msum[:, :], 1.0 / SEG, None, ALU.mult))
                        dve.sem_inc(xT_ready, 1)
                    if s == 1:
                        bank = job.take(dve)
                        nc.vector.tensor_scalar(qk_min[:, :], bank[:, 0:2 * D], 0.0, None, ALU.min)
                        nc.vector.tensor_scalar(qk_pos[:, :], bank[:, 0:2 * D], 0.0, None, ALU.max)
                        link(nc.vector.tensor_copy(v_t[:, :], bank[:, 2 * D:3 * D]))
                        dve.sem_inc(free_d, 1)
                        dve.sem_inc(qkmin_ready, 1)
                        bank = job.take(dve)
                        link(nc.vector.tensor_copy(u_both[:, :, :].rearrange("p a n -> p (a n)"), bank[:, 0:2 * D]))
                        dve.sem_inc(uT_ready, 1)
                        link(nc.vector.tensor_tensor(um[:, :], bank[:, 2 * D:3 * D], u_both[:, 1, :], ALU.mult))
                        freed(nc.vector.tensor_reduce(sc[:, NSEG:NSEG + 1], um[:, :], X_AXIS, ALU.add))
                    if s == 2:
                        bank = job.take(dve)
                        link(nc.vector.tensor_tensor(sc[:, 0:NSEG], bank[:, 0:NSEG],
                                                     seg_mask[:, bass.ds(u, 1), :].rearrange("p a n -> p (a n)"), ALU.add))
                        dve.sem_inc(free_d, 1)
                        link(nc.vector.tensor_reduce(mx1[:, :], sc[:, :], X_AXIS, ALU.max))
                        nc.vector.tensor_scalar(nb1[:, :], mx1[:, :], -GATE_SCALE, None, ALU.mult).then_inc(nb_ready, 1)
                    if s == 3:
                        bank = job.take(dve)
                        link(nc.vector.tensor_copy(gT[:, :], bank[:, 0:P]))
                        dve.sem_inc(gT_ready, 1)
                        dve.sem_inc(free_d, 1)
                        dve.wait_ge(pq_ready, ui + 1)
                        prefix(0)
                    if s == 4:
                        for j in range(1, 4):
                            prefix(j)
                    if s == 5:
                        bank = job.take(dve)
                        freed(nc.vector.tensor_tensor(state[:, :, :].rearrange("p h x -> p (h x)"), bank[:, 0:STC],
                                                      state[:, :, :].rearrange("p h x -> p (h x)"), ALU.add))
                        done()
                        dve.sem_inc(state_ready, 1)
                        sum_keys(num, prod)
                        link(nc.vector.tensor_reduce(den[:, :], prodz[:, :].rearrange("p (h k) -> p h k", k=DK),
                                                     X_AXIS, ALU.add))
                        link(nc.vector.tensor_scalar(den[:, :], den[:, :], EPS_RMS, None, ALU.add))
                        link(nc.vector.reciprocal(rden[:, :], den[:, :]))
                        nc.vector.tensor_tensor(lin[:, :].rearrange("p (h v) -> p h v", v=DK),
                                                num[:, :].rearrange("p (h v) -> p h v", v=DK),
                                                rden[:, :].unsqueeze(2).broadcast_to([P, H, DK]), ALU.mult)\
                            .then_inc(lin_ready, 1)
                    if s == 6:
                        for j in range(4):
                            freed(times_queries(prodr, job.take(dve), DK * DK, j))
                        done()
                        bank = job.take(dve)
                        link(nc.vector.tensor_copy(linT[:, :], bank[:, 0:P]))
                        dve.sem_inc(linT_ready, 1)
                        dve.sem_inc(free_d, 1)
                        link(sum_keys(hret, prodr))
                    if s == 7:
                        bank = job.take(dve)
                        link(nc.vector.tensor_tensor(xout[:, :], bank[:, 0:D], xs[:, 0, :], ALU.add))
                        freed(nc.vector.scalar_tensor_tensor(
                            s_all[:, bass.ds(ui & (2 * TILES - 1), 1), :].rearrange("p a d -> p (a d)"), xout[:, :],
                            gate_cur[:, 0:1], hret[:, :], ALU.mult, ALU.add))
                        for n in range(2):
                            bank = job.take(dve)
                            o4 = bank[:, 0:2 * P].rearrange("p (i j r) -> p i j r", i=2, r=32)
                            link(nc.vector.reciprocal(osum[:, n], o4[:, :, :, DK]))
                            for i in range(2):
                                dst = on[:, 2 * n + i:TILES:4, bass.ds(u * 2 * DK, 2 * DK)]
                                ins = nc.vector.tensor_tensor(
                                    dst.rearrange("p q (h d) -> p h q d", d=DK),
                                    o4[:, i, :, 0:DK].rearrange("p (h q) d -> p h q d", q=2),
                                    osum[:, n, i, :].rearrange("p (h q) -> p h q", q=2).unsqueeze(3)
                                    .broadcast_to([P, 2, 2, DK]), ALU.mult)
                            freed(ins)
                done()
                dve.sem_inc(on_ready, 1)
                if expert:
                    dve.sem_inc(acc_ready, 1)
                end_chain()

            def route(b, at):
                job = Taker(ring, full_d, at)
                dve.wait_ge(fin_done, b + 1)
                for hb in range(2):
                    hi = b * 2 + hb
                    tl = slice(hb * HT, (hb + 1) * HT)
                    rows = bass.ds((b & 1) * TILES + hb * HT, HT)
                    link(nc.vector.tensor_copy(onT[:, :], job.take(dve)[:, :]))
                    dve.sem_inc(onT_ready, 1)
                    dve.sem_inc(free_d, 1)
                    bank = job.take(dve)
                    link(nc.vector.tensor_tensor(x2[:, :, :], bank[:, :].rearrange("p (t d) -> p t d", d=D),
                                                 xs_all[:, rows, :], ALU.add))
                    dve.sem_inc(free_d, 1)
                    for t in range(HT):
                        ins = nc.vector.bn_stats(bn6[:, t, :], x2[:, t, :])
                    link(ins)
                    for t in range(HT):
                        ins = nc.vector.bn_aggr(mv[:, t, :], bn6[:, t, :])
                    link(ins)
                    link(nc.vector.tensor_scalar(var3[:, 0, 0:HT], mv[:, 0:HT, 1], EPS_LN, None, ALU.add))
                    rsqrt(rs3[:, 0, 0:HT], var3[:, 0, 0:HT], HT)
                    for t in range(HT):
                        ins = nc.vector.tensor_scalar(z2[:, t, :], x2[:, t, :], mv[:, t, 0:1], rs3[:, 0, t:t + 1],
                                                      ALU.subtract, ALU.mult)
                    link(ins)
                    dve.sem_inc(z2_ready, 1)
                    link(nc.vector.tensor_scalar(h2T[:, hb * HALF:(hb + 1) * HALF], job.take(dve)[:, :], g2_col, c2_col,
                                                 ALU.mult, ALU.add))
                    dve.sem_inc(h2T_ready, 1)
                    dve.sem_inc(free_d, 1)
                    link(nc.vector.tensor_copy(logit[:, :, :].rearrange("p t e -> p (t e)"),
                                               job.take(dve)[:, 0:HT * EXPERTS]))
                    dve.sem_inc(free_d, 1)
                    for t in range(HT):
                        ins = nc.vector.max(top8[:, t, :], logit[:, t, :])
                    link(ins)
                    link(nc.vector.tensor_tensor(tdiff[:, :], top8[:, :, 1], top8[:, :, 0], ALU.subtract))
                    dve.sem_inc(tdiff_ready, 1)
                    for t in range(HT):
                        ins = nc.vector.max_index(idx8[:, t, :], top8[:, t, :], logit[:, t, :])
                    link(ins)
                    link(nc.vector.tensor_copy(idxf[:, :, :], idx8[:, :, :]))
                    for k in range(2):
                        ins = nc.vector.tensor_tensor(pick[:, k, :, :],
                                                      iota8[:, :].unsqueeze(1).broadcast_to([P, HT, EXPERTS]),
                                                      idxf[:, :, k].unsqueeze(2).broadcast_to([P, HT, EXPERTS]),
                                                      ALU.is_equal)
                    link(ins)
                    dve.wait_ge(texp_ready, hi + 1)
                    link(nc.vector.tensor_scalar(tone[:, :], texp[:, :], 1.0, None, ALU.add))
                    link(nc.vector.reciprocal(w_top[:, 0, :], tone[:, :]))
                    link(nc.vector.tensor_tensor(w_top[:, 1, :], w_top[:, 0, :], texp[:, :], ALU.mult))
                    for k in range(2):
                        ins = nc.vector.tensor_tensor(pick[:, k, :, :], pick[:, k, :, :],
                                                      w_top[:, k, :].unsqueeze(2).broadcast_to([P, HT, EXPERTS]),
                                                      ALU.mult)
                    link(ins)
                    link(nc.vector.tensor_tensor(ew[:, tl, :], pick[:, 0, :, :], pick[:, 1, :, :], ALU.add))
                    dve.sem_inc(ew_ready, 1)
                    link(nc.vector.tensor_copy(ewT[:, :], job.take(dve)[0:EXPERTS, :]))
                    dve.sem_inc(ewT_ready, 1)
                    dve.sem_inc(free_d, 1)
                    bank = job.take(dve)
                    freed(nc.vector.tensor_tensor(acc[:, rows, :], bank[:, :].rearrange("p (t d) -> p t d", d=D),
                                                  x2[:, :, :], ALU.add))
                    done()

            def divide(b):
                dve.wait_ge(sg_exp, b + 1)
                link(nc.vector.tensor_scalar(sg_e[:, :, :], sg_e[:, :, :], 1.0, None, ALU.add))
                link(nc.vector.reciprocal(sg_e[:, :, :], sg_e[:, :, :]))
                dve.sem_inc(sg_ready, 1)

            for counter, credit in ((free_d, RING), (free_a, 1), (x_used, 1), (parts_out, 16), (e_used, 2), (o_out, 1),
                                    (unit_done, 2), (acc_ready, 2), (fin_done, 2), (stored, 16)):
                dve.sem_inc(counter, credit)
            dve.wait_ge(ld_w, 16 * N_LOADS)
            dve.wait_ge(pool_const, 2)
            job = Taker(ring, full_d, 0)
            freed(nc.vector.tensor_copy(wT[:, 0:3, :].rearrange("p a n -> p (a n)"), job.take(dve)[:, 0:3 * P]))
            bank = job.take(dve)
            nc.vector.tensor_copy(wT[:, 3:5, :].rearrange("p a n -> p (a n)"), bank[:, 0:2 * P])
            freed(nc.vector.tensor_copy(bv_all[:, :], bank[:, 2 * P:3 * P]))
            freed(nc.vector.tensor_copy(cols[:, :], job.take(dve)[:, 0:39]))
            done()
            dve.sem_inc(setup_done, 1)
            pre(0, SETUP_JOBS)
            end_chain()
            job = Taker(ring, full_d, SETUP_JOBS + PRE_JOBS)
            maxima(job, 0, 32)
            split_maxima()
            take_maxima(job, None)
            end_chain()
            pre(1, SETUP_JOBS + PRE_JOBS + MAX_JOBS)
            link(nc.vector.memset(state[:, :, :], 0.0))
            end_chain()
            with dve.Fori(0, PAIRS // BUFS) as it:
                for r in range(BUFS):
                    u = it * BUFS + r
                    unit(u, u, Taker(ring, full_d, FIRST_AT + u * UNIT_JOBS))
            with dve.Fori(1, B) as b:
                route(b - 1, base_d(b))
                end_chain()
                pre(b + 1, base_d(b) + ROUTE_JOBS)
                dve.wait_ge(fin_done, b + 1)
                link(nc.vector.memset(state[:, :, :], 0.0))
                end_chain()
                with dve.Fori(0, PAIRS // BUFS) as it:
                    for r in range(BUFS):
                        u = it * BUFS + r
                        unit(b * PAIRS + u, u, Taker(ring, full_d, base_d(b) + ROUTE_JOBS + PRE_JOBS
                                                     + u * (UNIT_JOBS + EXPERT_D)), ((b - 1) & 1) * TILES)
                divide(b - 1)
                end_chain()
            route(B - 1, TAIL_AT)
            end_chain()
            with dve.Fori(0, EXPERTS) as e:
                job = Taker(ring, full_d, TAIL_AT + ROUTE_JOBS + e * EXPERT_D)
                job.skip(EXPERT_A)
                for q in range(EXPERT_D):
                    bank = job.take(dve)
                    for t in range(2):
                        tile = 2 * q + t
                        at = acc[:, ((B - 1) & 1) * TILES + tile, :]
                        ins = nc.vector.scalar_tensor_tensor(at, bank[:, t * D:(t + 1) * D],
                                                             ew[:, tile, bass.ds(e, 1)], at, ALU.mult, ALU.add)
                    freed(ins)
                done()
                dve.sem_inc(acc_ready, 1)
                end_chain()
            divide(B - 1)

        @block.tensor
        def _(pe):
            def mm(dst, lhsT, rhs, first=True, last=True, **kw):
                return pe.matmul(dst, lhsT, rhs, start=first, stop=last, **kw)

            def full(ins, who=0):
                ins.then_inc((full_d, full_a)[who], 1)

            def ring_at(at_d, at_a=0):
                return Ring(ring, free_d, free_a, at_d, at_a)

            pe.wait_ge(ld_w, 16 * N_LOADS)
            pe.wait_ge(pool_const, 2)
            job = ring_at(0)
            bank = job.start(pe)
            for i in range(3):
                ins = pe.transpose(bank[:, i * P:(i + 1) * P], wnat[:, i, :], ident[:, :])
            full(ins)
            bank = job.start(pe)
            for i in range(2):
                pe.transpose(bank[:, i * P:(i + 1) * P], wnat[:, 3 + i, :], ident[:, :])
            full(mm(bank[:, 2 * P:3 * P], ones_row[:, :], bv_row[:, :]))
            bank = job.start(pe)
            pe.transpose(bank[:, 0:32], b1_rows[:, :], ident[0:32, 0:32])
            full(pe.transpose(bank[:, 32:39], vec_rows[:, :], ident[0:7, 0:7]))
            pe.wait_ge(setup_done, 1)

            def pre(pb, at):
                job = ring_at(at)
                pe.wait_ge(xh_ready, pb + 1)
                for t0, tiles in ((0, 4), (4, 2), (6, 2)):
                    bank = job.start(pe)
                    for t in range(tiles):
                        ins = pe.transpose(bank[:, t * P:(t + 1) * P], xh[:, t0 + t, :], ident[:, :])
                    full(ins)
                pe.wait_ge(hT_ready, pb + 1)
                for w in range(2):
                    for n in range(2):
                        full(mm(job.start(pe)[:, :], wqkv[:, w * D:(w + 1) * D], hT[:, n * HALF:(n + 1) * HALF]))
                for n in range(2):
                    bank = job.start(pe)
                    for t in range(HT):
                        tile = n * HT + t
                        ins = mm(bank[:, t * P:(t + 1) * P], hT[:, tile * P:(tile + 1) * P], wqkv[:, 2 * D:3 * D])
                    full(ins)

            def maxima(job, r, m0, m1):
                for m in range(m0, m1):
                    t, kk, hd = m // 4, (m // 2) % 2, m % 2
                    rows = slice(64 * hd, 64 * hd + QK_ROWS)
                    full(mm(job.start(pe)[:, :], qs[r][rows, t * P:(t + 1) * P], ks[r][rows, kk * HALF:(kk + 1) * HALF]))

            def turn_maxima(job, pi):
                bank = job.start(pe)
                pe.wait_ge(mparts_ready, pi + 1)
                full(pe.transpose(bank[:, 0:P], mparts[:, :], ident[:, :]))

            def unit(ui, r, job, lap, ei=None, w_laps=None):
                expert = ei is not None
                par = r % 2
                nxt = (r + 1) % BUFS

                def scores(s):
                    for half in range(2):
                        if s:
                            pe.wait_ge(exp_done, ui * 2 * TILES + 2 * (s - 1) + half + 1)
                        for hd in range(2):
                            rows = slice(64 * hd, 64 * hd + SC_ROWS)
                            ins = mm(score[:, 2 * half + hd, :], ks[r][rows, s * P:(s + 1) * P],
                                     qs[r][rows, half * HALF:(half + 1) * HALF])
                        ins.then_inc(score_full, 1)

                def weigh(s):
                    pe.wait_ge(exp_done, ui * 2 * TILES + 2 * s + 2)
                    if s == 0:
                        pe.wait_ge(o_out, ui + 1)
                        pe.wait_ge(vbuf_ready, ui + 1)
                    for hd in range(2):
                        for half in range(2):
                            j = 2 * hd + half
                            ins = mm(o_ps[32 * j:32 * j + 32, :], vbuf[par][:, s, hd, :],
                                     ebuf[:, s % 2, 2 * half + hd, :], s == 0, s == TILES - 1)
                    ins.then_inc(e_used, 1)

                pe.wait_ge(mrows_loaded, 32 * (ui + 1))
                scores(0)
                pe.wait_ge(pair_loaded[nxt], lap * 64 + 64)
                for s in range(TILES):
                    if s + 1 < TILES:
                        scores(s + 1)
                    maxima(job, nxt, *MAX_STEPS[s][0])
                    if s == 6:
                        turn_maxima(job, ui + 1)
                    if s:
                        weigh(s)
                    maxima(job, nxt, *MAX_STEPS[s][1])
                    if not s:
                        weigh(s)
                    if expert and s < FC:
                        if s == 0:
                            pe.wait_ge(w_loaded[par], w_laps * 32 + 32)
                        for tb in range(2):
                            full(mm(job.start(pe, 1)[:, :], w1_buf[par][:, s * P:(s + 1) * P],
                                    h2T[:, tb * HALF:(tb + 1) * HALF]), 1)
                    if expert and s >= FC:
                        if s == FC:
                            pe.wait_ge(free_a, (ei + 1) * EXPERT_A + 1)
                        bank = job.start(pe)
                        for t in range(2):
                            tile = 2 * (s - FC) + t
                            for c in range(FC):
                                ins = mm(bank[:, t * D:(t + 1) * D],
                                         hid[:, tile // HT, c, (tile % HT) * P:(tile % HT + 1) * P],
                                         w2_buf[par][:, c, :], c == 0, c == FC - 1)
                        full(ins)
                    if s == 0:
                        bank = job.start(pe)
                        pe.wait_ge(xs_ready, ui + 1)
                        pe.transpose(bank[:, 0:P], xs[:, 0, :], ident[:, :])
                        full(pe.transpose(bank[:, P:2 * P], xs[:, 1, :], ident[:, :]))
                    if s == 1:
                        bank = job.start(pe)
                        pe.wait_ge(xT_ready, ui + 1)
                        full(mm(bank[:, 0:3 * D], xnT[:, :], wT[:, 0:3, :].rearrange("p a n -> p (a n)")))
                        bank = job.start(pe)
                        mm(bank[:, 0:D], wT[:, 4, :], xT[:, :])
                        mm(bank[:, D:2 * D], xT[:, :], wT[:, 4, :])
                        full(mm(bank[:, 2 * D:3 * D], seg_mean[:, :, :].rearrange("p a n -> p (a n)"), xs[:, 0, :]))
                    if s == 2:
                        bank = job.start(pe)
                        pe.wait_ge(uT_ready, ui + 1)
                        full(mm(bank[:, 0:NSEG], u_both[:, 0, :], mT[:, :]))
                    if s == 3:
                        bank = job.start(pe)
                        pe.wait_ge(gates_ready, ui + 1)
                        full(pe.transpose(bank[:, 0:P], gates[:, :, :].rearrange("p j n -> p (j n)"), ident[:, :]))
                        pe.wait_ge(pv_ready, ui + 1)
                    if s in (3, 4):
                        for j in ((0,), (1, 2, 3))[s - 3]:
                            bank = job.start(pe)[:, 0:STC]
                            strip = slice(32 * j, 32 * j + 32)
                            mm(bank, tri[:, :], pv[:, 4 * j:4 * j + 4, :].rearrange("p h x -> p (h x)"), True, False)
                            full(mm(bank, last_seg[strip, :], state[strip, :, :].rearrange("p h x -> p (h x)"),
                                    False, True))
                    if s == 5:
                        bank = job.start(pe)
                        for j in range(4):
                            ins = mm(bank[32 * j:32 * j + 32, 0:STC], ends_t[:, :],
                                     pv[:, 4 * j:4 * j + 4, :].rearrange("p h x -> p (h x)"))
                        full(ins)
                    if s == 6:
                        pe.wait_ge(gT_ready, ui + 1)
                        pe.wait_ge(state_ready, ui + 1)
                        for j in range(4):
                            strip = slice(32 * j, 32 * j + 32)
                            full(mm(job.start(pe)[:, 0:4 * DK * DK], gT[strip, :], state[strip, :, 0:DK * DK]))
                        bank = job.start(pe)
                        pe.wait_ge(lin_ready, ui + 1)
                        full(pe.transpose(bank[:, 0:P], lin[:, :], ident[:, :]))
                    if s == 7:
                        bank = job.start(pe)
                        pe.wait_ge(linT_ready, ui + 1)
                        full(mm(bank[:, 0:D], linT[:, :], wT[:, 3, :]))
                        pe.wait_ge(o_out, ui + 2)
                        for n in range(2):
                            bank = job.start(pe)
                            for i in range(2):
                                ins = pe.transpose(bank[:, i * P:(i + 1) * P],
                                                   ot[:, (2 * n + i) * P:(2 * n + i + 1) * P], ident[:, :])
                            full(ins)
                assert job.made == [UNIT_JOBS + (EXPERT_D if expert else 0), EXPERT_A if expert else 0], job.made

            def route(b, at):
                job = ring_at(at)
                pe.wait_ge(on_ready, (b + 1) * PAIRS)
                for hb in range(2):
                    hi = b * 2 + hb
                    bank = job.start(pe)
                    for t in range(HT):
                        ins = pe.transpose(bank[:, t * P:(t + 1) * P], on[:, hb * HT + t, :], ident[:, :])
                    full(ins)
                    bank = job.start(pe)
                    pe.wait_ge(onT_ready, hi + 1)
                    for t in range(HT):
                        mm(bank[:, t * P:(t + 1) * P], onT[:, t * P:(t + 1) * P], wo_f[:, :], True, False)
                        ins = mm(bank[:, t * P:(t + 1) * P], ones_row[:, :], bo_row[:, :], False, True)
                    full(ins)
                    bank = job.start(pe)
                    pe.wait_ge(z2_ready, hi + 1)
                    for t in range(HT):
                        ins = pe.transpose(bank[:, t * P:(t + 1) * P], z2[:, t, :], ident[:, :])
                    full(ins)
                    bank = job.start(pe)
                    pe.wait_ge(h2T_ready, hi + 1)
                    for t in range(HT):
                        at = bank[:, t * EXPERTS:(t + 1) * EXPERTS]
                        tile = hb * HT + t
                        mm(at, h2T[:, tile * P:(tile + 1) * P], gate_sb[:, :], True, False)
                        ins = mm(at, ones_row[:, :], gateb_row[:, :], False, True)
                    full(ins)
                    bank = job.start(pe)
                    pe.wait_ge(ew_ready, hi + 1)
                    for t in range(HT):
                        ins = pe.transpose(bank[0:EXPERTS, t * P:(t + 1) * P], ew[:, hb * HT + t, :], ident[:, :])
                    full(ins)
                    bank = job.start(pe)
                    pe.wait_ge(ewT_ready, hi + 1)
                    for t in range(HT):
                        ins = mm(bank[:, t * P:(t + 1) * P], ewT[:, t * P:(t + 1) * P], b2_sb[:, :])
                    full(ins)

            pre(0, SETUP_JOBS)
            pe.wait_ge(pair_loaded[0], 64)
            job = ring_at(SETUP_JOBS + PRE_JOBS)
            maxima(job, 0, 0, 32)
            turn_maxima(job, 0)
            pre(1, SETUP_JOBS + PRE_JOBS + MAX_JOBS)
            with pe.Fori(0, PAIRS // BUFS) as it:
                for r in range(BUFS):
                    u = it * BUFS + r
                    unit(u, r, ring_at(FIRST_AT + u * UNIT_JOBS), it + (1 if r == BUFS - 1 else 0))
            with pe.Fori(1, B) as b:
                route(b - 1, base_d(b))
                pre(b + 1, base_d(b) + ROUTE_JOBS)
                with pe.Fori(0, PAIRS // BUFS) as it:
                    for r in range(BUFS):
                        u = it * BUFS + r
                        ei = (b - 1) * EXPERTS + u
                        unit(b * PAIRS + u, r, ring_at(base_d(b) + ROUTE_JOBS + PRE_JOBS + u * (UNIT_JOBS + EXPERT_D),
                                                       ei * EXPERT_A),
                             b * (PAIRS // BUFS) + it + (1 if r == BUFS - 1 else 0), ei,
                             (b - 1) * (EXPERTS // 2) + it * (BUFS // 2) + r // 2)
            route(B - 1, TAIL_AT)
            with pe.Fori(0, EXPERTS // 2) as e2:
                for par in range(2):
                    e = e2 * 2 + par
                    ei = (B - 1) * EXPERTS + e
                    job = ring_at(TAIL_AT + ROUTE_JOBS + e * EXPERT_D, ei * EXPERT_A)
                    pe.wait_ge(w_loaded[par], ((B - 1) * (EXPERTS // 2) + e2 + 1) * 32)
                    for c in range(FC):
                        for tb in range(2):
                            full(mm(job.start(pe, 1)[:, :], w1_buf[par][:, c * P:(c + 1) * P],
                                    h2T[:, tb * HALF:(tb + 1) * HALF]), 1)
                    pe.wait_ge(free_a, (ei + 1) * EXPERT_A + 1)
                    for q in range(EXPERT_D):
                        bank = job.start(pe)
                        for t in range(2):
                            tile = 2 * q + t
                            for c in range(FC):
                                ins = mm(bank[:, t * D:(t + 1) * D],
                                         hid[:, tile // HT, c, (tile % HT) * P:(tile % HT + 1) * P],
                                         w2_buf[par][:, c, :], c == 0, c == FC - 1)
                        full(ins)


_INS = ['L0_attn_x', 'L0_attn_norm_w', 'L0_attn_Wq', 'L0_attn_Wk', 'L0_attn_Wv', 'L0_attn_Wo', 'L0_attn_Wu',
        'L0_ffn_ln1_g', 'L0_ffn_ln1_b', 'L0_ffn_w_qkv', 'L0_ffn_b_qkv', 'L0_ffn_w_o', 'L0_ffn_b_o',
        'L0_ffn_ln2_g', 'L0_ffn_ln2_b', 'L0_ffn_gate_w', 'L0_ffn_gate_b', 'L0_ffn_W1', 'L0_ffn_b1',
        'L0_ffn_W2', 'L0_ffn_b2']
_OUTS = [((B, T, D), 'float32')]


def kernel(**inputs):
    import numpy as _np
    import concourse.bacc as _bacc
    from concourse import mybir as _mybir
    from concourse.bass_utils import run_bass_kernel_spmd as _run

    nc = _bacc.Bacc("TRN2", target_bir_lowering=False, num_devices=1)
    arrays, args = {}, []
    for name in _INS:
        a = _np.ascontiguousarray(inputs[name])
        arrays[f"in_{name}_dram"] = a
        args.append(nc.dram_tensor(f"in_{name}_dram", a.shape, _mybir.dt.from_np(a.dtype), kind="ExternalInput").ap())
    for i, (shape, dtype) in enumerate(_OUTS):
        dt = _mybir.dt.from_np(_np.dtype(dtype))
        args.append(nc.dram_tensor(f"out_{i}_dram", shape, dt, kind="ExternalOutput").ap())
    program(nc, *args)
    r = _run(nc, [arrays], core_ids=[0])
    return r.results[0]["out_0_dram"]
```

```python
import concourse.bass as bass
from concourse import mybir
from contextlib import ExitStack

FP32 = mybir.dt.float32
BF16 = mybir.dt.bfloat16
I32 = mybir.dt.int32
U32 = mybir.dt.uint32
ALU = mybir.AluOpType
ACT = mybir.ActivationFunctionType
X_AXIS = mybir.AxisListType.X

B, T, D = 4, 1024, 128
P = 128
TILES = T // P
H, DK = 16, 8
SEG = 32
NSEG = T // SEG
TSEG = P // SEG
EXPERTS, DFF = 8, 512
FC = DFF // P
HALF = T // 2
HT = TILES // 2
PVW = H * DK * DK
ZW = H * DK
EPS_LN, EPS_RMS = 1e-5, 1e-6
ATT_SCALE = float(DK) ** -0.5
GATE_SCALE = float(D) ** -0.5
MASKED = -1e30
SCORE_BANKS = 3
RING = 4
RSQRT_MAGIC = 0x5F3759DF

Q_PARTS = (0, 0, 0, 1, 1, 2)
K_PARTS = (0, 1, 2, 0, 1, 0)
QK_ROWS = DK * len(Q_PARTS)
SC_ROWS = QK_ROWS + 3
PAIRS = H // 2
BUFS = 4
HW = DK * DK + DK
STC = H * HW // 4

SETUP_JOBS = 4
AHEAD_JOBS = 8
MAX_JOBS = 4 * TILES + 1
ROUTE_JOBS = 12
UNIT_D, UNIT_A = 49, 3
EXPERT_D, EXPERT_A = 4, 8
LOOP_JOBS = ROUTE_JOBS + PAIRS * (UNIT_D + EXPERT_D)
FIRST_AT = SETUP_JOBS + AHEAD_JOBS + MAX_JOBS
LOOP_AT = FIRST_AT + PAIRS * UNIT_D
TAIL_AT = LOOP_AT + (B - 1) * LOOP_JOBS


MAXIMUM, TURN, HIDDEN0, HIDDEN1, EXPERT, SUMS0, SUMS1, AHEAD = range(8)
SCORES0, SCORES1, WEIGH, SPLIT, WEIGHTS, SUMMED, AVERAGED = range(10, 17)
NORMS = tuple(range(17, 25))
BRANCH = 30
NORMED, PROJECTED, MEANS, SEGMENTS, GATES = range(30, 35)
PREFIX = (35, 36, 37, 38)
STATES = 39
RETRIEVE = (40, 41, 42, 43)
DIVIDED, OUTPUT = 44, 45
MAXIMA = 4 * TILES
M = MAXIMUM
STEPS = (
    (SCORES0, M, M, HIDDEN0, M, SCORES1, WEIGH, NORMED, HIDDEN1, M, M, M),
    (SCORES0, M, PROJECTED, WEIGH, M, SCORES1, M, HIDDEN0, M, MEANS, HIDDEN1, M, M),
    (SCORES0, M, WEIGH, SEGMENTS, SCORES1, M, M, HIDDEN0, M, M, HIDDEN1, M),
    (SCORES0, M, WEIGH, WEIGHTS, SCORES1, M, HIDDEN0, M, M, GATES, HIDDEN1, M, M),
    (SCORES0, PREFIX[0], M, WEIGH, SCORES1, M, PREFIX[1], EXPERT, M, PREFIX[2], M),
    (SCORES0, M, PREFIX[3], WEIGH, M, SCORES1, M, M, SPLIT, EXPERT, STATES),
    (SCORES0, WEIGH, TURN, SCORES1, RETRIEVE[0], RETRIEVE[1], EXPERT, RETRIEVE[2], RETRIEVE[3], AVERAGED),
    (WEIGH, SUMMED, EXPERT, DIVIDED, SUMS0, SUMS1, OUTPUT),
)


def steps(r, expert):
    for s, stages in enumerate(STEPS):
        if r and s == 1:
            yield s, AHEAD
        if r == 0 and s == 6:
            yield s, AHEAD
        norms = 0
        for stage in stages:
            if r == 0 and s in (1, 2, 4, 5) and stage == MAXIMUM and norms < 2:
                yield s, NORMS[2 * (s - 1 if s < 3 else s - 2) + norms]
                norms += 1
            if expert or stage not in (HIDDEN0, HIDDEN1, EXPERT):
                yield s, stage


def jobs(stage):
    return 1 if stage < SCORES0 or stage >= BRANCH else 0


class Ring:

    def __init__(self, banks, free_d, free_a, at_d, at_a):
        self.banks, self.free, self.at = banks, (free_d, free_a), (at_d, at_a)
        self.n, self.made, self.users = 0, [0, 0], [(0, i - RING) for i in range(RING)]

    def start(self, pe, who=0):
        bank = self.n % RING
        user, index = self.users[bank]
        pe.wait_ge(self.free[user], self.at[user] + index + 1 + (RING, 1)[user])
        self.users[bank] = (who, self.made[who])
        self.made[who] += 1
        self.n += 1
        return self.banks[bank]


class Taker:

    def __init__(self, banks, full, at):
        self.banks, self.full, self.at, self.n, self.k = banks, full, at, 0, 0

    def skip(self, jobs=1):
        self.n += jobs

    def take(self, engine):
        engine.wait_ge(self.full, self.at + self.k + 1)
        self.k += 1
        self.n += 1
        return self.banks[(self.n - 1) % RING]


def program(nc, x, norm_w, Wq, Wk, Wv, Wo, Wu, ln1_g, ln1_b, w_qkv, b_qkv, w_o, b_o,
            ln2_g, ln2_b, gate_w, gate_b, W1, b1, W2, b2, out):
    with ExitStack() as ctx:
        def sb(name, shape, dt=FP32):
            return ctx.enter_context(nc.sbuf_tensor(name, shape, dt))

        def sem(name):
            return ctx.enter_context(nc.semaphore(name))

        ident = sb("ident", [P, P])
        tri = sb("tri", [P, P])
        seg_mean = sb("seg_mean", [P, TSEG, SEG])
        seg_ends = sb("seg_ends", [P, TILES, NSEG])
        seg_mask = sb("seg_mask", [P, TILES, NSEG])
        last_seg = sb("last_seg", [P, P])
        ones_row = sb("ones_row", [1, P])
        zero_col = sb("zero_col", [P, 1])
        iota8 = sb("iota8", [P, EXPERTS])
        wnat = sb("wnat", [P, 5, P])
        wT = sb("wT", [P, 5, P])
        b1_rows = sb("b1_rows", [EXPERTS * FC, P])
        vec_rows = sb("vec_rows", [7, P])
        cols = sb("cols", [P, 39])
        b1_cols = cols[:, 0:32]
        nw_col, g1_col, c1_col, g2_col, c2_col, bq_col, bk_col = (cols[:, 32 + i:33 + i] for i in range(7))
        wqkv = sb("wqkv", [P, 3 * D])
        bv_row = sb("bv_row", [1, D])
        bv_all = sb("bv_all", [P, D])
        wo_f = sb("wo_f", [P, D])
        bo_row = sb("bo_row", [1, D])
        gate_sb = sb("gate_sb", [P, EXPERTS])
        gateb_row = sb("gateb_row", [1, EXPERTS])
        b2_sb = sb("b2_sb", [EXPERTS, D])
        w1_buf = [sb(f"w1_buf{i}", [P, DFF]) for i in range(2)]
        w2_buf = [sb(f"w2_buf{i}", [P, FC, D]) for i in range(2)]
        xin = sb("xin", [P, HT, D])
        bn6 = sb("bn6", [P, HT, 6])
        mv = sb("mv", [P, HT, 2])
        bn6_2 = sb("bn6_2", [P, TILES, 6])
        mv_2 = sb("mv_2", [P, TILES, 2])
        var_2 = sb("var_2", [P, TILES])
        rs_2 = sb("rs_2", [P, TILES])
        var3 = sb("var3", [P, 3, HT])
        rs3 = sb("rs3", [P, 3, HT])
        r13 = sb("r13", [P, HT])
        rtmp = sb("rtmp", [P, 2 * HT])
        rtmp2 = sb("rtmp2", [P, 2 * HT])
        xh = sb("xh", [P, HT, D])
        hT = sb("hT", [P, HALF])
        qk_f = sb("qk_f", [P, 2, HALF])
        qk_r = sb("qk_r", [P, HALF])
        parts = sb("parts", [P, 2, 3, HALF], BF16)
        xs_all = sb("xs_all", [P, 2 * TILES, D])
        rms_all = sb("rms_all", [P, (B + 1) * TILES])
        v_all = sb("v_all", [P, 2, 2 * PAIRS, HT, 2 * DK])
        s_all = sb("s_all", [P, 2 * TILES, D])
        acc = sb("acc", [P, 2 * TILES, D])
        xs = sb("xs", [P, 2, D])
        xT = sb("xT", [P, P])
        xnT = sb("xnT", [P, P])
        qk_min = sb("qk_min", [P, 2 * D])
        qk_pos = sb("qk_pos", [P, 2 * D])
        qk_exp = sb("qk_exp", [P, 2 * D])
        pqk = sb("pqk", [P, 2 * D])
        v_t = sb("v_t", [P, D])
        pv = sb("pv", [P, H, HW])
        u_both = sb("u_both", [P, 2, D])
        um = sb("um", [P, D])
        mT = sb("mT", [P, NSEG])
        msum = sb("msum", [P, TSEG])
        sc = sb("sc", [P, NSEG + 1])
        mx1 = sb("mx1", [P, 1])
        nb1 = sb("nb1", [P, 1])
        eg = sb("eg", [P, NSEG + 1])
        egsum = sb("egsum", [P, 1])
        egr = sb("egr", [P, 1])
        gates = sb("gates", [P, 4, NSEG])
        gate_cur = sb("gate_cur", [P, 1])
        gT = sb("gT", [P, P])
        ends_t = sb("ends_t", [P, NSEG])
        state = sb("state", [P, 4, HW])
        prod = sb("prod", [P, PVW])
        prodz = sb("prodz", [P, ZW])
        prodr = sb("prodr", [P, PVW])
        num = sb("num", [P, ZW])
        den = sb("den", [P, H])
        rden = sb("rden", [P, H])
        lin = sb("lin", [P, D])
        linT = sb("linT", [P, P])
        hret = sb("hret", [P, D])
        xout = sb("xout", [P, D])
        qs = [sb(f"qs{i}", [P, T], BF16) for i in range(BUFS)]
        ks = [sb(f"ks{i}", [P, T], BF16) for i in range(BUFS)]
        vbuf = [sb(f"vbuf{i}", [P, TILES, 2, 32]) for i in range(2)]
        mx = sb("mx", [P, 2, 2, TILES])
        mneg = sb("mneg", [P, 2, TILES])
        mres = sb("mres", [P, 2, TILES])
        mparts = sb("mparts", [P, P])
        mrow16 = sb("mrow16", [P, 2, 3, TILES], BF16)
        mrows = sb("mrows", [2 * 3 * TILES, P], BF16)
        ebuf = sb("ebuf", [P, 2, 4, HALF])
        ot = sb("ot", [P, HALF])
        osum = sb("osum", [P, HT, 4])
        on = sb("on", [P, TILES, D])
        onT = sb("onT", [P, T])
        x2 = sb("x2", [P, TILES, D])
        z2 = sb("z2", [P, TILES, D])
        h2T = sb("h2T", [P, T])
        logit = sb("logit", [P, TILES, EXPERTS])
        top8 = sb("top8", [P, TILES, 8])
        idx8 = sb("idx8", [P, TILES, 8], U32)
        idxf = sb("idxf", [P, TILES, 8])
        tdiff = sb("tdiff", [P, TILES])
        texp = sb("texp", [P, TILES])
        tone = sb("tone", [P, TILES])
        w_top = sb("w_top", [P, 2, TILES])
        pick = sb("pick", [P, 2, TILES, EXPERTS])
        ew = sb("ew", [P, TILES, EXPERTS])
        ewT = sb("ewT", [EXPERTS, T])
        b1_t = sb("b1_t", [P, FC])
        hid = sb("hid", [P, 2, FC, HALF])
        sg_e = sb("sg_e", [P, TILES, D])
        fin = sb("fin", [P, TILES, D])

        psum = ctx.enter_context(nc.psum_tensor("psum", [P, 8, HALF], FP32))
        score = [psum[:, i, :] for i in range(SCORE_BANKS)]
        o_ps = psum[:, SCORE_BANKS, :]
        first_ring = [psum[:, SCORE_BANKS + 1 + i, :] for i in range(RING)]
        ring = first_ring[FIRST_AT % RING:] + first_ring[:FIRST_AT % RING]

        scratch = nc.dram_tensor("qk_parts", (2, (B + 1) * H, QK_ROWS, T), BF16, kind="Internal").ap()

        ld_w = sem("ld_w")
        pool_const = sem("pool_const")
        pool_step = sem("pool_step")
        dve_step = sem("dve_step")
        setup_done = sem("setup_done")
        full_d = sem("full_d")
        free_d = sem("free_d")
        full_a = sem("full_a")
        free_a = sem("free_a")
        x_loaded = sem("x_loaded")
        x_used = sem("x_used")
        hT_ready = sem("hT_ready")
        xh_ready = sem("xh_ready")
        qkf_ready = sem("qkf_ready")
        parts_step = sem("parts_step")
        parts_ready = [sem(f"parts_ready{i}") for i in range(2)]
        parts_out = [sem(f"parts_out{i}") for i in range(2)]
        v_ready = sem("v_ready")
        pair_loaded = [sem(f"pair_loaded{i}") for i in range(BUFS)]
        vbuf_ready = sem("vbuf_ready")
        mparts_ready = sem("mparts_ready")
        mrows_ready = sem("mrows_ready")
        mrows_loaded = sem("mrows_loaded")
        score_full = sem("score_full")
        exp_done = sem("exp_done")
        e_used = sem("e_used")
        o_out = sem("o_out")
        xs_ready = sem("xs_ready")
        xT_ready = sem("xT_ready")
        qkmin_ready = sem("qkmin_ready")
        qkexp_ready = sem("qkexp_ready")
        pq_ready = sem("pq_ready")
        pv_ready = sem("pv_ready")
        uT_ready = sem("uT_ready")
        nb_ready = sem("nb_ready")
        eg_ready = sem("eg_ready")
        gates_ready = sem("gates_ready")
        gT_ready = sem("gT_ready")
        state_ready = sem("state_ready")
        lin_ready = sem("lin_ready")
        linT_ready = sem("linT_ready")
        on_ready = sem("on_ready")
        onT_ready = sem("onT_ready")
        z2_ready = sem("z2_ready")
        h2T_ready = sem("h2T_ready")
        tdiff_ready = sem("tdiff_ready")
        texp_ready = sem("texp_ready")
        ew_ready = sem("ew_ready")
        ewT_ready = sem("ewT_ready")
        w_loaded = [sem(f"w_loaded{i}") for i in range(2)]
        acc_ready = sem("acc_ready")
        b1_ready = sem("b1_ready")
        sg_exp = sem("sg_exp")
        sg_ready = sem("sg_ready")
        fin_step = sem("fin_step")
        fin_loaded = sem("fin_loaded")
        fin_done = sem("fin_done")
        stored = sem("stored")

        x_halves = x.rearrange("b (h t p) d -> (b h) p t d", p=P, h=2)
        x_dram = x.rearrange("b (t p) d -> b p t d", p=P)
        out_dram = out.rearrange("b (t p) d -> b p t d", p=P)
        w1_dram = W1.rearrange("e d f -> (e d) f")
        w2_dram = W2.rearrange("e (c p) d -> e p c d", p=P)
        N_LOADS = 20

        def row(v):
            return v.rearrange("(a n) -> a n", a=1)

        def base_d(b):
            return LOOP_AT + (b - 1) * LOOP_JOBS

        def base_a(b):
            return PAIRS * UNIT_A + (b - 1) * PAIRS * (UNIT_A + EXPERT_A)

        block = ctx.enter_context(nc.Block())

        @block.sync
        def _(sp):
            PARTS = (Q_PARTS, K_PARTS)
            WRITES = 16 * len(Q_PARTS)

            def write_parts(w, hp, pb, half):
                sp.wait_ge(parts_ready[w], hp + 2)
                for slot, part in enumerate(PARTS[w]):
                    sp.dma_start(scratch[w, bass.ds(pb * H, H), slot * DK:(slot + 1) * DK, bass.ds(half * HALF, HALF)],
                                 parts[:, w, part, :]).then_inc(parts_out[w], 16)

            def load_pair(pi, r):
                for w, buf in enumerate((qs[r], ks[r])):
                    for hd in range(2):
                        sp.dma_start(buf[64 * hd:64 * hd + QK_ROWS, :],
                                     scratch[w, bass.ds(pi * 2 + hd, 1)].rearrange("a r n -> (a r) n"))\
                            .then_inc(pair_loaded[r], 16)

            def load_maxima(pi, r):
                sp.wait_ge(mrows_ready, pi + 1)
                for hd in range(2):
                    sp.dma_start(qs[r][64 * hd + QK_ROWS:64 * hd + SC_ROWS, :],
                                 mrows[3 * TILES * hd:3 * TILES * (hd + 1), :]).then_inc(mrows_loaded, 16)

            def load_expert(ei, e, r):
                sp.wait_ge(acc_ready, ei + 1)
                sp.dma_start(w1_buf[r][:, :], w1_dram[bass.ds(e * D, D), :]).then_inc(w_loaded[r], 16)
                sp.dma_start(w2_buf[r][:, :, :], w2_dram[bass.ds(e, 1)].rearrange("a p c d -> p (a c) d"))\
                    .then_inc(w_loaded[r], 16)

            def load_final(b):
                sp.wait_ge(stored, b * 16 + 16)
                sp.dma_start(fin[:, :, :], x_dram[bass.ds(b, 1)].rearrange("a p t d -> p (a t) d"))\
                    .then_inc(fin_loaded, 16)

            def store(b):
                sp.wait_ge(fin_done, b + 3)
                sp.dma_start(out_dram[bass.ds(b, 1)].rearrange("a p t d -> p (a t) d"), fin[:, :, :])\
                    .then_inc(stored, 16)

            sp.dma_start(xin[:, :, :], x_halves[0]).then_inc(x_loaded, 16)
            for i, w in enumerate((Wq, Wk, Wv, Wo, Wu)):
                sp.dma_start(wnat[:, i, :], w).then_inc(ld_w, 16)
            sp.dma_start(b1_rows[:, :], b1.rearrange("e (c p) -> (e c) p", p=P)).then_inc(ld_w, 16)
            for i, v in enumerate((norm_w, ln1_g, ln1_b, ln2_g, ln2_b, b_qkv[0:D], b_qkv[D:2 * D])):
                sp.dma_start(vec_rows[i:i + 1, :], row(v)).then_inc(ld_w, 16)
            sp.dma_start(wqkv[:, :], w_qkv).then_inc(ld_w, 16)
            sp.dma_start(bv_row[:, :], row(b_qkv[2 * D:3 * D])).then_inc(ld_w, 16)
            sp.dma_start(wo_f[:, :], w_o).then_inc(ld_w, 16)
            sp.dma_start(bo_row[:, :], row(b_o)).then_inc(ld_w, 16)
            sp.dma_start(gate_sb[:, :], gate_w).then_inc(ld_w, 16)
            sp.dma_start(gateb_row[:, :], row(gate_b)).then_inc(ld_w, 16)
            sp.dma_start(b2_sb[:, :], b2).then_inc(ld_w, 16)
            for half in range(2):
                sp.wait_ge(x_used, half + 1)
                sp.dma_start(xin[:, :, :], x_halves[half + 1]).then_inc(x_loaded, 16)
                for w in range(2):
                    write_parts(w, half, 0, half)
            sp.wait_ge(pool_const, 2)
            for w in range(2):
                sp.wait_ge(parts_out[w], 2 * WRITES + 16)
            load_pair(0, 0)
            load_pair(1, 1)
            load_maxima(0, 0)

            def unit(ui, r, b, half, ei=None, e=None):
                hp = b * 2 + 2 + half
                if ei is not None:
                    load_expert(ei + 1, e, (r + 1) % 2)
                if r in (1, 2):
                    write_parts(r - 1, hp, b + 1, half)
                sp.wait_ge(o_out, ui + 1)
                if r == 2:
                    for w in range(2):
                        sp.wait_ge(parts_out[w], (hp + 1) * WRITES + 16)
                load_pair(ui + 2, (r + 2) % BUFS)
                load_maxima(ui + 1, (r + 1) % BUFS)

            with sp.Fori(0, PAIRS // BUFS) as it:
                for r in range(BUFS):
                    unit(it * BUFS + r, r, 0, it)
            load_expert(0, 0, 0)
            with sp.Fori(1, B) as b:
                with sp.Fori(0, PAIRS // BUFS) as it:
                    for r in range(BUFS):
                        u = it * BUFS + r
                        unit(b * PAIRS + u, r, b, it, (b - 1) * EXPERTS + u,
                             u + 1 if r < BUFS - 1 else it * -BUFS + BUFS)
                load_final(b - 1)
                store(b - 1)
            load_expert((B - 1) * EXPERTS + 1, 1, 1)
            with sp.Fori(1, EXPERTS // 2) as e2:
                for r in range(2):
                    load_expert((B - 1) * EXPERTS + e2 * 2 + r, e2 * 2 + r, r)
            load_final(B - 1)
            store(B - 1)
            sp.wait_ge(stored, 16 * (B + 1))
            sp.wait_ge(mrows_loaded, 32 * (B * PAIRS + 1))
            sp.wait_ge(x_loaded, 16 * (2 * B + 3))
            for r in range(BUFS):
                sp.wait_ge(pair_loaded[r], 64 * (B * PAIRS // BUFS + (1 if r < 2 else 0)))

        @block.gpsimd
        def _(pool):
            step = 0

            def link(ins):
                nonlocal step
                step += 1
                ins.then_inc(pool_step, 1)
                pool.wait_ge(pool_step, step)

            pool.memset(ones_row[:, :], 1.0)
            pool.memset(ident[:, :], 0.0)
            pool.memset(tri[:, :], 1.0)
            pool.memset(seg_ends[:, :, :], 1.0)
            pool.memset(seg_mask[:, :, :], 0.0)
            pool.memset(last_seg[:, :], 0.0)
            pool.memset(mT[:, :], 0.0)
            pool.memset(zero_col[:, :], 0.0)
            pool.memset(mparts[:, :], 0.0)
            for i in range(2):
                link(pool.memset(vbuf[i][:, :, :, :], 0.0))
            for i in range(BUFS):
                link(pool.memset(ks[i][32:64, :], 1.0))
                link(pool.memset(ks[i][96:128, :], 1.0))
            for c in range(SEG):
                pool.memset(seg_mean[:, :, c:c + 1], 1.0 / (c + 1))
            link(pool.iota(iota8[:, :], [[1, EXPERTS]], base=0, channel_multiplier=0,
                           allow_small_or_imprecise_dtypes=True))
            for i in range(2):
                pool.memset(vbuf[i][:, :, :, DK:DK + 1], 1.0)
            pool.affine_select(out=ident[:, :], in_=ident[:, :], compare_op=ALU.not_equal, fill=1.0, base=0,
                               pattern=[[-1, P]], channel_multiplier=1)
            pool.affine_select(out=tri[:, :], in_=tri[:, :], compare_op=ALU.is_ge, fill=0.0, base=0,
                               pattern=[[1, P]], channel_multiplier=-1)
            link(pool.affine_select(out=seg_mean[:, :, :], in_=seg_mean[:, :, :], compare_op=ALU.is_ge, fill=0.0,
                                    base=0, pattern=[[SEG, TSEG], [1, SEG]], channel_multiplier=-1))
            pool.affine_select(out=seg_mean[:, :, :], in_=seg_mean[:, :, :], compare_op=ALU.is_ge, fill=0.0,
                               base=0, pattern=[[-SEG, TSEG], [0, SEG]], channel_multiplier=1)
            pool.affine_select(out=seg_ends[:, :, :], in_=seg_ends[:, :, :], compare_op=ALU.is_ge, fill=0.0,
                               base=SEG - 1, pattern=[[-P, TILES], [SEG, NSEG]], channel_multiplier=-1)
            for j in range(4):
                link(pool.affine_select(out=last_seg[:, :], in_=last_seg[:, :], compare_op=ALU.not_equal, fill=1.0,
                                        base=-(NSEG * j + NSEG - 1), pattern=[[0, P]], channel_multiplier=1))
            pool.affine_select(out=seg_mask[:, :, :], in_=seg_mask[:, :, :], compare_op=ALU.is_ge, fill=MASKED,
                               base=-SEG, pattern=[[P, TILES], [-SEG, NSEG]], channel_multiplier=1)\
                .then_inc(pool_const, 2)

            def values(pi, r):
                for half in range(2):
                    ins = pool.tensor_copy(
                        vbuf[r % 2][:, half * HT:(half + 1) * HT, :, 0:DK],
                        v_all[:, half, bass.ds(pi & (2 * PAIRS - 1), 1), :, :]
                        .rearrange("p a t (h d) -> p (a t) h d", d=DK))
                ins.then_inc(vbuf_ready, 1)

            def rounded(dst, src):
                return pool.tensor_tensor(dst, src, zero_col[:, :].broadcast_to([P, HALF]), ALU.add)

            def split(w, hp):
                pool.wait_ge(qkf_ready, 2 * hp + w + 1)
                pool.wait_ge(parts_out[w], hp * 16 * len(Q_PARTS) + 16)
                at = 8 * hp + 4 * w
                rounded(parts[:, w, 0, :], qk_f[:, w, :]).then_inc(parts_step, 1)
                pool.wait_ge(parts_step, at + 1)
                pool.tensor_tensor(qk_r[:, :], qk_f[:, w, :], parts[:, w, 0, :], ALU.subtract).then_inc(parts_step, 1)
                pool.wait_ge(parts_step, at + 2)
                rounded(parts[:, w, 1, :], qk_r[:, :]).then_inc(parts_step, 1)
                pool.wait_ge(parts_step, at + 3)
                pool.tensor_tensor(parts[:, w, 2, :], qk_r[:, :], parts[:, w, 1, :], ALU.subtract)\
                    .then_inc(parts_step, 1)
                pool.wait_ge(parts_step, at + 4)
                pool.sem_inc(parts_ready[w], 1)

            def unit(ui, r, b, half):
                if r in (1, 2):
                    split(r - 1, b * 2 + 2 + half)
                if r == BUFS - 1:
                    pool.wait_ge(v_ready, b * 2 + 3 + half)
                pool.wait_ge(o_out, ui + 1)
                values(ui + 1, r + 1)
                pool.wait_ge(qkexp_ready, ui + 1)
                pool.tensor_tensor(pqk[:, :], qk_exp[:, :], qk_pos[:, :], ALU.add).then_inc(pq_ready, 1)
                pool.wait_ge(pq_ready, ui + 1)
                keys = pqk[:, D:2 * D].rearrange("p (h k) -> p h k", k=DK)
                vals = v_t[:, :].rearrange("p (h v) -> p h v", v=DK)
                pool.tensor_tensor(pv[:, :, 0:DK * DK].rearrange("p h (k v) -> p h k v", k=DK),
                                   keys.unsqueeze(3).broadcast_to([P, H, DK, DK]),
                                   vals.unsqueeze(2).broadcast_to([P, H, DK, DK]), ALU.mult)
                pool.tensor_copy(pv[:, :, DK * DK:HW], keys).then_inc(pv_ready, 1)

            def final(b):
                tl = bass.ds((b & 1) * TILES, TILES)
                pool.wait_ge(sg_ready, b + 1)
                pool.tensor_tensor(sg_e[:, :, :], acc[:, tl, :], sg_e[:, :, :], ALU.mult).then_inc(fin_step, 1)
                pool.wait_ge(fin_step, b * 2 + 1)
                pool.tensor_tensor(sg_e[:, :, :], sg_e[:, :, :], s_all[:, tl, :], ALU.mult).then_inc(fin_step, 1)
                pool.wait_ge(fin_step, b * 2 + 2)
                pool.wait_ge(fin_loaded, b * 16 + 16)
                pool.tensor_tensor(fin[:, :, :], fin[:, :, :], sg_e[:, :, :], ALU.add).then_inc(fin_done, 1)

            for half in range(2):
                for w in range(2):
                    split(w, half)
            pool.wait_ge(v_ready, 2)
            values(0, 0)
            with pool.Fori(0, PAIRS // BUFS) as it:
                for r in range(BUFS):
                    unit(it * BUFS + r, r, 0, it)
            with pool.Fori(1, B) as b:
                with pool.Fori(0, PAIRS // BUFS) as it:
                    for r in range(BUFS):
                        unit(b * PAIRS + it * BUFS + r, r, b, it)
                final(b - 1)
            final(B - 1)

        @block.scalar
        def _(act):
            def exps(ui, s, half):
                act.wait_ge(e_used, ui * TILES + s + 1)
                for hd in range(2):
                    n = 4 * s + 2 * half + hd
                    act.wait_ge(score_full, ui * 4 * TILES + n + 1)
                    act.activation(ebuf[:, s % 2, 2 * half + hd, :], score[n % SCORE_BANKS][:, :], ACT.Exp,
                                   scale=ATT_SCALE).then_inc(exp_done, 1)

            def bias(job, ei, e):
                act.wait_ge(free_a, job.at + 1)
                act.activation(b1_t[:, :], b1_cols[:, bass.ds(e * FC, FC)], ACT.Copy).then_inc(b1_ready, 1)
                act.wait_ge(b1_ready, ei + 1)

            def hidden(job, c, tb):
                bank = job.take(act)
                act.activation(hid[:, tb, c, :], bank[:, :], ACT.Relu, bias=b1_t[:, c:c + 1]).then_inc(free_a, 1)

            def unit(ui, r, b, half, job, e=None):
                expert = e is not None
                exps(ui, 0, 0)
                exps(ui, 0, 1)
                if r == 1:
                    hp = b * 2 + 2 + half
                    act.wait_ge(x_used, hp + 1)
                    act.dma_start(xin[:, :, :], x_halves[bass.ds((hp + 1) & (2 * B - 1), 1)]
                                  .rearrange("a p t d -> p (a t) d")).then_inc(x_loaded, 16)
                if expert:
                    bias(job, (b - 1) * EXPERTS + e, e)
                for s, stage in steps(r, expert):
                    if stage in (SCORES0, SCORES1):
                        exps(ui, s + 1, stage - SCORES0)
                    if stage in (HIDDEN0, HIDDEN1):
                        hidden(job, s, stage - HIDDEN0)
                    elif stage == NORMED:
                        bank = job.take(act)
                        act.activation(xT[:, :], bank[:, 0:P], ACT.Copy)
                        act.activation(xnT[:, :], bank[:, P:2 * P], ACT.Copy, scale=nw_col).then_inc(xT_ready, 1)
                        act.wait_ge(xT_ready, ui + 1)
                        act.sem_inc(free_a, 1)
                    elif stage == GATES:
                        bank = job.take(act)
                        act.activation(gT[:, :], bank[:, 0:P], ACT.Copy).then_inc(gT_ready, 1)
                        act.wait_ge(gT_ready, ui + 1)
                        act.sem_inc(free_a, 1)
                    elif stage == TURN:
                        bank = job.take(act)
                        act.wait_ge(mrows_loaded, 32 * (ui + 1))
                        act.activation(mrows[:, :], bank[0:2 * 3 * TILES, 0:P], ACT.Copy).then_inc(mrows_ready, 1)
                        act.wait_ge(mrows_ready, ui + 2)
                        act.sem_inc(free_a, 1)
                    else:
                        job.skip(jobs(stage))
                    if stage == PROJECTED:
                        act.wait_ge(qkmin_ready, ui + 1)
                        act.activation(qk_exp[:, :], qk_min[:, :], ACT.Exp).then_inc(qkexp_ready, 1)
                    if stage == SUMMED:
                        act.wait_ge(e_used, (ui + 1) * TILES + 2)
                        act.wait_ge(on_ready, ui + 1)
                        act.activation(ot[:, :], o_ps[:, :], ACT.Copy).then_inc(o_out, 1)
                    if stage == SEGMENTS:
                        act.wait_ge(nb_ready, ui + 1)
                        act.activation(eg[:, :], sc[:, :], ACT.Exp, bias=nb1[:, 0:1], scale=GATE_SCALE,
                                       accum_out=egsum[:, 0:1]).then_inc(eg_ready, 1)

            def route(b):
                act.wait_ge(tdiff_ready, b + 1)
                act.activation(texp[:, :], tdiff[:, :], ACT.Exp).then_inc(texp_ready, 1)

            def silu(b):
                act.wait_ge(acc_ready, (b + 1) * EXPERTS + 2)
                act.wait_ge(fin_done, b + 2)
                act.wait_ge(pool_const, 2)
                act.activation(sg_e[:, :, :], acc[:, bass.ds((b & 1) * TILES, TILES), :], ACT.Exp, scale=-1.0)\
                    .then_inc(sg_exp, 1)

            with act.Fori(0, PAIRS // BUFS) as it:
                for r in range(BUFS):
                    u = it * BUFS + r
                    unit(u, r, 0, it, Taker(ring, full_a, u * UNIT_A))
            with act.Fori(1, B) as b:
                route(b - 1)
                with act.Fori(0, PAIRS // BUFS) as it:
                    for r in range(BUFS):
                        u = it * BUFS + r
                        unit(b * PAIRS + u, r, b, it, Taker(ring, full_a, base_a(b) + u * (UNIT_A + EXPERT_A)), u)
                silu(b - 1)
            route(B - 1)
            with act.Fori(0, EXPERTS) as e:
                job = Taker(ring, full_a, base_a(B) + e * EXPERT_A)
                bias(job, (B - 1) * EXPERTS + e, e)
                for c in range(FC):
                    for tb in range(2):
                        hidden(job, c, tb)
            silu(B - 1)

        @block.vector
        def _(dve):
            chain = [0]

            def link(ins):
                chain[0] += 1
                ins.then_inc(dve_step, 1)
                dve.wait_ge(dve_step, chain[0])

            def done():
                link(nc.vector.memset(rtmp2[:, 0:1], 0.0))

            def end_chain():
                done()
                dve.sem_clear(dve_step)
                chain[0] = 0

            def rsqrt_start(dst, src):
                a = rtmp[:, 0:dst.shape[-1]]
                link(nc.vector.tensor_scalar(a.bitcast(I32), src.bitcast(I32), 1, None, ALU.arith_shift_right))
                link(nc.vector.tensor_scalar(dst.bitcast(I32), a.bitcast(I32), -1, RSQRT_MAGIC, ALU.mult, ALU.add))

            def rsqrt_step(dst, src):
                c = rtmp2[:, 0:dst.shape[-1]]
                link(nc.vector.tensor_tensor(c, dst, dst, ALU.mult))
                link(nc.vector.tensor_tensor(c, c, src, ALU.mult))
                link(nc.vector.tensor_scalar(c, c, -0.5, 1.5, ALU.mult, ALU.add))
                link(nc.vector.tensor_tensor(dst, dst, c, ALU.mult))

            def freed(ins):
                ins.then_inc(free_d, 1)

            def norms(n, hp, tile):
                outer, both = rs3[:, 0, :], rs3[:, 1:3, :].rearrange("p a t -> p (a t)")
                outer_var, both_var = var3[:, 0, :], var3[:, 1:3, :].rearrange("p a t -> p (a t)")
                if n == 0:
                    dve.wait_ge(x_loaded, hp * 16 + 16)
                    for t in range(HT):
                        ins = nc.vector.bn_stats(bn6[:, t, :], xin[:, t, :])
                    link(ins)
                    for t in range(HT):
                        ins = nc.vector.bn_aggr(mv[:, t, :], bn6[:, t, :])
                    link(ins)
                    link(nc.vector.tensor_scalar(outer_var, mv[:, :, 1], EPS_LN, None, ALU.add))
                    rsqrt_start(outer, outer_var)
                elif n in (1, 2, 5, 6):
                    for _ in range(2):
                        rsqrt_step(*((outer, outer_var) if n < 3 else (both, both_var)))
                elif n == 3:
                    link(nc.vector.tensor_tensor(outer_var, mv[:, :, 1], outer, ALU.mult))
                    link(nc.vector.tensor_tensor(outer_var, outer_var, outer, ALU.mult))
                    nc.vector.tensor_scalar(var3[:, 1, :], outer_var, EPS_RMS, None, ALU.add)
                    link(nc.vector.tensor_scalar(var3[:, 2, :], outer_var, EPS_LN, None, ALU.add))
                    rsqrt_start(both, both_var)
                elif n == 4:
                    for t in range(HT):
                        ins = nc.vector.tensor_scalar(
                            xs_all[:, bass.ds(tile + t, 1), :].rearrange("p a d -> p (a d)"),
                            xin[:, t, :], mv[:, t, 0:1], rs3[:, 0, t:t + 1], ALU.subtract, ALU.mult)
                    link(ins)
                elif n == 7:
                    nc.vector.tensor_copy(rms_all[:, bass.ds(hp * HT, HT)], rs3[:, 1, :])
                    link(nc.vector.tensor_tensor(r13[:, :], rs3[:, 0, :], rs3[:, 2, :], ALU.mult))
                    for t in range(HT):
                        ins = nc.vector.tensor_scalar(xh[:, t, :], xin[:, t, :], mv[:, t, 0:1], r13[:, t:t + 1],
                                                      ALU.subtract, ALU.mult)
                    link(ins)
                    dve.sem_inc(xh_ready, 1)
                    dve.sem_inc(x_used, 1)

            def project(r, job, hp, half, pair):
                bank = job.take(dve)
                if r == 0:
                    link(nc.vector.tensor_scalar(hT[:, :], bank[:, :], g1_col, c1_col, ALU.mult, ALU.add))
                    dve.sem_inc(free_d, 1)
                    dve.sem_inc(hT_ready, 1)
                elif r < 3:
                    dve.wait_ge(parts_ready[r - 1], hp + 1)
                    link(nc.vector.tensor_scalar(qk_f[:, r - 1, :], bank[:, :], (bq_col, bk_col)[r - 1], None, ALU.add))
                    dve.sem_inc(free_d, 1)
                    dve.sem_inc(qkf_ready, 1)
                else:
                    for t in range(HT):
                        ins = nc.vector.tensor_tensor(
                            v_all[:, bass.ds(half, 1), bass.ds(pair, PAIRS), t, :].rearrange("p h a c -> p (h a) c"),
                            bank[:, t * P:(t + 1) * P].rearrange("p (a c) -> p a c", c=2 * DK),
                            bv_all[:, :].rearrange("p (a c) -> p a c", c=2 * DK), ALU.add)
                    link(ins)
                    dve.sem_inc(free_d, 1)
                    dve.sem_inc(v_ready, 1)

            def maxima(job, m0, m1):
                for m in range(m0, m1):
                    t, kk, hd = m // 4, (m // 2) % 2, m % 2
                    bank = job.take(dve)
                    freed(nc.vector.tensor_reduce(mx[:, kk, hd, t:t + 1], bank[:, :], X_AXIS, ALU.max))

            def split_maxima():
                done()
                link(nc.vector.tensor_tensor(mneg[:, :, :], mx[:, 0], mx[:, 1], ALU.max))
                link(nc.vector.tensor_scalar(mneg[:, :, :], mneg[:, :, :], -1.0, None, ALU.mult))
                link(nc.vector.tensor_copy(mrow16[:, :, 0, :], mneg[:, :, :]))
                link(nc.vector.tensor_tensor(mres[:, :, :], mneg[:, :, :], mrow16[:, :, 0, :], ALU.subtract))
                link(nc.vector.tensor_copy(mrow16[:, :, 1, :], mres[:, :, :]))
                link(nc.vector.tensor_tensor(mrow16[:, :, 2, :], mres[:, :, :], mrow16[:, :, 1, :], ALU.subtract))
                link(nc.vector.tensor_copy(mparts[:, 0:2 * 3 * TILES], mrow16[:, :, :, :].rearrange("p h s t -> p (h s t)")))
                dve.sem_inc(mparts_ready, 1)

            def take_maxima(job):
                bank = job.take(dve)
                link(nc.vector.tensor_copy(mrows[:, :], bank[0:2 * 3 * TILES, 0:P]))
                dve.sem_inc(free_d, 1)
                dve.sem_inc(mrows_ready, 1)

            def unit(ui, u, r, b, half, job, acc_at=None):
                expert = acc_at is not None
                hp = b * 2 + 2 + half
                nxt = (b + 1) & 1
                nc.vector.tensor_copy(xs[:, 0, :], xs_all[:, bass.ds(ui & (2 * TILES - 1), 1), :].rearrange("p a d -> p (a d)"))
                nc.vector.tensor_copy(ends_t[:, :], seg_ends[:, bass.ds(u, 1), :].rearrange("p a n -> p (a n)"))
                link(nc.vector.tensor_scalar(xs[:, 1, :], xs_all[:, bass.ds(ui & (2 * TILES - 1), 1), :].rearrange("p a d -> p (a d)"),
                                             rms_all[:, bass.ds(ui, 1)], None, ALU.mult))
                dve.sem_inc(xs_ready, 1)

                def times_queries(dst, bank, width, j):
                    return nc.vector.tensor_tensor(
                        dst[:, j * 256:(j + 1) * 256].rearrange("p (h k v) -> p h k v", k=DK, v=DK),
                        bank[:, 0:4 * width].rearrange("p (h x) -> p h x", x=width)[:, :, 0:DK * DK]
                        .rearrange("p h (k v) -> p h k v", k=DK),
                        pqk[:, j * 32:(j + 1) * 32].rearrange("p (h k) -> p h k", k=DK)
                        .unsqueeze(3).broadcast_to([P, 4, DK, DK]), ALU.mult)

                def sum_keys(dst, src):
                    return nc.vector.tensor_reduce(dst[:, :].rearrange("p (h v) -> p h v", v=DK),
                                                   src[:, :].rearrange("p (h k v) -> p h v k", k=DK, v=DK),
                                                   X_AXIS, ALU.add)

                def prefix(j):
                    bank = job.take(dve)
                    times_queries(prod, bank, HW, j)
                    freed(nc.vector.tensor_tensor(
                        prodz[:, j * 32:(j + 1) * 32].rearrange("p (h k) -> p h k", k=DK),
                        bank[:, 0:STC].rearrange("p (h x) -> p h x", x=HW)[:, :, DK * DK:HW],
                        pqk[:, j * 32:(j + 1) * 32].rearrange("p (h k) -> p h k", k=DK), ALU.mult))

                def branch(stage):
                    if stage == PROJECTED:
                        bank = job.take(dve)
                        nc.vector.tensor_scalar(qk_min[:, :], bank[:, 0:2 * D], 0.0, None, ALU.min)
                        nc.vector.tensor_scalar(qk_pos[:, :], bank[:, 0:2 * D], 0.0, None, ALU.max)
                        link(nc.vector.tensor_copy(v_t[:, :], bank[:, 2 * D:3 * D]))
                        dve.sem_inc(free_d, 1)
                        dve.sem_inc(qkmin_ready, 1)
                        dve.wait_ge(xT_ready, ui + 1)
                        link(nc.vector.tensor_reduce(msum[:, :], xT[:, :].rearrange("p (n c) -> p n c", c=SEG), X_AXIS,
                                                     ALU.add))
                        link(nc.vector.tensor_scalar(mT[:, bass.ds(u * TSEG, TSEG)], msum[:, :], 1.0 / SEG, None, ALU.mult))
                    if stage == MEANS:
                        bank = job.take(dve)
                        link(nc.vector.tensor_copy(u_both[:, :, :].rearrange("p a n -> p (a n)"), bank[:, 0:2 * D]))
                        dve.sem_inc(uT_ready, 1)
                        link(nc.vector.tensor_tensor(um[:, :], bank[:, 2 * D:3 * D], u_both[:, 1, :], ALU.mult))
                        freed(nc.vector.tensor_reduce(sc[:, NSEG:NSEG + 1], um[:, :], X_AXIS, ALU.add))
                    if stage == SEGMENTS:
                        bank = job.take(dve)
                        link(nc.vector.tensor_tensor(sc[:, 0:NSEG], bank[:, 0:NSEG],
                                                     seg_mask[:, bass.ds(u, 1), :].rearrange("p a n -> p (a n)"), ALU.add))
                        dve.sem_inc(free_d, 1)
                        link(nc.vector.tensor_reduce(mx1[:, :], sc[:, :], X_AXIS, ALU.max))
                        nc.vector.tensor_scalar(nb1[:, :], mx1[:, :], -GATE_SCALE, None, ALU.mult).then_inc(nb_ready, 1)
                    if stage == GATES:
                        job.skip()
                        dve.wait_ge(pq_ready, ui + 1)
                    if stage in PREFIX:
                        prefix(stage - PREFIX[0])
                    if stage == STATES:
                        bank = job.take(dve)
                        freed(nc.vector.tensor_tensor(state[:, :, :].rearrange("p h x -> p (h x)"), bank[:, 0:STC],
                                                      state[:, :, :].rearrange("p h x -> p (h x)"), ALU.add))
                        done()
                        dve.sem_inc(state_ready, 1)
                    if stage in RETRIEVE:
                        freed(times_queries(prodr, job.take(dve), DK * DK, stage - RETRIEVE[0]))
                    if stage == DIVIDED:
                        done()
                        bank = job.take(dve)
                        link(nc.vector.tensor_copy(linT[:, :], bank[:, 0:P]))
                        dve.sem_inc(linT_ready, 1)
                        dve.sem_inc(free_d, 1)
                    if stage == OUTPUT:
                        link(sum_keys(hret, prodr))
                        bank = job.take(dve)
                        link(nc.vector.tensor_tensor(xout[:, :], bank[:, 0:D], xs[:, 0, :], ALU.add))
                        freed(nc.vector.scalar_tensor_tensor(
                            s_all[:, bass.ds(ui & (2 * TILES - 1), 1), :].rearrange("p a d -> p (a d)"), xout[:, :],
                            gate_cur[:, 0:1], hret[:, :], ALU.mult, ALU.add))

                def take_sums(n):
                    bank = job.take(dve)
                    o4 = bank[:, 0:2 * P].rearrange("p (i j r) -> p i j r", i=2, r=32)
                    recip = osum[:, 2 * n:2 * n + 2, :]
                    link(nc.vector.reciprocal(recip, o4[:, :, :, DK]))
                    for i in range(2):
                        dst = on[:, 2 * n + i:TILES:HT, bass.ds(u * 2 * DK, 2 * DK)]
                        ins = nc.vector.tensor_tensor(
                            dst.rearrange("p q (h d) -> p h q d", d=DK),
                            o4[:, i, :, 0:DK].rearrange("p (h q) d -> p h q d", q=2),
                            recip[:, i, :].rearrange("p (h q) -> p h q", q=2).unsqueeze(3)
                            .broadcast_to([P, 2, 2, DK]), ALU.mult)
                    freed(ins)

                m = 0
                for s, stage in steps(r, expert):
                    if stage == MAXIMUM:
                        maxima(job, m, m + 1)
                        m += 1
                    elif stage == SPLIT:
                        split_maxima()
                    elif stage == AVERAGED:
                        sum_keys(num, prod)
                        link(nc.vector.tensor_reduce(den[:, :], prodz[:, :].rearrange("p (h k) -> p h k", k=DK),
                                                     X_AXIS, ALU.add))
                        link(nc.vector.tensor_scalar(den[:, :], den[:, :], EPS_RMS, None, ALU.add))
                        link(nc.vector.reciprocal(rden[:, :], den[:, :]))
                        nc.vector.tensor_tensor(lin[:, :].rearrange("p (h v) -> p h v", v=DK),
                                                num[:, :].rearrange("p (h v) -> p h v", v=DK),
                                                rden[:, :].unsqueeze(2).broadcast_to([P, H, DK]), ALU.mult)\
                            .then_inc(lin_ready, 1)
                    elif stage in NORMS:
                        norms(stage - NORMS[0], hp, nxt * TILES + half * HT)
                    elif stage == AHEAD:
                        project(r, job, hp, half, nxt * PAIRS)
                    elif stage == WEIGHTS:
                        dve.wait_ge(eg_ready, ui + 1)
                        link(nc.vector.reciprocal(egr[:, :], egsum[:, :]))
                        nc.vector.tensor_scalar(gates[:, :, :], eg[:, 0:NSEG].unsqueeze(1).broadcast_to([P, 4, NSEG]),
                                                egr[:, 0:1], None, ALU.mult)
                        link(nc.vector.tensor_scalar(gate_cur[:, :], eg[:, NSEG:NSEG + 1], egr[:, 0:1], None, ALU.mult))
                        dve.sem_inc(gates_ready, 1)
                    elif stage in (HIDDEN0, HIDDEN1, NORMED, TURN):
                        job.skip()
                    elif stage == EXPERT:
                        bank = job.take(dve)
                        for t in range(2):
                            tile = 2 * (s - FC) + t
                            at = acc[:, bass.ds(acc_at + tile, 1), :].rearrange("p a d -> p (a d)")
                            ins = nc.vector.scalar_tensor_tensor(at, bank[:, t * D:(t + 1) * D],
                                                                 ew[:, tile, bass.ds(u, 1)], at, ALU.mult, ALU.add)
                        freed(ins)
                    elif stage in (SUMS0, SUMS1):
                        take_sums(stage - SUMS0)
                    elif stage >= BRANCH:
                        branch(stage)
                done()
                dve.sem_inc(on_ready, 1)
                if expert:
                    dve.sem_inc(acc_ready, 1)
                end_chain()

            def route(b, at):
                job = Taker(ring, full_d, at)

                def per_half(op, ready):
                    for hb in range(2):
                        link(op(job.take(dve), hb, slice(hb * HT, (hb + 1) * HT), slice(hb * HALF, (hb + 1) * HALF)))
                        dve.sem_inc(free_d, 1)
                        if ready is not None:
                            dve.sem_inc(ready, 1)

                def rows(hb):
                    return bass.ds((b & 1) * TILES + hb * HT, HT)

                dve.wait_ge(fin_done, b + 1)
                per_half(lambda bank, hb, tl, cl: nc.vector.tensor_copy(onT[:, cl], bank[:, :]), onT_ready)
                per_half(lambda bank, hb, tl, cl: nc.vector.tensor_tensor(
                    x2[:, tl, :], bank[:, :].rearrange("p (t d) -> p t d", d=D), xs_all[:, rows(hb), :], ALU.add), None)
                for t in range(TILES):
                    ins = nc.vector.bn_stats(bn6_2[:, t, :], x2[:, t, :])
                link(ins)
                for t in range(TILES):
                    ins = nc.vector.bn_aggr(mv_2[:, t, :], bn6_2[:, t, :])
                link(ins)
                link(nc.vector.tensor_scalar(var_2[:, :], mv_2[:, :, 1], EPS_LN, None, ALU.add))
                rsqrt_start(rs_2[:, :], var_2[:, :])
                for _ in range(4):
                    rsqrt_step(rs_2[:, :], var_2[:, :])
                for hb in range(2):
                    for t in range(hb * HT, (hb + 1) * HT):
                        ins = nc.vector.tensor_scalar(z2[:, t, :], x2[:, t, :], mv_2[:, t, 0:1], rs_2[:, t:t + 1],
                                                      ALU.subtract, ALU.mult)
                    link(ins)
                    dve.sem_inc(z2_ready, 1)
                per_half(lambda bank, hb, tl, cl: nc.vector.tensor_scalar(h2T[:, cl], bank[:, :], g2_col, c2_col,
                                                                          ALU.mult, ALU.add), h2T_ready)
                per_half(lambda bank, hb, tl, cl: nc.vector.tensor_copy(
                    logit[:, tl, :].rearrange("p t e -> p (t e)"), bank[:, 0:HT * EXPERTS]), None)
                for t in range(TILES):
                    ins = nc.vector.max(top8[:, t, :], logit[:, t, :])
                link(ins)
                link(nc.vector.tensor_tensor(tdiff[:, :], top8[:, :, 1], top8[:, :, 0], ALU.subtract))
                dve.sem_inc(tdiff_ready, 1)
                for t in range(TILES):
                    ins = nc.vector.max_index(idx8[:, t, :], top8[:, t, :], logit[:, t, :])
                link(ins)
                link(nc.vector.tensor_copy(idxf[:, :, :], idx8[:, :, :]))
                for k in range(2):
                    ins = nc.vector.tensor_tensor(pick[:, k, :, :],
                                                  iota8[:, :].unsqueeze(1).broadcast_to([P, TILES, EXPERTS]),
                                                  idxf[:, :, k].unsqueeze(2).broadcast_to([P, TILES, EXPERTS]),
                                                  ALU.is_equal)
                link(ins)
                dve.wait_ge(texp_ready, b + 1)
                link(nc.vector.tensor_scalar(tone[:, :], texp[:, :], 1.0, None, ALU.add))
                link(nc.vector.reciprocal(w_top[:, 0, :], tone[:, :]))
                link(nc.vector.tensor_tensor(w_top[:, 1, :], w_top[:, 0, :], texp[:, :], ALU.mult))
                for k in range(2):
                    ins = nc.vector.tensor_tensor(pick[:, k, :, :], pick[:, k, :, :],
                                                  w_top[:, k, :].unsqueeze(2).broadcast_to([P, TILES, EXPERTS]),
                                                  ALU.mult)
                link(ins)
                link(nc.vector.tensor_tensor(ew[:, :, :], pick[:, 0, :, :], pick[:, 1, :, :], ALU.add))
                dve.sem_inc(ew_ready, 1)
                per_half(lambda bank, hb, tl, cl: nc.vector.tensor_copy(ewT[:, cl], bank[0:EXPERTS, :]), ewT_ready)
                per_half(lambda bank, hb, tl, cl: nc.vector.tensor_tensor(
                    acc[:, rows(hb), :], bank[:, :].rearrange("p (t d) -> p t d", d=D), x2[:, tl, :], ALU.add), None)

            def divide(b):
                dve.wait_ge(sg_exp, b + 1)
                link(nc.vector.tensor_scalar(sg_e[:, :, :], sg_e[:, :, :], 1.0, None, ALU.add))
                link(nc.vector.reciprocal(sg_e[:, :, :], sg_e[:, :, :]))
                dve.sem_inc(sg_ready, 1)

            for counter, credit in ((free_d, RING), (free_a, 1), (parts_out[0], 16), (parts_out[1], 16),
                                    (exp_done, 2), (parts_ready[0], 1), (parts_ready[1], 1), (e_used, 2), (o_out, 1),
                                    (on_ready, 1), (acc_ready, 2), (fin_done, 2), (stored, 16)):
                dve.sem_inc(counter, credit)
            dve.wait_ge(ld_w, 16 * N_LOADS)
            dve.wait_ge(pool_const, 2)
            job = Taker(first_ring, full_d, 0)
            freed(nc.vector.tensor_copy(wT[:, 0:3, :].rearrange("p a n -> p (a n)"), job.take(dve)[:, 0:3 * P]))
            freed(nc.vector.tensor_copy(wT[:, 3:5, :].rearrange("p a n -> p (a n)"), job.take(dve)[:, 0:2 * P]))
            freed(nc.vector.tensor_copy(bv_all[:, :], job.take(dve)[:, 0:P]))
            freed(nc.vector.tensor_copy(cols[:, :], job.take(dve)[:, 0:39]))
            done()
            dve.sem_inc(setup_done, 1)
            for half in range(2):
                for n in range(len(NORMS)):
                    norms(n, half, half * HT)
                for r in range(BUFS):
                    project(r, job, half, half, 0)
            end_chain()
            maxima(job, 0, MAXIMA)
            split_maxima()
            take_maxima(job)
            end_chain()
            link(nc.vector.memset(state[:, :, :], 0.0))
            end_chain()
            with dve.Fori(0, PAIRS // BUFS) as it:
                for r in range(BUFS):
                    u = it * BUFS + r
                    unit(u, u, r, 0, it, Taker(ring, full_d, FIRST_AT + u * UNIT_D))
            with dve.Fori(1, B) as b:
                route(b - 1, base_d(b))
                end_chain()
                dve.wait_ge(fin_done, b + 1)
                link(nc.vector.memset(state[:, :, :], 0.0))
                end_chain()
                with dve.Fori(0, PAIRS // BUFS) as it:
                    for r in range(BUFS):
                        u = it * BUFS + r
                        unit(b * PAIRS + u, u, r, b, it, Taker(ring, full_d, base_d(b) + ROUTE_JOBS
                                                     + u * (UNIT_D + EXPERT_D)), ((b - 1) & 1) * TILES)
                divide(b - 1)
                end_chain()
            route(B - 1, TAIL_AT)
            end_chain()
            with dve.Fori(0, EXPERTS) as e:
                job = Taker(ring, full_d, TAIL_AT + ROUTE_JOBS + e * EXPERT_D)
                job.skip(EXPERT_A)
                for q in range(EXPERT_D):
                    bank = job.take(dve)
                    for t in range(2):
                        tile = 2 * q + t
                        at = acc[:, ((B - 1) & 1) * TILES + tile, :]
                        ins = nc.vector.scalar_tensor_tensor(at, bank[:, t * D:(t + 1) * D],
                                                             ew[:, tile, bass.ds(e, 1)], at, ALU.mult, ALU.add)
                    freed(ins)
                done()
                dve.sem_inc(acc_ready, 1)
                end_chain()
            divide(B - 1)

        @block.tensor
        def _(pe):
            def mm(dst, lhsT, rhs, first=True, last=True, **kw):
                return pe.matmul(dst, lhsT, rhs, start=first, stop=last, **kw)

            def full(ins, who=0):
                ins.then_inc((full_d, full_a)[who], 1)

            def ring_at(at_d, at_a=0):
                return Ring(ring, free_d, free_a, at_d, at_a)

            pe.wait_ge(ld_w, 16 * N_LOADS)
            pe.wait_ge(pool_const, 2)
            job = Ring(first_ring, free_d, free_a, 0, 0)
            bank = job.start(pe)
            for i in range(3):
                ins = pe.transpose(bank[:, i * P:(i + 1) * P], wnat[:, i, :], ident[:, :])
            full(ins)
            bank = job.start(pe)
            for i in range(2):
                ins = pe.transpose(bank[:, i * P:(i + 1) * P], wnat[:, 3 + i, :], ident[:, :])
            full(ins)
            full(mm(job.start(pe)[:, 0:P], ones_row[:, :], bv_row[:, :]))
            bank = job.start(pe)
            pe.transpose(bank[:, 0:32], b1_rows[:, :], ident[0:32, 0:32])
            full(pe.transpose(bank[:, 32:39], vec_rows[:, :], ident[0:7, 0:7]))
            pe.wait_ge(setup_done, 1)

            def project(r, job, hp):
                bank = job.start(pe)
                if r == 0:
                    pe.wait_ge(xh_ready, hp + 1)
                    for t in range(HT):
                        ins = pe.transpose(bank[:, t * P:(t + 1) * P], xh[:, t, :], ident[:, :])
                elif r < 3:
                    pe.wait_ge(hT_ready, hp + 1)
                    ins = mm(bank[:, :], wqkv[:, (r - 1) * D:r * D], hT[:, :])
                else:
                    for t in range(HT):
                        ins = mm(bank[:, t * P:(t + 1) * P], hT[:, t * P:(t + 1) * P], wqkv[:, 2 * D:3 * D])
                full(ins)

            def maxima(job, r, m0, m1):
                for m in range(m0, m1):
                    t, kk, hd = m // 4, (m // 2) % 2, m % 2
                    rows = slice(64 * hd, 64 * hd + QK_ROWS)
                    full(mm(job.start(pe)[:, :], qs[r][rows, t * P:(t + 1) * P], ks[r][rows, kk * HALF:(kk + 1) * HALF]))

            def turn_maxima(job, pi, who):
                bank = job.start(pe, who)
                pe.wait_ge(mparts_ready, pi + 1)
                full(pe.transpose(bank[:, 0:P], mparts[:, :], ident[:, :]), who)

            def unit(ui, r, hp, job, lap, ei=None, w_laps=None):
                expert = ei is not None
                par = r % 2
                nxt = (r + 1) % BUFS

                def scores(s, half):
                    for hd in range(2):
                        n = 4 * s + 2 * half + hd
                        held = ui * 4 * TILES + (n - SCORE_BANKS if n >= SCORE_BANKS
                                                 else n - 4 * TILES % SCORE_BANKS)
                        if n != SCORE_BANKS - 1:
                            pe.wait_ge(exp_done, held + 1 + 2)
                        rows = slice(64 * hd, 64 * hd + SC_ROWS)
                        mm(score[n % SCORE_BANKS][:, :], ks[r][rows, s * P:(s + 1) * P],
                           qs[r][rows, half * HALF:(half + 1) * HALF]).then_inc(score_full, 1)

                def weigh(s):
                    pe.wait_ge(exp_done, ui * 4 * TILES + 4 * s + 4 + 2)
                    if s == 0:
                        pe.wait_ge(o_out, ui + 1)
                        pe.wait_ge(vbuf_ready, ui + 1)
                    for hd in range(2):
                        for half in range(2):
                            j = 2 * hd + half
                            ins = mm(o_ps[32 * j:32 * j + 32, :], vbuf[par][:, s, hd, :],
                                     ebuf[:, s % 2, 2 * half + hd, :], s == 0, s == TILES - 1)
                    ins.then_inc(e_used, 1)

                def branch(stage):
                    who = 1 if stage in (NORMED, GATES) else 0
                    bank = job.start(pe, who)
                    if stage == NORMED:
                        pe.wait_ge(xs_ready, ui + 1)
                        pe.transpose(bank[:, 0:P], xs[:, 0, :], ident[:, :])
                        full(pe.transpose(bank[:, P:2 * P], xs[:, 1, :], ident[:, :]), who)
                    if stage == PROJECTED:
                        pe.wait_ge(xT_ready, ui + 1)
                        full(mm(bank[:, 0:3 * D], xnT[:, :], wT[:, 0:3, :].rearrange("p a n -> p (a n)")))
                    if stage == MEANS:
                        mm(bank[:, 0:D], wT[:, 4, :], xT[:, :])
                        mm(bank[:, D:2 * D], xT[:, :], wT[:, 4, :])
                        full(mm(bank[:, 2 * D:3 * D], seg_mean[:, :, :].rearrange("p a n -> p (a n)"), xs[:, 0, :]))
                    if stage == SEGMENTS:
                        pe.wait_ge(uT_ready, ui + 1)
                        full(mm(bank[:, 0:NSEG], u_both[:, 0, :], mT[:, :]))
                    if stage == GATES:
                        pe.wait_ge(gates_ready, ui + 1)
                        full(pe.transpose(bank[:, 0:P], gates[:, :, :].rearrange("p j n -> p (j n)"), ident[:, :]), who)
                    if stage in PREFIX:
                        j = stage - PREFIX[0]
                        if j == 0:
                            pe.wait_ge(pv_ready, ui + 1)
                        strip = slice(32 * j, 32 * j + 32)
                        mm(bank[:, 0:STC], tri[:, :], pv[:, 4 * j:4 * j + 4, :].rearrange("p h x -> p (h x)"), True, False)
                        full(mm(bank[:, 0:STC], last_seg[strip, :], state[strip, :, :].rearrange("p h x -> p (h x)"),
                                False, True))
                    if stage == STATES:
                        for j in range(4):
                            ins = mm(bank[32 * j:32 * j + 32, 0:STC], ends_t[:, :],
                                     pv[:, 4 * j:4 * j + 4, :].rearrange("p h x -> p (h x)"))
                        full(ins)
                    if stage in RETRIEVE:
                        j = stage - RETRIEVE[0]
                        if j == 0:
                            pe.wait_ge(gT_ready, ui + 1)
                            pe.wait_ge(state_ready, ui + 1)
                        strip = slice(32 * j, 32 * j + 32)
                        full(mm(bank[:, 0:4 * DK * DK], gT[strip, :], state[strip, :, 0:DK * DK]))
                    if stage == DIVIDED:
                        pe.wait_ge(lin_ready, ui + 1)
                        full(pe.transpose(bank[:, 0:P], lin[:, :], ident[:, :]))
                    if stage == OUTPUT:
                        pe.wait_ge(linT_ready, ui + 1)
                        full(mm(bank[:, 0:D], linT[:, :], wT[:, 3, :]))

                def turn_sums(n):
                    bank = job.start(pe)
                    pe.wait_ge(o_out, ui + 2)
                    for i in range(2 * n, 2 * n + 2):
                        ins = pe.transpose(bank[:, (i % 2) * P:(i % 2 + 1) * P], ot[:, i * P:(i + 1) * P], ident[:, :])
                    full(ins)

                pe.wait_ge(mrows_loaded, 32 * (ui + 1))
                scores(0, 0)
                scores(0, 1)
                pe.wait_ge(pair_loaded[nxt], lap * 64 + 64)
                m = 0
                for s, stage in steps(r, expert):
                    if stage in (SCORES0, SCORES1):
                        scores(s + 1, stage - SCORES0)
                    elif stage == MAXIMUM:
                        maxima(job, nxt, m, m + 1)
                        m += 1
                    elif stage == TURN:
                        turn_maxima(job, ui + 1, 1)
                    elif stage == AHEAD:
                        project(r, job, hp)
                    elif stage == WEIGH:
                        weigh(s)
                    elif stage in (HIDDEN0, HIDDEN1):
                        if s == 0 and stage == HIDDEN0:
                            pe.wait_ge(w_loaded[par], w_laps * 32 + 32)
                        tb = stage - HIDDEN0
                        full(mm(job.start(pe, 1)[:, :], w1_buf[par][:, s * P:(s + 1) * P],
                                h2T[:, tb * HALF:(tb + 1) * HALF]), 1)
                    elif stage == EXPERT:
                        if s == FC:
                            pe.wait_ge(free_a, job.at[1] + job.made[1] + 1)
                        bank = job.start(pe)
                        for t in range(2):
                            tile = 2 * (s - FC) + t
                            for c in range(FC):
                                ins = mm(bank[:, t * D:(t + 1) * D],
                                         hid[:, tile // HT, c, (tile % HT) * P:(tile % HT + 1) * P],
                                         w2_buf[par][:, c, :], c == 0, c == FC - 1)
                        full(ins)
                    elif stage in (SUMS0, SUMS1):
                        turn_sums(stage - SUMS0)
                    elif stage >= BRANCH:
                        branch(stage)
                assert job.made == [UNIT_D + (EXPERT_D if expert else 0), UNIT_A + (EXPERT_A if expert else 0)], job.made

            def route(b, at):
                job = ring_at(at)
                pe.wait_ge(on_ready, (b + 1) * PAIRS + 1)
                for hb in range(2):
                    bank = job.start(pe)
                    for t in range(HT):
                        ins = pe.transpose(bank[:, t * P:(t + 1) * P], on[:, hb * HT + t, :], ident[:, :])
                    full(ins)
                for hb in range(2):
                    bank = job.start(pe)
                    pe.wait_ge(onT_ready, b * 2 + hb + 1)
                    for t in range(HT):
                        tile = hb * HT + t
                        mm(bank[:, t * P:(t + 1) * P], onT[:, tile * P:(tile + 1) * P], wo_f[:, :], True, False)
                        ins = mm(bank[:, t * P:(t + 1) * P], ones_row[:, :], bo_row[:, :], False, True)
                    full(ins)
                for hb in range(2):
                    bank = job.start(pe)
                    pe.wait_ge(z2_ready, b * 2 + hb + 1)
                    for t in range(HT):
                        ins = pe.transpose(bank[:, t * P:(t + 1) * P], z2[:, hb * HT + t, :], ident[:, :])
                    full(ins)
                for hb in range(2):
                    bank = job.start(pe)
                    pe.wait_ge(h2T_ready, b * 2 + hb + 1)
                    for t in range(HT):
                        at = bank[:, t * EXPERTS:(t + 1) * EXPERTS]
                        tile = hb * HT + t
                        mm(at, h2T[:, tile * P:(tile + 1) * P], gate_sb[:, :], True, False)
                        ins = mm(at, ones_row[:, :], gateb_row[:, :], False, True)
                    full(ins)
                for hb in range(2):
                    bank = job.start(pe)
                    pe.wait_ge(ew_ready, b + 1)
                    for t in range(HT):
                        ins = pe.transpose(bank[0:EXPERTS, t * P:(t + 1) * P], ew[:, hb * HT + t, :], ident[:, :])
                    full(ins)
                for hb in range(2):
                    bank = job.start(pe)
                    pe.wait_ge(ewT_ready, b * 2 + hb + 1)
                    for t in range(HT):
                        tile = hb * HT + t
                        ins = mm(bank[:, t * P:(t + 1) * P], ewT[:, tile * P:(tile + 1) * P], b2_sb[:, :])
                    full(ins)

            for half in range(2):
                for r in range(BUFS):
                    project(r, job, half)
            pe.wait_ge(pair_loaded[0], 64)
            maxima(job, 0, 0, MAXIMA)
            turn_maxima(job, 0, 0)
            with pe.Fori(0, PAIRS // BUFS) as it:
                for r in range(BUFS):
                    u = it * BUFS + r
                    unit(u, r, 2 + it, ring_at(FIRST_AT + u * UNIT_D, u * UNIT_A), it + (1 if r == BUFS - 1 else 0))
            with pe.Fori(1, B) as b:
                route(b - 1, base_d(b))
                with pe.Fori(0, PAIRS // BUFS) as it:
                    for r in range(BUFS):
                        u = it * BUFS + r
                        ei = (b - 1) * EXPERTS + u
                        unit(b * PAIRS + u, r, b * 2 + 2 + it,
                             ring_at(base_d(b) + ROUTE_JOBS + u * (UNIT_D + EXPERT_D),
                                                       base_a(b) + u * (UNIT_A + EXPERT_A)),
                             b * (PAIRS // BUFS) + it + (1 if r == BUFS - 1 else 0), ei,
                             (b - 1) * (EXPERTS // 2) + it * (BUFS // 2) + r // 2)
            route(B - 1, TAIL_AT)
            with pe.Fori(0, EXPERTS // 2) as e2:
                for par in range(2):
                    e = e2 * 2 + par
                    ei = (B - 1) * EXPERTS + e
                    job = ring_at(TAIL_AT + ROUTE_JOBS + e * EXPERT_D, base_a(B) + e * EXPERT_A)
                    pe.wait_ge(w_loaded[par], ((B - 1) * (EXPERTS // 2) + e2 + 1) * 32)
                    for c in range(FC):
                        for tb in range(2):
                            full(mm(job.start(pe, 1)[:, :], w1_buf[par][:, c * P:(c + 1) * P],
                                    h2T[:, tb * HALF:(tb + 1) * HALF]), 1)
                    pe.wait_ge(free_a, job.at[1] + EXPERT_A + 1)
                    for q in range(EXPERT_D):
                        bank = job.start(pe)
                        for t in range(2):
                            tile = 2 * q + t
                            for c in range(FC):
                                ins = mm(bank[:, t * D:(t + 1) * D],
                                         hid[:, tile // HT, c, (tile % HT) * P:(tile % HT + 1) * P],
                                         w2_buf[par][:, c, :], c == 0, c == FC - 1)
                        full(ins)


_INS = ['L0_attn_x', 'L0_attn_norm_w', 'L0_attn_Wq', 'L0_attn_Wk', 'L0_attn_Wv', 'L0_attn_Wo', 'L0_attn_Wu',
        'L0_ffn_ln1_g', 'L0_ffn_ln1_b', 'L0_ffn_w_qkv', 'L0_ffn_b_qkv', 'L0_ffn_w_o', 'L0_ffn_b_o',
        'L0_ffn_ln2_g', 'L0_ffn_ln2_b', 'L0_ffn_gate_w', 'L0_ffn_gate_b', 'L0_ffn_W1', 'L0_ffn_b1',
        'L0_ffn_W2', 'L0_ffn_b2']
_OUTS = [((B, T, D), 'float32')]


def kernel(**inputs):
    import numpy as _np
    import concourse.bacc as _bacc
    from concourse import mybir as _mybir
    from concourse.bass_utils import run_bass_kernel_spmd as _run

    nc = _bacc.Bacc("TRN2", target_bir_lowering=False, num_devices=1)
    arrays, args = {}, []
    for name in _INS:
        a = _np.ascontiguousarray(inputs[name])
        arrays[f"in_{name}_dram"] = a
        args.append(nc.dram_tensor(f"in_{name}_dram", a.shape, _mybir.dt.from_np(a.dtype), kind="ExternalInput").ap())
    for i, (shape, dtype) in enumerate(_OUTS):
        dt = _mybir.dt.from_np(_np.dtype(dtype))
        args.append(nc.dram_tensor(f"out_{i}_dram", shape, dt, kind="ExternalOutput").ap())
    program(nc, *args)
    r = _run(nc, [arrays], core_ids=[0])
    return r.results[0]["out_0_dram"]
```
